# Optimizing a Trainium2 kernel written in Bass

```python
import numpy as np
import jax
import jax.numpy as jnp

def _softmax(x, axis=-1):
    return jax.nn.softmax(x, axis=axis)

def _gelu(x):
    return jax.nn.gelu(x, approximate=True)

def _silu(x):
    return jax.nn.silu(x)

def _sigmoid(x):
    return jax.nn.sigmoid(x)

def _layernorm(x, axis=-1, eps=1e-05):
    m = jnp.mean(x, axis=axis, keepdims=True)
    v = jnp.var(x, axis=axis, keepdims=True)
    return (x - m) / jnp.sqrt(v + eps)

def _scatter_add(tgt, idx, src, axis=0):
    return tgt.at[idx].add(src)

def _segment_sum(src, seg, n):
    return jax.ops.segment_sum(src, seg, n)
kernel_name = 'mk_decoder_postln_d1_seqx_r8_27dd03'

def setup_inputs(seed: int=0):
    np.random.seed(seed)
    _w = jnp.asarray

    def _rec_inputs():
        import jax
        import jax.numpy as jnp
        _rk = jax.random.key(seed)
        x = -0.0002928 + 1 * jax.random.normal(jax.random.fold_in(_rk, 1), (16, 128, 256), jnp.float32)
        _lenS = 128 - jax.random.randint(jax.random.fold_in(_rk, 7), (16,), 0, max(1, 128 // 4) + 1, jnp.int32)
        _lenS2 = 128 - jax.random.randint(jax.random.fold_in(_rk, 8), (16,), 0, max(1, 128 // 4) + 1, jnp.int32)
        fside_S2_0 = -0.00337071 + 1.01897 * jax.random.normal(jax.random.fold_in(_rk, 11), (128,), jnp.float32)
        _ctx_2048P = jax.random.normal(jax.random.fold_in(_rk, 12), (16, 16, 256), jnp.float32)
        _ctx_2048c = jax.random.dirichlet(jax.random.fold_in(_rk, 512), 0.3 * jnp.ones((16,), jnp.float32), (16, 128))
        _ctx_2048t = jnp.einsum('bsk,bkd->bsd', _ctx_2048c, _ctx_2048P)
        _ctx_2048t = _ctx_2048t * jax.lax.rsqrt(jnp.mean(jnp.square(_ctx_2048t)) + 1e-12) * 0.953939
        ctx_2048 = 0.000675642 + 1.00031 * (_ctx_2048t + 0.3 * jax.random.normal(jax.random.fold_in(_rk, 612), (16, 128, 256), jnp.float32))
        return (x, fside_S2_0, ctx_2048)
    x, fside_S2_0, ctx_2048 = _rec_inputs()

    def _L0_attn_setup():
        import jax, jax.numpy as jnp
        import numpy as np
        B, N, DIM = (2, 256, 256)
        H, DH = (16, 128)
        SOFTCAP = 50.0
        SCALE = DH ** (-0.5)
        key = jax.random.key(seed)
        k1, k2, k3, k4 = jax.random.split(key, 4)
        s = 1.0 / np.sqrt(DIM)
        x = jax.random.normal(k1, (B, N, DIM), dtype=jnp.float32)
        w_qkv = jax.random.normal(k2, (DIM, 3 * H * DH), dtype=jnp.float32) * s
        w_gates = jax.random.normal(k3, (DIM, H), dtype=jnp.float32) * s
        w_out = jax.random.normal(k4, (H * DH, DIM), dtype=jnp.float32) * s
        return {'x': x, 'w_qkv': w_qkv, 'w_gates': w_gates, 'w_out': w_out}
    _L0_attn_all = _L0_attn_setup()
    _L0_attn_in = {k: v for k, v in _L0_attn_all.items() if k in ('w_qkv', 'w_gates', 'w_out')}
    del _L0_attn_all

    def _L0_xattn_setup():
        import jax, jax.numpy as jnp
        import numpy as np
        key = jax.random.key(seed)
        ks = jax.random.split(key, 5)
        B, D, L, NH = (2, 128, 256, 8)
        H = D // NH
        return {'v': jax.random.normal(ks[0], (B, D, L), jnp.float32), 'k': jax.random.normal(ks[1], (H, L), jnp.float32) * 0.1, 'bias': jax.random.normal(ks[2], (D,), jnp.float32), 'x1': jax.random.normal(ks[3], (B, D, L), jnp.float32), 'x2': jax.random.normal(ks[4], (B, D, L), jnp.float32), 'num_heads': NH}
    _L0_xattn_all = _L0_xattn_setup()
    _L0_xattn_in = {k: v for k, v in _L0_xattn_all.items() if k in ('k',)}
    del _L0_xattn_all

    def _L0_ffn_setup():
        import jax, jax.numpy as jnp
        import numpy as np
        TOP_K = 6
        CAP_FACTOR = 2

        def _moe_block(x2d, wg_router, w_gate, w_up, w_down, ws_gate, ws_up, ws_down):
            T, D = x2d.shape
            E = wg_router.shape[0]
            scores = jax.nn.softmax(x2d @ wg_router.T, axis=-1)
            topk_w, topk_idx = jax.lax.top_k(scores, TOP_K)
            topk_w = topk_w / (jnp.sum(topk_w, axis=-1, keepdims=True) + 1e-20)
            flat_idx = topk_idx.reshape(-1)
            oh = jax.nn.one_hot(flat_idx, E, dtype=jnp.int32)
            pos = jnp.cumsum(oh, axis=0) - 1
            pos_in_e = jnp.take_along_axis(pos, flat_idx[:, None], axis=1)[:, 0]
            C = CAP_FACTOR * (T * TOP_K // E)
            valid = pos_in_e < C
            safe_pos = jnp.where(valid, pos_in_e, 0)
            tok_id = jnp.repeat(jnp.arange(T), TOP_K)
            vmask = valid[:, None].astype(x2d.dtype)
            x_rep = x2d[tok_id] * vmask
            xe = jnp.zeros((E, C, D), x2d.dtype).at[flat_idx, safe_pos].add(x_rep)
            g = jnp.einsum('ecd,edf->ecf', xe, w_gate)
            u = jnp.einsum('ecd,edf->ecf', xe, w_up)
            ye = jnp.einsum('ecf,efd->ecd', jax.nn.silu(g) * u, w_down)
            y_tok = ye[flat_idx, safe_pos] * vmask
            y = jnp.sum(y_tok.reshape(T, TOP_K, D) * topk_w[..., None], axis=1)
            sh = jax.nn.silu(x2d @ ws_gate) * (x2d @ ws_up) @ ws_down
            return y + sh
        key = jax.random.key(seed)
        ks = jax.random.split(key, 9)
        B, S, D, F, E = (1, 256, 256, 176, 32)
        FS = F * 2
        s = 0.02
        return {'hidden_states': jax.random.normal(ks[0], (B, S, D), jnp.float32), 'wg_router': jax.random.normal(ks[1], (E, D), jnp.float32) * s, 'w_gate': jax.random.normal(ks[2], (E, D, F), jnp.float32) * s, 'w_up': jax.random.normal(ks[3], (E, D, F), jnp.float32) * s, 'w_down': jax.random.normal(ks[4], (E, F, D), jnp.float32) * s, 'ws_gate': jax.random.normal(ks[5], (D, FS), jnp.float32) * s, 'ws_up': jax.random.normal(ks[6], (D, FS), jnp.float32) * s, 'ws_down': jax.random.normal(ks[7], (FS, D), jnp.float32) * s}
    _L0_ffn_all = _L0_ffn_setup()
    _L0_ffn_in = {k: v for k, v in _L0_ffn_all.items() if k in ('wg_router', 'w_gate', 'w_up', 'w_down', 'ws_gate', 'ws_up', 'ws_down')}
    del _L0_ffn_all
    return {'x': x, 'fside_S2_0': fside_S2_0, 'ctx_2048': ctx_2048, 'L0_attn_w_qkv': _L0_attn_in['w_qkv'], 'L0_attn_w_gates': _L0_attn_in['w_gates'], 'L0_attn_w_out': _L0_attn_in['w_out'], 'L0_xattn_k': _L0_xattn_in['k'], 'L0_ffn_wg_router': _L0_ffn_in['wg_router'], 'L0_ffn_w_gate': _L0_ffn_in['w_gate'], 'L0_ffn_w_up': _L0_ffn_in['w_up'], 'L0_ffn_w_down': _L0_ffn_in['w_down'], 'L0_ffn_ws_gate': _L0_ffn_in['ws_gate'], 'L0_ffn_ws_up': _L0_ffn_in['ws_up'], 'L0_ffn_ws_down': _L0_ffn_in['ws_down']}

def reference(x, fside_S2_0, ctx_2048, L0_attn_w_qkv, L0_attn_w_gates, L0_attn_w_out, L0_xattn_k, L0_ffn_wg_router, L0_ffn_w_gate, L0_ffn_w_up, L0_ffn_w_down, L0_ffn_ws_gate, L0_ffn_ws_up, L0_ffn_ws_down):
    import jax
    import jax.numpy as jnp

    def _L0_attn_ref(x, w_qkv, w_gates, w_out):
        import jax, jax.numpy as jnp
        import numpy as np
        B, N, DIM = (2, 256, 256)
        H, DH = (16, 128)
        SOFTCAP = 50.0
        SCALE = DH ** (-0.5)
        b, n, _ = x.shape
        qkv = (x @ w_qkv).reshape(b, n, 3, H, DH).transpose(2, 0, 3, 1, 4)
        q, k, v = (qkv[0], qkv[1], qkv[2])
        q = q * SCALE
        sim = jnp.einsum('bhid,bhjd->bhij', q, k)
        sim = jnp.tanh(sim / SOFTCAP) * SOFTCAP
        mask_value = -jnp.finfo(sim.dtype).max
        causal_mask = jnp.triu(jnp.ones((n, n), dtype=bool), 1)
        sim = jnp.where(causal_mask, mask_value, sim)
        attn = jax.nn.softmax(sim, axis=-1)
        out = jnp.einsum('bhij,bhjd->bhid', attn, v)
        gates = jax.nn.sigmoid(x @ w_gates)
        out = out * gates.transpose(0, 2, 1)[..., None]
        out = out.transpose(0, 2, 1, 3).reshape(b, n, H * DH) @ w_out
        return out

    def _L0_xattn_ref(v, k, bias, x1, x2, num_heads):
        import jax, jax.numpy as jnp
        import numpy as np
        B, D, L = v.shape
        H = D // num_heads
        fft_size = 2 * L
        vr = v.reshape(B, H, num_heads, L)
        x1r = x1.reshape(B, H, num_heads, L)
        x2r = x2.reshape(B, H, num_heads, L)
        kv = vr[:, :, :, None, :] * x2r[:, :, None, :, :]
        k_f = jnp.fft.rfft(k.astype(jnp.float32), n=fft_size)
        y = jnp.fft.irfft(jnp.fft.rfft(kv, n=fft_size) * k_f[None, :, None, None, :], n=fft_size)[..., :L]
        skip = bias.astype(jnp.float32).reshape(H, num_heads)[None, :, :, None, None]
        y = y + kv * skip
        out = jnp.einsum('bhijl,bhil->bhjl', y, x1r)
        return out.reshape(B, D, L)

    def _L0_ffn_ref(hidden_states, wg_router, w_gate, w_up, w_down, ws_gate, ws_up, ws_down):
        import jax, jax.numpy as jnp
        import numpy as np
        TOP_K = 6
        CAP_FACTOR = 2

        def _moe_block(x2d, wg_router, w_gate, w_up, w_down, ws_gate, ws_up, ws_down):
            T, D = x2d.shape
            E = wg_router.shape[0]
            scores = jax.nn.softmax(x2d @ wg_router.T, axis=-1)
            topk_w, topk_idx = jax.lax.top_k(scores, TOP_K)
            topk_w = topk_w / (jnp.sum(topk_w, axis=-1, keepdims=True) + 1e-20)
            flat_idx = topk_idx.reshape(-1)
            oh = jax.nn.one_hot(flat_idx, E, dtype=jnp.int32)
            pos = jnp.cumsum(oh, axis=0) - 1
            pos_in_e = jnp.take_along_axis(pos, flat_idx[:, None], axis=1)[:, 0]
            C = CAP_FACTOR * (T * TOP_K // E)
            valid = pos_in_e < C
            safe_pos = jnp.where(valid, pos_in_e, 0)
            tok_id = jnp.repeat(jnp.arange(T), TOP_K)
            vmask = valid[:, None].astype(x2d.dtype)
            x_rep = x2d[tok_id] * vmask
            xe = jnp.zeros((E, C, D), x2d.dtype).at[flat_idx, safe_pos].add(x_rep)
            g = jnp.einsum('ecd,edf->ecf', xe, w_gate)
            u = jnp.einsum('ecd,edf->ecf', xe, w_up)
            ye = jnp.einsum('ecf,efd->ecd', jax.nn.silu(g) * u, w_down)
            y_tok = ye[flat_idx, safe_pos] * vmask
            y = jnp.sum(y_tok.reshape(T, TOP_K, D) * topk_w[..., None], axis=1)
            sh = jax.nn.silu(x2d @ ws_gate) * (x2d @ ws_up) @ ws_down
            return y + sh
        B, S, D = hidden_states.shape
        x2d = hidden_states.reshape(-1, D)
        out = _moe_block(x2d, wg_router, w_gate, w_up, w_down, ws_gate, ws_up, ws_down)
        return out.reshape(B, S, D)
    x = _layernorm(x + _L0_attn_ref(x, L0_attn_w_qkv, L0_attn_w_gates, L0_attn_w_out), axis=-1)
    x = _layernorm(x + _L0_xattn_ref(x, L0_xattn_k, fside_S2_0, ctx_2048, ctx_2048, 8), axis=-1)
    x = _layernorm(x + _L0_ffn_ref(x, L0_ffn_wg_router, L0_ffn_w_gate, L0_ffn_w_up, L0_ffn_w_down, L0_ffn_ws_gate, L0_ffn_ws_up, L0_ffn_ws_down), axis=-1)
    return x

_drawn_inputs = setup_inputs


def setup_inputs(seed=0):
    import zlib

    import numpy as np

    out = dict(_drawn_inputs(seed))
    spreads = {}
    factors = {'L0_ffn_wg_router': 8.0,
     'L0_ffn_w_gate': 8.0,
     'L0_ffn_w_up': 8.0,
     'L0_ffn_w_down': 8.0,
     'L0_ffn_ws_gate': 2.897,
     'L0_ffn_ws_up': 2.86,
     'L0_ffn_ws_down': 2.851}
    for name, (base, spread) in spreads.items():
        noise = np.random.default_rng([zlib.crc32(name.encode()), seed]).standard_normal(out[name].shape)
        drawn = base * np.exp(spread * noise) if base else spread * noise
        out[name] = jnp.asarray(drawn.astype(out[name].dtype))
    for name, factor in factors.items():
        out[name] = (out[name] * factor).astype(out[name].dtype)
    return out
```

```python
from contextlib import ExitStack

import concourse.bass as bass
from concourse import mybir

F32 = mybir.dt.float32
F32R = mybir.dt.float32r
U32 = mybir.dt.uint32
I32 = mybir.dt.int32
ALU = mybir.AluOpType
ACT = mybir.ActivationFunctionType
AX = mybir.AxisListType

P = 128
LN_EPS = 1e-5
GB = 4


class Scope:

    def __init__(self, nc, ctx, prefix):
        self.nc, self.ctx, self.prefix = nc, ctx, prefix

    def sb(self, name, shape, dt=F32):
        return self.ctx.enter_context(self.nc.sbuf_tensor(self.prefix + name, shape, dt))

    def ps(self, name, shape, dt=F32):
        return self.ctx.enter_context(self.nc.psum_tensor(self.prefix + name, shape, dt))

    def sem(self, name):
        return self.ctx.enter_context(self.nc.semaphore(self.prefix + name))


def split3(pe, out, lhs, rhs, first, last):
    pe.matmul(out, lhs[0], rhs[0], start=first, stop=False, skip_group_check=True)
    pe.matmul(out, lhs[0], rhs[1], start=False, stop=False, skip_group_check=True)
    return pe.matmul(out, lhs[1], rhs[0], start=False, stop=last, skip_group_check=True)


def layer_norm(dve, x, out, stats, agg, std, rstd, steps, std_ready, n_before, tick):
    count = x.shape[1]
    for n in range(count):
        last = dve.bn_stats(stats[:, n, :], x[:, n, :])
    last.then_inc(steps, 1)
    carried_wait(dve, steps, 3 * n_before + 1, tick)
    for n in range(count):
        last = dve.bn_aggr(agg[:, n, :], stats[:, n, :])
    last.then_inc(steps, 1)
    dve.wait_ge(std_ready, n_before + 1)
    dve.reciprocal(rstd[:], std[:]).then_inc(steps, 1)
    dve.wait_ge(steps, 3 * n_before + 3)
    for n in range(count):
        last = dve.tensor_scalar(out[:, n, :], x[:, n, :], agg[:, n, 0:1], rstd[:, n:n + 1],
                                 ALU.subtract, ALU.mult)
    return last


def layer_norm_std(act, agg, std, eps, steps, std_ready, n_before):
    act.wait_ge(steps, 3 * n_before + 2)
    act.activation(std[:], agg[:, :, 1], ACT.Sqrt, bias=eps).then_inc(std_ready, 1)


def carried_wait(dve, sem, value, tick):
    dve.wait_ge(sem, value)
    dve.memset(tick, 0.0)


def attention_stage(nc, ident, eps, x, w_qkv, w_gates, w_out, x1, fills):
    B, N, D = x.shape
    H = w_gates.shape[1]
    DH = w_qkv.shape[1] // (3 * H)
    G = B // GB
    KB = D // P
    SOFTCAP, SCALE = 50.0, DH ** -0.5
    HG = 4
    VW = DH + 2
    T = GB * N
    NV = H
    EARLY = GB
    CH = 512
    NCH = w_qkv.shape[1] // CH
    WOH = 4
    NRAW = 4
    assert (N, DH, T, HG * DH, H // HG, WOH * D, KB * CH) == (P, P, 512, 512, GB, 1024, 1024)

    x_in = x.rearrange("b p c -> p b c")
    x1_out = x1.rearrange("b p c -> p b c")
    w_in = w_qkv.rearrange("(k p) n -> p k n", p=P)
    wg_in = w_gates.rearrange("(k p) n -> p k n", p=P)
    wo_in = w_out.rearrange("(h p) c -> p h c", p=P)

    with ExitStack() as ctx:
        s = Scope(nc, ctx, "at_")
        w_hi, w_lo = s.sb("w_hi", [P, KB, 3 * H * DH], F32R), s.sb("w_lo", [P, KB, 3 * H * DH], F32R)
        wo_hi, wo_lo = s.sb("wo_hi", [P, H, D], F32R), s.sb("wo_lo", [P, H, D], F32R)
        wg_hi, wg_lo = s.sb("wg_hi", [P, KB, H], F32R), s.sb("wg_lo", [P, KB, H], F32R)
        raw, wg_raw = s.sb("raw", [P, NRAW, 1024]), s.sb("wg_raw", [P, KB, H])
        xT_hi, xT_lo = s.sb("xT_hi", [P, KB, T], F32R), s.sb("xT_lo", [P, KB, T], F32R)
        qT, kT = s.sb("qT", [P, T]), s.sb("kT", [P, T])
        v = s.sb("v", [P, 2, GB, HG, VW])
        capped = s.sb("capped", [P, T])
        probs = s.sb("probs", [P, 2, T])
        o_norm = s.sb("o_norm", [P, GB, DH])
        oT_hi, oT_lo = s.sb("oT_hi", [P, T], F32R), s.sb("oT_lo", [P, T], F32R)
        gate_exp, gate_den = s.sb("gate_exp", [P, GB, H]), s.sb("gate_den", [P, GB, H])
        o_den, o_scale = s.sb("o_den", [P, GB]), s.sb("o_scale", [P, GB])
        stats, agg = s.sb("stats", [P, GB, 6]), s.sb("agg", [P, GB, 2])
        tick = s.sb("tick", [P, 1])
        causal = s.sb("causal", [P, N])
        std, rstd = s.sb("std", [P, GB]), s.sb("rstd", [P, GB])
        x_for_T, x_res, x_out = (raw[:, n, :].rearrange("p (b c) -> p b c", b=GB) for n in range(3))

        ps_qv, ps_k, ps_s, ps_oT = (s.ps(n, [P, T]) for n in ("ps_qv", "ps_k", "ps_s", "ps_oT"))
        ps_o, ps_acc = s.ps("ps_o", [P, GB, D]), s.ps("ps_acc", [P, GB, D])
        ps_xT = ps_o[:, :, :].rearrange("p b c -> p (b c)").rearrange("p (k t) -> p k t", k=KB)
        ps_gate = ps_k[:, 0:GB * H].rearrange("p (b h) -> p b h", b=GB)

        raw_loaded = [s.sem(f"raw_loaded{n}") for n in range(NRAW)]
        gates_loaded, hi_split, lo_split, ones_ready, causal_ready = (
            s.sem(n) for n in ("gates_loaded", "hi_split", "lo_split", "ones_ready", "causal_ready"))
        filled = s.sem("filled")
        x_for_T_loaded, x_res_loaded, x1_stored = (s.sem(n) for n in ("x_for_T_loaded", "x_res_loaded", "x1_stored"))
        xT_in_psum, xT_hi_ready, xT_lo_ready = (s.sem(n) for n in ("xT_in_psum", "xT_hi_ready", "xT_lo_ready"))
        q_in_psum, q_ready = s.sem("q_in_psum"), s.sem("q_ready")
        k_in_psum, k_ready = s.sem("k_in_psum"), s.sem("k_ready")
        v_in_psum, v_ready = s.sem("v_in_psum"), s.sem("v_ready")
        gate_in_psum, gate_exp_ready, gate_ready = (s.sem(n) for n in ("gate_in_psum", "gate_exp_ready", "gate_ready"))
        s_in_psum, capped_ready, exp_ready, probs_ready = (
            s.sem(n) for n in ("s_in_psum", "capped_ready", "exp_ready", "probs_ready"))
        o_in_psum, o_steps, o_ready = (s.sem(n) for n in ("o_in_psum", "o_steps", "o_ready"))
        oT_in_psum, oT_hi_ready, oT_lo_ready = (s.sem(n) for n in ("oT_in_psum", "oT_hi_ready", "oT_lo_ready"))
        acc_in_psum, sum_ready, ln_steps, std_ready, x1_ready = (
            s.sem(n) for n in ("acc_in_psum", "sum_ready", "ln_steps", "std_ready", "x1_ready"))

        chunks = [(w_in[:, :, c * CH:(c + 1) * CH], w_hi[:, :, c * CH:(c + 1) * CH],
                   w_lo[:, :, c * CH:(c + 1) * CH], KB) for c in range(NCH)]
        chunks += [(wo_in[:, h:h + WOH, :], wo_hi[:, h:h + WOH, :], wo_lo[:, h:h + WOH, :], WOH)
                   for h in range(0, H, WOH)]

        def raw_chunk(n, k):
            return raw[:, n % NRAW, :].rearrange("p (k c) -> p k c", k=k)

        def piece(h):
            return (h - 1) // GB + 1, (h - 1) % GB if 1 <= h <= NV - EARLY else None

        block = ctx.enter_context(nc.Block())

        @block.sync
        def _(sp):
            sp.dma_start(wg_raw[:], wg_in).then_inc(gates_loaded, 16)
            for n, (src, _, _, k) in enumerate(chunks):
                if n >= NRAW:
                    sp.wait_ge(hi_split, n - NRAW + 1)
                    sp.wait_ge(lo_split, n - NRAW + 1)
                sp.dma_start(raw_chunk(n, k), src).then_inc(raw_loaded[n % NRAW], 16)
            sp.wait_ge(hi_split, len(chunks))
            sp.wait_ge(lo_split, len(chunks))
            sp.dma_start(x_for_T, x_in[:, 0:GB, :]).then_inc(x_for_T_loaded, 16)

            FR = 12

            def fill(g):
                for dst, row in fills:
                    width = dst.shape[1]
                    share = dst.shape[0] // G
                    for n in range(share // (P * FR)):
                        sp.dma_start(dst[bass.ds(g * share + n * P * FR, P * FR), :]
                                     .rearrange("(p r) w -> p r w", p=P),
                                     row[:].unsqueeze(1).broadcast_to([P, FR, width])).then_inc(filled, 16)

            def group(g, last):
                sp.wait_ge(sum_ready, g)
                sp.dma_start(x_res, x_in[:, bass.ds(g * GB, GB), :]).then_inc(x_res_loaded, 16)
                if not last:
                    sp.wait_ge(xT_in_psum, g + 1)
                    sp.dma_start(x_for_T, x_in[:, bass.ds(g * GB + GB, GB), :]).then_inc(x_for_T_loaded, 16)
                fill(g)
                sp.wait_ge(x1_ready, g + 1)
                sp.dma_start(x1_out[:, bass.ds(g * GB, GB), :], x_out).then_inc(x1_stored, 16)

            with sp.Fori(0, G - 1) as g:
                group(g, False)
            group(G - 1, True)
            sp.wait_ge(x1_stored, 16 * G)
            sp.wait_ge(filled, 16 * sum(dst.shape[0] // (P * FR) for dst, _ in fills))

        @block.tensor
        def _(pe):
            pe.wait_ge(hi_split, len(chunks) + 1)
            pe.wait_ge(lo_split, len(chunks) + 1)
            pe.wait_ge(ones_ready, 1)

            def project(out, w_cols):
                for k in range(KB):
                    last = split3(pe, out, (w_hi[:, k, w_cols], w_lo[:, k, w_cols]),
                                  (xT_hi[:, k, :], xT_lo[:, k, :]), k == 0, k == KB - 1)
                return last

            def v_piece(out, hg, b):
                cols = slice((2 * H + hg * HG) * DH, (2 * H + (hg + 1) * HG) * DH)
                tok = slice(b * N, (b + 1) * N)
                for k in range(KB):
                    last = split3(pe, out, (xT_hi[:, k, tok], xT_lo[:, k, tok]),
                                  (w_hi[:, k, cols], w_lo[:, k, cols]), k == 0, k == KB - 1)
                return last

            with pe.Fori(0, G) as g:
                pe.wait_ge(x_for_T_loaded, g * 16 + 16)
                pe.wait_ge(o_ready, g * H)
                for k in range(KB):
                    for b in range(GB):
                        last = pe.transpose(ps_xT[:, k, b * N:(b + 1) * N], x_for_T[:, b, k * P:(k + 1) * P], ident)
                last.then_inc(xT_in_psum, 1)
                pe.wait_ge(xT_hi_ready, g + 1)
                pe.wait_ge(xT_lo_ready, g + 1)
                for n in range(EARLY):
                    if n >= 2:
                        pe.wait_ge(v_ready, g * NV + n - 1)
                    v_piece((ps_qv, ps_k)[n % 2][:], 0, n).then_inc(v_in_psum, 1)
                pe.wait_ge(v_ready, g * NV + EARLY)
                for b in range(GB):
                    tok = slice(b * N, (b + 1) * N)
                    for k in range(KB):
                        last = split3(pe, ps_gate[:, b, :], (xT_hi[:, k, tok], xT_lo[:, k, tok]),
                                      (wg_hi[:, k, :], wg_lo[:, k, :]), k == 0, k == KB - 1)
                last.then_inc(gate_in_psum, 1)

                made = EARLY
                for h in range(H + 2):
                    if h < H:
                        pe.wait_ge(v_ready, g * NV + made)
                        project(ps_qv[:], slice(h * DH, (h + 1) * DH)).then_inc(q_in_psum, 1)
                    if h >= 2:
                        pe.wait_ge(o_ready, g * H + h - 1)
                        pe.wait_ge(oT_hi_ready, g * H + h - 2)
                        pe.wait_ge(oT_lo_ready, g * H + h - 2)
                        for b in range(GB):
                            last = pe.transpose(ps_oT[:, b * N:(b + 1) * N], o_norm[:, b, :], ident)
                        last.then_inc(oT_in_psum, 1)
                    if h < H:
                        pe.wait_ge(k_ready, g * H + h)
                        if h == 0:
                            pe.wait_ge(gate_exp_ready, g + 1)
                        project(ps_k[:], slice((H + h) * DH, (H + h + 1) * DH)).then_inc(k_in_psum, 1)
                    if h < H:
                        pe.wait_ge(q_ready, g * H + h + 1)
                    if 1 <= h <= NV - EARLY:
                        v_piece(ps_qv[:], (h - 1) // GB + 1, (h - 1) % GB).then_inc(v_in_psum, 1)
                        made += 1
                    if h < H:
                        pe.wait_ge(k_ready, g * H + h + 1)
                        pe.wait_ge(capped_ready, g * H + h)
                        for b in range(GB):
                            tok = slice(b * N, (b + 1) * N)
                            last = pe.matmul(ps_s[:, tok], kT[:, tok], qT[:, tok], start=True, stop=True,
                                             skip_group_check=True)
                        last.then_inc(s_in_psum, 1)
                    if 1 <= h <= H:
                        pe.wait_ge(probs_ready, g * H + h)
                        pe.wait_ge(v_ready, g * NV + ((h - 1) // HG + 1) * GB)
                        pe.wait_ge(o_ready, g * H + h - 1)
                        for b in range(GB):
                            last = pe.matmul(ps_o[:, b, 0:VW], probs[:, (h - 1) % 2, b * N:(b + 1) * N],
                                             v[:, (h - 1) // HG % 2, b, (h - 1) % HG, :], start=True, stop=True,
                                             skip_group_check=True)
                        last.then_inc(o_in_psum, 1)
                    if h >= 2:
                        pe.wait_ge(oT_hi_ready, g * H + h - 1)
                        pe.wait_ge(oT_lo_ready, g * H + h - 1)
                        if h == 2:
                            pe.wait_ge(sum_ready, g)
                        for b in range(GB):
                            tok = slice(b * N, (b + 1) * N)
                            last = split3(pe, ps_acc[:, b, :], (oT_hi[:, tok], oT_lo[:, tok]),
                                          (wo_hi[:, h - 2, :], wo_lo[:, h - 2, :]), h == 2 and b % 2 == 0,
                                          h == H + 1)
                last.then_inc(acc_in_psum, 1)

        @block.scalar
        def _(act):
            for n, (_, hi, _, k) in enumerate(chunks):
                act.wait_ge(raw_loaded[n % NRAW], 16 * (n // NRAW + 1))
                act.activation(hi, raw_chunk(n, k), ACT.Copy).then_inc(hi_split, 1)
            act.wait_ge(gates_loaded, 16)
            act.activation(wg_hi[:], wg_raw[:], ACT.Copy).then_inc(hi_split, 1)
            with act.Fori(0, G) as g:
                act.wait_ge(xT_in_psum, g + 1)
                act.activation(xT_hi[:], ps_xT, ACT.Copy).then_inc(xT_hi_ready, 1)
                act.wait_ge(gate_in_psum, g + 1)
                act.wait_ge(gate_ready, g)
                act.activation(gate_exp[:], ps_gate, ACT.Exp, scale=-1.0).then_inc(gate_exp_ready, 1)
                for h in range(H + 2):
                    if h < H:
                        act.wait_ge(q_in_psum, g * H + h + 1)
                        act.activation(qT[:], ps_qv[:], ACT.Copy).then_inc(q_ready, 1)
                    if h >= 2:
                        act.wait_ge(oT_in_psum, g * H + h - 1)
                        act.activation(oT_hi[:], ps_oT[:], ACT.Copy).then_inc(oT_hi_ready, 1)
                    if h < H:
                        act.wait_ge(s_in_psum, g * H + h + 1)
                        act.wait_ge(exp_ready, g * H + h)
                        act.activation(capped[:], ps_s[:], ACT.Tanh, scale=SCALE / SOFTCAP).then_inc(capped_ready, 1)
                        act.wait_ge(capped_ready, g * H + h + 1)
                        if h >= 2:
                            act.wait_ge(o_in_psum, g * H + h - 1)
                        else:
                            act.wait_ge(o_in_psum, g * H)
                        act.activation(probs[:, h % 2, :], capped[:], ACT.Exp, scale=SOFTCAP).then_inc(exp_ready, 1)
                layer_norm_std(act, agg, std, eps, ln_steps, std_ready, g)

        @block.gpsimd
        def _(pool):
            pool.wait_ge(ones_ready, 2)
            pool.affine_select(out=causal[:], in_=causal[:], compare_op=ALU.is_ge, fill=0.0, base=0,
                               pattern=[[1, N]], channel_multiplier=-1).then_inc(causal_ready, 1)
            pool.wait_ge(causal_ready, 1)
            with pool.Fori(0, G) as g:
                for h in range(H):
                    pool.wait_ge(exp_ready, g * H + h + 1)
                    half = probs[:, h % 2, :].rearrange("p (b i) -> p b i", b=GB)
                    pool.tensor_tensor(half, half, causal[:].unsqueeze(1).broadcast_to([P, GB, N]), ALU.mult)\
                        .then_inc(probs_ready, 1)

        @block.vector
        def _(dve):
            dve.memset(v[:, :, :, :, DH:VW], 1.0).then_inc(ones_ready, 1)
            dve.memset(causal[:], 1.0).then_inc(ones_ready, 1)
            for n, (_, hi, lo, k) in enumerate(chunks):
                dve.wait_ge(hi_split, n + 1)
                dve.tensor_tensor(lo, raw_chunk(n, k), hi.bitcast(F32), ALU.subtract).then_inc(lo_split, 1)
            dve.wait_ge(hi_split, len(chunks) + 1)
            dve.tensor_tensor(wg_lo[:], wg_raw[:], wg_hi[:].bitcast(F32), ALU.subtract).then_inc(lo_split, 1)

            def v_copy(bank, hg, b):
                dve.tensor_copy(v[:, hg % 2, b, :, 0:DH],
                                bank[:].rearrange("p (h d) -> p h d", h=HG)).then_inc(v_ready, 1)

            with dve.Fori(0, G) as g:
                dve.wait_ge(xT_hi_ready, g + 1)
                dve.tensor_tensor(xT_lo[:], ps_xT, xT_hi[:].bitcast(F32), ALU.subtract).then_inc(xT_lo_ready, 1)
                for n in range(EARLY):
                    dve.wait_ge(v_in_psum, g * NV + n + 1)
                    v_copy((ps_qv, ps_k)[n % 2], 0, n)
                dve.wait_ge(gate_exp_ready, g + 1)
                dve.tensor_scalar(gate_den[:], gate_exp[:], 1.0, None, ALU.add).then_inc(gate_ready, 1)
                made = EARLY
                for h in range(H + 2):
                    if h >= 2:
                        dve.wait_ge(oT_hi_ready, g * H + h - 1)
                        dve.tensor_tensor(oT_lo[:], ps_oT[:], oT_hi[:].bitcast(F32), ALU.subtract)\
                           .then_inc(oT_lo_ready, 1)
                    if h < H:
                        dve.wait_ge(k_in_psum, g * H + h + 1)
                        dve.tensor_copy(kT[:], ps_k[:]).then_inc(k_ready, 1)
                    if 1 <= h <= NV - EARLY:
                        made += 1
                        dve.wait_ge(v_in_psum, g * NV + made)
                        v_copy(ps_qv, (h - 1) // GB + 1, (h - 1) % GB)
                    if 1 <= h <= H:
                        dve.wait_ge(o_in_psum, g * H + h)
                        if h == 1:
                            dve.wait_ge(gate_ready, g + 1)
                        dve.tensor_tensor(o_den[:], ps_o[:, :, DH], gate_den[:, :, h - 1], ALU.mult)\
                           .then_inc(o_steps, 1)
                        dve.wait_ge(o_steps, g * 2 * H + 2 * h - 1)
                        dve.reciprocal(o_scale[:], o_den[:]).then_inc(o_steps, 1)
                        dve.wait_ge(o_steps, g * 2 * H + 2 * h)
                        if h >= 2:
                            dve.wait_ge(oT_in_psum, g * H + h - 1)
                        dve.tensor_tensor(o_norm[:], ps_o[:, :, 0:DH],
                                          o_scale[:].unsqueeze(2).broadcast_to([P, GB, DH]), ALU.mult)\
                           .then_inc(o_ready, 1)
                dve.wait_ge(acc_in_psum, g + 1)
                dve.wait_ge(x_res_loaded, g * 16 + 16)
                dve.wait_ge(x1_stored, g * 16)
                dve.tensor_tensor(x_out, ps_acc[:], x_res, ALU.add).then_inc(sum_ready, 1)
                dve.wait_ge(sum_ready, g + 1)
                layer_norm(dve, x_out, x_out, stats, agg, std, rstd, ln_steps, std_ready, g, tick[:]).then_inc(x1_ready, 1)


def convolution_stage(nc, ident, eps, x1, ctx_in, k, skip_in, padded_kernels, x2):
    B, C, L = x1.shape
    H = k.shape[0]
    NI = C // H
    G = B // GB
    LB = L // P
    assert (C, LB, GB * NI * NI) == (P, 2, 256)

    x1_src = x1.rearrange("b p c -> p b c")
    ctx_src = ctx_in.rearrange("b p c -> p b c")
    x2_dst = x2.rearrange("b p c -> p b c")
    row = H * (P + L)
    toeplitz_src = bass.AP(padded_kernels.tensor, P, [[row - 1, P], [P + L, H], [1, L]])

    with ExitStack() as ctx:
        s = Scope(nc, ctx, "cv_")
        toeplitz = s.sb("toeplitz", [P, H, L])
        zeros = s.sb("zeros", [P, H, P])
        same_head, skip = s.sb("same_head", [P, P]), s.sb("skip", [P, 1])
        x1_nat, c_nat, out_nat = s.sb("x1_nat", [P, GB, L]), s.sb("c_nat", [P, GB, L]), s.sb("out_nat", [P, GB, L])
        skipped = s.sb("skipped", [P, GB, L])
        vT, cT = s.sb("vT", [P, LB, GB, C]), s.sb("cT", [P, LB, GB, C])
        pairs = s.sb("pairs", [P, 2, LB * GB, NI, NI])
        weighted = s.sb("weighted", [P, 2, LB * GB, NI, NI])
        outT = s.sb("outT", [P, LB, GB, C])
        stats, agg = s.sb("stats", [P, GB, 6]), s.sb("agg", [P, GB, 2])
        std, rstd, tick = s.sb("std", [P, GB]), s.sb("rstd", [P, GB]), s.sb("tick", [P, 1])
        ps_v, ps_c = s.ps("ps_v", [P, GB * L]), s.ps("ps_c", [P, GB * L])
        ps_y = [s.ps(f"ps_y{n}", [P, LB * GB, NI, NI]) for n in range(2)]

        zeros_ready, pad_stored, kernels_stored, toeplitz_loaded, skip_loaded = (s.sem(n) for n in (
            "zeros_ready", "pad_stored", "kernels_stored", "toeplitz_loaded", "skip_loaded"))
        band_steps, same_head_ready = s.sem("band_steps"), s.sem("same_head_ready")
        x1_loaded, c_loaded, x2_stored = s.sem("x1_loaded"), s.sem("c_loaded"), s.sem("x2_stored")
        v_in_psum, c_in_psum, vT_ready, cT_ready = (s.sem(n) for n in ("v_in_psum", "c_in_psum", "vT_ready", "cT_ready"))
        pairs_ready, y_in_psum, weighted_ready, head_out = (
            s.sem(n) for n in ("pairs_ready", "y_in_psum", "weighted_ready", "head_out"))
        skipped_ready, result_in_psum, skip_in_psum = (s.sem(n) for n in ("skipped_ready", "result_in_psum", "skip_in_psum"))
        sum_steps, ln_steps, std_ready, x2_ready = (s.sem(n) for n in ("sum_steps", "ln_steps", "std_ready", "x2_ready"))

        block = ctx.enter_context(nc.Block())

        @block.sync
        def _(sp):
            sp.wait_ge(zeros_ready, 1)
            sp.dma_start(padded_kernels[:, :, 0:P], zeros[:]).then_inc(pad_stored, 16)
            sp.dma_start(padded_kernels[:, :, P:P + L], k.unsqueeze(0).broadcast_to([P, H, L]))\
                .then_inc(kernels_stored, 16)
            sp.dma_start(skip[:], skip_in.rearrange("(p a) -> p a", a=1)).then_inc(skip_loaded, 16)
            sp.wait_ge(pad_stored, 16)
            sp.wait_ge(kernels_stored, 16)
            sp.dma_start(toeplitz[:], toeplitz_src).then_inc(toeplitz_loaded, 16)
            with sp.Fori(0, G) as g:
                sp.wait_ge(x2_ready, g)
                sp.dma_start(x1_nat[:], x1_src[:, bass.ds(g * GB, GB), :]).then_inc(x1_loaded, 16)
                sp.dma_start(c_nat[:], ctx_src[:, bass.ds(g * GB, GB), :]).then_inc(c_loaded, 16)
                sp.wait_ge(x2_ready, g + 1)
                sp.dma_start(x2_dst[:, bass.ds(g * GB, GB), :], out_nat[:]).then_inc(x2_stored, 16)
            sp.wait_ge(x2_stored, 16 * G)

        @block.tensor
        def _(pe):
            pe.wait_ge(toeplitz_loaded, 16)
            pe.wait_ge(same_head_ready, 1)
            with pe.Fori(0, G) as g:
                pe.wait_ge(sum_steps, g * 3)
                pe.wait_ge(x1_loaded, g * 16 + 16)
                for lb in range(LB):
                    for b in range(GB):
                        last = pe.transpose(ps_v[:, (lb * GB + b) * C:(lb * GB + b + 1) * C],
                                            x1_nat[:, b, lb * P:(lb + 1) * P], ident)
                last.then_inc(v_in_psum, 1)
                pe.wait_ge(c_loaded, g * 16 + 16)
                for lb in range(LB):
                    for b in range(GB):
                        last = pe.transpose(ps_c[:, (lb * GB + b) * C:(lb * GB + b + 1) * C],
                                            c_nat[:, b, lb * P:(lb + 1) * P], ident)
                last.then_inc(c_in_psum, 1)
                for h in range(H):
                    pe.wait_ge(pairs_ready, g * H + h + 1)
                    if h >= 2:
                        pe.wait_ge(weighted_ready, g * H + h - 1)
                    y = ps_y[h % 2]
                    half = LB * GB // 2
                    pe.matmul(y[:], toeplitz[:, h, 0:P], pairs[:, h % 2], start=True, stop=False, skip_group_check=True)
                    pe.matmul(y[:, half:2 * half], toeplitz[:, h, P:L], pairs[:, h % 2, 0:half], start=False,
                              stop=True, skip_group_check=True).then_inc(y_in_psum, 1)
                pe.wait_ge(skipped_ready, g + 1)
                pe.wait_ge(cT_ready, g + 1)
                for n in range(2):
                    half = slice(n * 512, (n + 1) * 512)
                    last = pe.matmul(ps_c[:, half], same_head[:],
                                     skipped[:].rearrange("p b l -> p (b l)")[:, half], start=True, stop=True)
                last.then_inc(skip_in_psum, 1)
                pe.wait_ge(head_out, g * H + H)
                for b in range(GB):
                    for lb in range(LB):
                        last = pe.transpose(ps_v[:, b * L + lb * P:b * L + (lb + 1) * P], outT[:, lb, b, :], ident)
                last.then_inc(result_in_psum, 1)

        @block.scalar
        def _(act):
            with act.Fori(0, G) as g:
                act.wait_ge(v_in_psum, g + 1)
                act.activation(vT[:].rearrange("p a b c -> p (a b c)"), ps_v[:], ACT.Copy).then_inc(vT_ready, 1)
                act.wait_ge(c_in_psum, g + 1)
                act.activation(cT[:].rearrange("p a b c -> p (a b c)"), ps_c[:], ACT.Copy).then_inc(cT_ready, 1)
                layer_norm_std(act, agg, std, eps, ln_steps, std_ready, g)

        @block.gpsimd
        def _(pool):
            pool.memset(zeros[:], 0.0).then_inc(zeros_ready, 1)
            pool.memset(same_head[:], 1.0).then_inc(band_steps, 1)
            pool.wait_ge(band_steps, 1)
            grid = same_head[:].rearrange("p (h j) -> p h j", h=H)
            pool.affine_select(out=grid, in_=grid, compare_op=ALU.is_ge, fill=0.0, base=0,
                               pattern=[[-NI, H], [0, NI]], channel_multiplier=1).then_inc(band_steps, 1)
            pool.wait_ge(band_steps, 2)
            pool.affine_select(out=grid, in_=grid, compare_op=ALU.is_ge, fill=0.0, base=NI - 1,
                               pattern=[[NI, H], [0, NI]], channel_multiplier=-1).then_inc(same_head_ready, 1)
            with pool.Fori(0, G) as g:
                pool.wait_ge(vT_ready, g + 1)
                pool.wait_ge(cT_ready, g + 1)
                for h in range(H):
                    if h >= 2:
                        pool.wait_ge(y_in_psum, g * H + h - 1)
                    else:
                        pool.wait_ge(y_in_psum, g * H)
                    ch = slice(h * NI, (h + 1) * NI)
                    vh = vT[:].rearrange("p a b c -> p (a b) c")[:, :, ch].unsqueeze(3)
                    chh = cT[:].rearrange("p a b c -> p (a b) c")[:, :, ch].unsqueeze(2)
                    full = [P, LB * GB, NI, NI]
                    pool.tensor_tensor(pairs[:, h % 2], vh.broadcast_to(full), chh.broadcast_to(full), ALU.mult)\
                        .then_inc(pairs_ready, 1)

        @block.vector
        def _(dve):
            dve.wait_ge(skip_loaded, 16)
            with dve.Fori(0, G) as g:
                dve.wait_ge(x1_loaded, g * 16 + 16)
                dve.wait_ge(c_loaded, g * 16 + 16)
                dve.wait_ge(skip_in_psum, g)
                dve.scalar_tensor_tensor(out=skipped[:], in0=x1_nat[:], scalar=skip[:], in1=c_nat[:],
                                         op0=ALU.mult, op1=ALU.mult).then_inc(skipped_ready, 1)
                dve.wait_ge(cT_ready, g + 1)
                for h in range(H + 1):
                    if h < H:
                        ch = slice(h * NI, (h + 1) * NI)
                        ci = cT[:].rearrange("p a b c -> p (a b) c")[:, :, ch].unsqueeze(3)
                        if h >= 2:
                            dve.wait_ge(head_out, g * H + h - 1)
                        else:
                            dve.wait_ge(head_out, g * H)
                        dve.wait_ge(y_in_psum, g * H + h + 1)
                        dve.tensor_tensor(weighted[:, h % 2], ps_y[h % 2][:], ci.broadcast_to([P, LB * GB, NI, NI]),
                                          ALU.mult).then_inc(weighted_ready, 1)
                    if h >= 1:
                        ch = slice((h - 1) * NI, h * NI)
                        if h == 1:
                            dve.wait_ge(result_in_psum, g)
                        dve.wait_ge(weighted_ready, g * H + h)
                        dve.tensor_reduce(outT[:].rearrange("p a b c -> p (a b) c")[:, :, ch],
                                          weighted[:, (h - 1) % 2].rearrange("p n i j -> p n j i"),
                                          AX.X, ALU.add).then_inc(head_out, 1)
                flat = out_nat[:].rearrange("p b l -> p (b l)")
                dve.wait_ge(x2_stored, g * 16)
                dve.wait_ge(skip_in_psum, g + 1)
                dve.tensor_tensor(flat, ps_c[:], c_nat[:].rearrange("p b l -> p (b l)"), ALU.mult).then_inc(sum_steps, 1)
                dve.wait_ge(sum_steps, g * 3 + 1)
                dve.tensor_tensor(flat, flat, x1_nat[:].rearrange("p b l -> p (b l)"), ALU.add).then_inc(sum_steps, 1)
                dve.wait_ge(sum_steps, g * 3 + 2)
                dve.wait_ge(result_in_psum, g + 1)
                dve.tensor_tensor(flat, flat, ps_v[:], ALU.add).then_inc(sum_steps, 1)
                dve.wait_ge(sum_steps, g * 3 + 3)
                layer_norm(dve, out_nat[:], out_nat[:], stats, agg, std, rstd, ln_steps, std_ready, g, tick[:])\
                    .then_inc(x2_ready, 1)


TOP_K = 6
CAP_FACTOR = 2
BLOCK = 256
FAR = 1 << 20


def routing_stage(nc, ident, x2, wg_router, ws_gate, ws_up, ws_down, queues, base, plan):
    B, N, D = x2.shape
    E = wg_router.shape[0]
    F = ws_gate.shape[1]
    KB = D // P
    CAP = queues.shape[0] // E
    W = D + 2
    T = GB * N
    NCHUNK = B // GB
    FB = [(f, min(P, F - f)) for f in range(0, F, P)]
    assert CAP == CAP_FACTOR * (B * N * TOP_K // E) and CAP == 3 * BLOCK and B * E == 512

    with ExitStack() as ctx:
        s = Scope(nc, ctx, "rt_")
        x2_nat, x2T = s.sb("x2_nat", [P, B, D]), s.sb("x2T", [P, KB, B * N])
        router, routerT = s.sb("router", [E, D]), s.sb("routerT", [P, KB, E])
        gate_w, up_w, down_w = s.sb("gate_w", [P, KB, F]), s.sb("up_w", [P, KB, F]), s.sb("down_w", [P, len(FB), D])
        silu, hidden = s.sb("silu", [P, 2, T]), s.sb("hidden", [P, 2, T])
        sharedT, summed = s.sb("sharedT", [P, KB, T]), s.sb("summed", [P, GB, D])
        logits, top, top_i = s.sb("logits", [P, B, E]), s.sb("top", [P, B, 8]), s.sb("top_i", [P, B, 8], U32)
        shifted, top_shifted = s.sb("shifted", [P, B, E]), s.sb("top_shifted", [P, B, 8])
        expd, top_expd = s.sb("expd", [P, B, E]), s.sb("top_expd", [P, B, 8])
        norm, top_p = s.sb("norm", [P, B]), s.sb("top_p", [P, B, TOP_K])
        top_sum = s.sb("top_sum", [P, B])
        chosen, expert_no = s.sb("chosen", [P, B, TOP_K]), s.sb("expert_no", [P, E])
        top_no = s.sb("top_no", [P, B, TOP_K])
        one_hot, picked = s.sb("one_hot", [P, B, TOP_K, E]), s.sb("picked", [P, B, TOP_K, E])
        member = s.sb("member", [P, B, E])
        earlier, ones = s.sb("earlier", [P, P]), s.sb("ones", [P, P])
        before = s.sb("before", [P, B + 1, E])
        place, over, queue_start = s.sb("place", [P, B, E]), s.sb("over", [P, B, E]), s.sb("queue_start", [P, E])
        place_k, place_i = s.sb("place_k", [P, B, TOP_K]), s.sb("place_i", [P, B, TOP_K], U32)
        tags = s.sb("tags", [P, B, TOP_K, 2])
        rows = [s.sb(f"rows{n}", [P, TOP_K, W]) for n in range(2)]
        rows_i = [s.sb(f"rows_i{n}", [P, TOP_K], U32) for n in range(2)]
        blocks, over_block = s.sb("blocks", [1, E]), s.sb("over_block", [1, E])
        blocks_sum, one_row = s.sb("blocks_sum", [1, E]), s.sb("one_row", [1, E])

        ps_g = [s.ps(f"ps_g{n}", [P, T]) for n in range(2)]
        ps_u = [s.ps(f"ps_u{n}", [P, T]) for n in range(2)]
        ps_yT, ps_y = s.ps("ps_yT", [P, KB, T]), s.ps("ps_y", [P, GB, D])
        ps_x2T = [(ps_g[0], ps_g[1]), (ps_u[0], ps_u[1])]
        ps_logits = ps_yT[:, 0, :]
        ps_place = ps_y[:, 0:2, :].rearrange("p b c -> p (b c)")
        ps_total = ps_y[:, 2:4, :].rearrange("p b c -> p (b c)")

        x2_loaded, router_loaded, weights_loaded = s.sem("x2_loaded"), s.sem("router_loaded"), s.sem("weights_loaded")
        base_stored = s.sem("base_stored")
        constants, iotas = s.sem("constants"), s.sem("iotas")
        x2T_in_psum, x2T_ready = s.sem("x2T_in_psum"), s.sem("x2T_ready")
        routerT_in_psum, routerT_ready = s.sem("routerT_in_psum"), s.sem("routerT_ready")
        logits_copied, places_read = s.sem("logits_copied"), s.sem("places_read")
        logits_in_psum, shifted_ready, exp_ready = s.sem("logits_in_psum"), s.sem("shifted_ready"), s.sem("exp_ready")
        steps, member_ready, places_in_psum = s.sem("steps"), s.sem("member_ready"), s.sem("places_in_psum")
        rows_ready = [s.sem(f"rows_ready{n}") for n in range(2)]
        rows_scattered = [s.sem(f"rows_scattered{n}") for n in range(2)]
        gu_in_psum, silu_ready, hidden_ready, yT_in_psum, yT_ready, y_in_psum, summed_ready = (s.sem(n) for n in (
            "gu_in_psum", "silu_ready", "hidden_ready", "yT_in_psum", "yT_ready", "y_in_psum", "summed_ready"))

        block = ctx.enter_context(nc.Block())

        @block.sync
        def _(sp):
            sp.dma_start(router[:], wg_router).then_inc(router_loaded, 16)
            for c in range(NCHUNK):
                sp.dma_start(x2_nat[:, c * GB:(c + 1) * GB, :],
                             x2[c * GB:(c + 1) * GB].rearrange("b p c -> p b c")).then_inc(x2_loaded, 16)
                sp.wait_ge(x2_loaded, 16 * (c + 1))
            sp.dma_start(gate_w[:], ws_gate.rearrange("(k p) f -> p k f", p=P)).then_inc(weights_loaded, 16)
            sp.dma_start(up_w[:], ws_up.rearrange("(k p) f -> p k f", p=P)).then_inc(weights_loaded, 16)
            for n, (f, size) in enumerate(FB):
                sp.dma_start(down_w[0:size, n, :], ws_down[f:f + size, :]).then_inc(weights_loaded, 16)
            for c in range(NCHUNK):
                sp.wait_ge(summed_ready, c + 1)
                sp.dma_start(base[c * GB:(c + 1) * GB].rearrange("b p c -> p b c"), summed[:])\
                  .then_inc(base_stored, 16)
            sp.wait_ge(base_stored, 16 * NCHUNK)

        @block.tensor
        def _(pe):
            pe.wait_ge(router_loaded, 16)
            for k in range(KB):
                last = pe.transpose(ps_y[:, 0, k * E:(k + 1) * E], router[:, k * P:(k + 1) * P], ident[0:E, 0:E])
            last.then_inc(routerT_in_psum, 1)
            for c in range(NCHUNK):
                pe.wait_ge(x2_loaded, 16 * (c + 1))
                if c >= 2:
                    pe.wait_ge(x2T_ready, c - 1)
                for k in range(KB):
                    for b in range(GB):
                        last = pe.transpose(ps_x2T[c % 2][k][:, b * N:(b + 1) * N],
                                            x2_nat[:, c * GB + b, k * P:(k + 1) * P], ident)
                last.then_inc(x2T_in_psum, 1)
            pe.wait_ge(routerT_ready, 1)
            for b in range(B):
                pe.wait_ge(x2T_ready, b // GB + 1)
                for k in range(KB):
                    last = pe.matmul(ps_logits[:, b * E:(b + 1) * E], x2T[:, k, b * N:(b + 1) * N], routerT[:, k, :],
                                     start=k == 0, stop=k == KB - 1, skip_group_check=True)
            last.then_inc(logits_in_psum, 1)
            pe.wait_ge(weights_loaded, 16 * (2 + len(FB)))

            def gate_up(n):
                c, (f, size) = n // len(FB), FB[n % len(FB)]
                if n >= 2:
                    pe.wait_ge(hidden_ready, n - 1)
                for bank, w in ((ps_g[n % 2], gate_w), (ps_u[n % 2], up_w)):
                    for k in range(KB):
                        last = pe.matmul(bank[0:size, :], w[:, k, f:f + size], x2T[:, k, c * T:(c + 1) * T],
                                         start=k == 0, stop=k == KB - 1)
                last.then_inc(gu_in_psum, 1)

            def down(n):
                c, fb = n // len(FB), n % len(FB)
                size = FB[fb][1]
                pe.wait_ge(hidden_ready, n + 1)
                if n == 0:
                    pe.wait_ge(logits_copied, 1)
                elif fb == 0:
                    pe.wait_ge(yT_ready, c)
                for k in range(KB):
                    last = pe.matmul(ps_yT[:, k, :], down_w[0:size, fb, k * P:(k + 1) * P],
                                     hidden[0:size, n % 2, :], start=fb == 0, stop=fb == len(FB) - 1)
                if fb == len(FB) - 1:
                    last.then_inc(yT_in_psum, 1)

            def back(c):
                pe.wait_ge(yT_ready, c + 1)
                if c == 0:
                    pe.wait_ge(places_read, 1)
                else:
                    pe.wait_ge(summed_ready, c)
                for b in range(GB):
                    for k in range(KB):
                        last = pe.transpose(ps_y[:, b, k * P:(k + 1) * P], sharedT[:, k, b * N:(b + 1) * N], ident)
                last.then_inc(y_in_psum, 1)

            total = NCHUNK * len(FB)
            gate_up(0)
            gate_up(1)
            pe.wait_ge(member_ready, 1)
            pe.wait_ge(constants, 5)
            flat = member[:].rearrange("p b e -> p (b e)")
            pe.matmul(ps_place, earlier[:], flat, start=True, stop=True)
            pe.matmul(ps_total, ones[:], flat, start=True, stop=True).then_inc(places_in_psum, 1)
            for n in range(total):
                down(n)
                if n + 2 < total:
                    gate_up(n + 2)
                if n % len(FB) == 0 and n:
                    back(n // len(FB) - 1)
            back(NCHUNK - 1)

        def copy_result(act, c):
            act.wait_ge(yT_in_psum, c + 1)
            if c >= 1:
                act.wait_ge(y_in_psum, c)
            act.activation(sharedT[:], ps_yT[:], ACT.Copy).then_inc(yT_ready, 1)

        @block.scalar
        def _(act):
            act.wait_ge(routerT_in_psum, 1)
            act.activation(routerT[:].rearrange("p k e -> p (k e)"), ps_y[:, 0, 0:KB * E], ACT.Copy)\
               .then_inc(routerT_ready, 1)
            for c in range(NCHUNK):
                act.wait_ge(x2T_in_psum, c + 1)
                for k in range(KB):
                    last = act.activation(x2T[:, k, c * T:(c + 1) * T], ps_x2T[c % 2][k][:], ACT.Copy)
                last.then_inc(x2T_ready, 1)
            act.wait_ge(shifted_ready, 2)
            act.activation(expd[:], shifted[:], ACT.Exp).then_inc(exp_ready, 1)
            act.activation(top_expd[:], top_shifted[:], ACT.Exp).then_inc(exp_ready, 1)
            for n in range(NCHUNK * len(FB)):
                c, size = n // len(FB), FB[n % len(FB)][1]
                act.wait_ge(gu_in_psum, n + 1)
                if n >= 2:
                    act.wait_ge(hidden_ready, n - 1)
                act.activation(silu[0:size, n % 2, :], ps_g[n % 2][0:size, :], ACT.Silu).then_inc(silu_ready, 1)
                if n % len(FB) == 0 and n:
                    copy_result(act, c - 1)
            copy_result(act, NCHUNK - 1)

        @block.gpsimd
        def _(pool):
            pool.memset(earlier[:], 1.0).then_inc(iotas, 1)
            pool.wait_ge(iotas, 1)
            pool.affine_select(out=earlier[:], in_=earlier[:], compare_op=ALU.is_gt, fill=0.0, base=0,
                               pattern=[[1, P]], channel_multiplier=-1).then_inc(constants, 1)
            pool.memset(ones[:], 1.0).then_inc(constants, 1)
            pool.iota(expert_no[:], [[1, E]], base=0, channel_multiplier=0,
                      allow_small_or_imprecise_dtypes=True).then_inc(constants, 1)
            pool.iota(queue_start[:], [[CAP, E]], base=0, channel_multiplier=0,
                      allow_small_or_imprecise_dtypes=True).then_inc(constants, 1)
            pool.iota(tags[:, :, :, 1], [[N * TOP_K, B], [1, TOP_K]], base=0, channel_multiplier=TOP_K,
                      allow_small_or_imprecise_dtypes=True).then_inc(constants, 1)
            for b in range(B):
                pool.wait_ge(rows_ready[b % 2], b // 2 + 1)
                for k in range(TOP_K):
                    pool.indirect_dma_start(queues, bass.IndirectOffsetOnAxis(ap=rows_i[b % 2][:, k:k + 1], axis=0),
                                            rows[b % 2][:, k, :], None, bounds_check=E * CAP - 1,
                                            oob_is_err=False).then_inc(rows_scattered[b % 2], 16)
            for half in range(2):
                pool.wait_ge(rows_scattered[half], 16 * TOP_K * (B // 2))

        @block.vector
        def _(dve):
            count = [0]

            def step(instruction):
                count[0] += 1
                instruction.then_inc(steps, 1)
                dve.wait_ge(steps, count[0])

            def over_k(ap):
                return ap.unsqueeze(2).broadcast_to([P, B, TOP_K, E])

            dve.memset(before[:, 0, :], 0.0)
            dve.memset(one_row[:], 1.0)
            dve.wait_ge(logits_in_psum, 1)
            step(dve.tensor_copy(logits[:].rearrange("p b e -> p (b e)"), ps_logits))
            for b in range(B):
                last = dve.max(top[:, b, :], logits[:, b, :])
            last.then_inc(logits_copied, 1)
            dve.wait_ge(logits_copied, 1)
            for b in range(B):
                last = dve.max_index(top_i[:, b, :], top[:, b, :], logits[:, b, :])
            step(last)
            dve.tensor_tensor(shifted[:], logits[:], top[:, :, 0:1].broadcast_to([P, B, E]), ALU.subtract)\
               .then_inc(shifted_ready, 1)
            dve.tensor_tensor(top_shifted[:], top[:], top[:, :, 0:1].broadcast_to([P, B, 8]), ALU.subtract)\
               .then_inc(shifted_ready, 1)
            step(dve.tensor_copy(top_no[:], top_i[:, :, 0:TOP_K]))
            dve.wait_ge(constants, 5)
            flat_no = top_no[:].rearrange("p b k -> p (b k)").unsqueeze(2).broadcast_to([P, B * TOP_K, E])
            flat_hot = one_hot[:].rearrange("p b k e -> p (b k) e")
            step(dve.tensor_tensor(flat_hot, expert_no[:].unsqueeze(1).broadcast_to([P, B * TOP_K, E]), flat_no,
                                   ALU.is_equal))
            dve.tensor_reduce(member[:], one_hot[:].rearrange("p b k e -> p b e k"), AX.X, ALU.add)\
               .then_inc(member_ready, 1)
            dve.wait_ge(exp_ready, 2)
            step(dve.tensor_reduce(norm[:], expd[:], AX.X, ALU.add))
            step(dve.reciprocal(norm[:], norm[:]))
            step(dve.tensor_tensor(top_p[:], top_expd[:, :, 0:TOP_K],
                                   norm[:].unsqueeze(2).broadcast_to([P, B, TOP_K]), ALU.mult))
            step(dve.tensor_reduce(top_sum[:], top_p[:], AX.X, ALU.add))
            step(dve.tensor_scalar(top_sum[:], top_sum[:], 1e-20, None, ALU.add))
            step(dve.reciprocal(top_sum[:], top_sum[:]))
            step(dve.tensor_tensor(tags[:, :, :, 0], top_p[:], top_sum[:].unsqueeze(2).broadcast_to([P, B, TOP_K]),
                                   ALU.mult))
            dve.wait_ge(places_in_psum, 1)
            for b in range(B):
                step(dve.tensor_tensor(before[:, b + 1, :], before[:, b, :], ps_total[:, b * E:(b + 1) * E], ALU.add))
            step(dve.tensor_tensor(place[:], ps_place.rearrange("p (b e) -> p b e", b=B), before[:, 0:B, :], ALU.add))
            step(dve.tensor_scalar(over[:], place[:], float(CAP), float(FAR), ALU.is_ge, ALU.mult))
            step(dve.tensor_tensor(place[:], place[:], over[:], ALU.add))
            dve.tensor_tensor(place[:], place[:], queue_start[:].unsqueeze(1).broadcast_to([P, B, E]), ALU.add)\
               .then_inc(places_read, 1)
            dve.wait_ge(places_read, 1)
            step(dve.tensor_tensor(picked[:], one_hot[:], over_k(place[:]), ALU.mult))
            step(dve.tensor_reduce(place_k[:].rearrange("p b k -> p (b k)"),
                                   picked[:].rearrange("p b k e -> p (b k) e"), AX.X, ALU.add))
            step(dve.tensor_copy(place_i[:], place_k[:]))
            total = before[0:1, B, :]
            step(dve.tensor_scalar(blocks[:], total, float(BLOCK), 1.0, ALU.is_gt, ALU.add))
            step(dve.tensor_scalar(over_block[:], total, float(2 * BLOCK), None, ALU.is_gt))
            step(dve.tensor_tensor(blocks[:], blocks[:], over_block[:], ALU.add))
            step(dve.tensor_tensor_scan(blocks_sum[:], one_row[:], blocks[:], 0.0, ALU.mult, ALU.add))
            step(dve.tensor_copy(plan[0:1, 0, :], blocks[:]))
            step(dve.tensor_tensor(plan[0:1, 1, :], blocks_sum[:], blocks[:], ALU.subtract))

            def make_rows(b):
                half, turn = b % 2, b // 2
                if turn >= 1:
                    dve.wait_ge(rows_scattered[half], 16 * TOP_K * turn)
                dve.tensor_copy(rows[half][:, :, 0:D], x2_nat[:, b, :].unsqueeze(1).broadcast_to([P, TOP_K, D]))
                dve.tensor_copy(rows[half][:, :, D:W], tags[:, b])
                dve.tensor_copy(rows_i[half][:], place_i[:, b, :]).then_inc(rows_ready[half], 1)

            def make_hidden(n):
                size = FB[n % len(FB)][1]
                dve.wait_ge(silu_ready, n + 1)
                dve.tensor_tensor(hidden[0:size, n % 2, :], silu[0:size, n % 2, :], ps_u[n % 2][0:size, :], ALU.mult)\
                   .then_inc(hidden_ready, 1)

            def make_sum(c):
                dve.wait_ge(y_in_psum, c + 1)
                if c >= 1:
                    dve.wait_ge(base_stored, 16 * c)
                dve.tensor_tensor(summed[:], ps_y[:], x2_nat[:, c * GB:(c + 1) * GB, :], ALU.add)\
                   .then_inc(summed_ready, 1)

            make_rows(0)
            make_rows(1)
            b = 2
            for n in range(NCHUNK * len(FB)):
                make_hidden(n)
                if n % len(FB) == 1 and n >= len(FB):
                    make_sum(n // len(FB) - 1)
            for b in range(2, B):
                make_rows(b)
                if b == 2:
                    make_sum(NCHUNK - 1)


def expert_stage(nc, ident, queues, w_gate, w_up, w_down, plan, results):
    E, D, F = w_gate.shape
    KB = D // P
    CAP = queues.shape[0] // E
    MAXB = CAP // BLOCK
    SUB = BLOCK // P
    FB = 2
    FS = F // FB
    W = D + 2
    assert FS * FB == F and FS <= P and SUB == 2

    with ExitStack() as ctx:
        s = Scope(nc, ctx, "ex_")
        rows, rowsT = s.sb("rows", [P, SUB, W]), s.sb("rowsT", [P, KB, BLOCK])
        gate_up = [s.sb(f"gate_up{n}", [P, KB, 2 * F]) for n in range(2)]
        down = [s.sb(f"down{n}", [FS, FB, D]) for n in range(2)]
        silu, hidden = s.sb("silu", [P, SUB, F]), s.sb("hidden", [P, SUB, F])
        hiddenT = s.sb("hiddenT", [FS, SUB, FB, P])
        tags_next, tags = s.sb("tags_next", [P, SUB, 2]), s.sb("tags", [P, SUB, 2])
        number = [s.sb(f"number{n}", [P, 1], U32) for n in range(SUB)]
        out = [s.sb(f"out{n}", [P, D]) for n in range(SUB)]
        tick = s.sb("tick", [P, 2])

        ps_rowsT = s.ps("ps_rowsT", [P, KB, BLOCK])
        ps_gu = [s.ps(f"ps_gu{n}", [P, 512]) for n in range(SUB)]
        ps_hT = [s.ps(f"ps_hT{n}", [P, 512]) for n in range(SUB)]
        ps_out = [s.ps(f"ps_out{n}", [P, 512]) for n in range(SUB)]

        rows_loaded, rowsT_in_psum, rowsT_ready, tags_taken = (
            s.sem(n) for n in ("rows_loaded", "rowsT_in_psum", "rowsT_ready", "tags_taken"))
        weights_loaded = [s.sem(f"weights_loaded{n}") for n in range(2)]
        weights_used = [s.sem(f"weights_used{n}") for n in range(2)]
        gu_in_psum = [s.sem(f"gu_in_psum{n}") for n in range(SUB)]
        silu_ready = [s.sem(f"silu_ready{n}") for n in range(SUB)]
        hidden_ready = [s.sem(f"hidden_ready{n}") for n in range(SUB)]
        hT_in_psum = [s.sem(f"hT_in_psum{n}") for n in range(SUB)]
        hT_ready = [s.sem(f"hT_ready{n}") for n in range(SUB)]
        out_in_psum = [s.sem(f"out_in_psum{n}") for n in range(SUB)]
        out_ready = [s.sem(f"out_ready{n}") for n in range(SUB)]
        scattered = [s.sem(f"scattered{n}") for n in range(SUB)]
        tags_ready, tick_ready = s.sem("tags_ready"), s.sem("tick_ready")

        def for_blocks(eng, body, before_expert=None, after_expert=None):
            with eng.Fori(0, E // 2) as pair:
                for half in range(2):
                    e = pair * 2 + half
                    blocks = eng.value_load(plan[0:1, 0, bass.ds(e, 1)], min_val=1, max_val=MAXB)
                    start = eng.value_load(plan[0:1, 1, bass.ds(e, 1)], min_val=0, max_val=MAXB * E)
                    with eng.Fori(0, blocks) as i:
                        body(start + i, half, pair, e, i)
                    if after_expert:
                        after_expert(half, pair, e)

        block = ctx.enter_context(nc.Block())

        @block.sync
        def _(sp):
            def load_rows(first_row):
                sp.dma_start(rows[:], queues[bass.ds(first_row, BLOCK), :].rearrange("(a p) w -> p a w", p=P))\
                  .then_inc(rows_loaded, 16)

            def load_weights(half, e):
                sp.dma_start(gate_up[half][:, :, 0:F], w_gate[bass.ds(e, 1)].rearrange("e (k p) f -> p (e k) f", p=P))\
                  .then_inc(weights_loaded[half], 16)
                sp.dma_start(gate_up[half][:, :, F:2 * F], w_up[bass.ds(e, 1)].rearrange("e (k p) f -> p (e k) f", p=P))\
                  .then_inc(weights_loaded[half], 16)
                sp.dma_start(down[half][:], w_down[bass.ds(e, 1)].rearrange("e (b p) c -> p (e b) c", p=FS))\
                  .then_inc(weights_loaded[half], 16)

            def body(n, half, pair, e, i):
                sp.wait_ge(rowsT_in_psum, n)
                sp.wait_ge(tags_taken, n)
                load_rows((e * MAXB + i) * BLOCK)

            def next_weights(half, pair, e):
                if half == 0:
                    sp.wait_ge(weights_used[1], pair)
                    load_weights(1, e + 1)
                else:
                    sp.wait_ge(weights_used[0], pair + 1)
                    load_weights(0, (e + 1) % E)

            load_weights(0, 0)
            for_blocks(sp, body, after_expert=next_weights)
            blocks_in_all = sp.value_load(plan[0:1, 0, E - 1:E], min_val=1, max_val=MAXB) + \
                sp.value_load(plan[0:1, 1, E - 1:E], min_val=0, max_val=MAXB * E)
            sp.wait_ge(rowsT_in_psum, blocks_in_all)
            sp.wait_ge(tags_taken, blocks_in_all)
            load_rows(0)
            sp.wait_ge(weights_loaded[0], 16 * 3 * (E // 2 + 1))

        @block.tensor
        def _(pe):
            def transpose_rows(n):
                pe.wait_ge(rows_loaded, n * 16 + 16)
                for k in range(KB):
                    for a in range(SUB):
                        last = pe.transpose(ps_rowsT[:, k, a * P:(a + 1) * P], rows[:, a, k * P:(k + 1) * P], ident)
                last.then_inc(rowsT_in_psum, 1)

            def body(n, half, pair, e, i):
                pe.wait_ge(rowsT_ready, n + 1)
                pe.wait_ge(weights_loaded[half], pair * 48 + 48)
                for a in range(SUB):
                    pe.wait_ge(hidden_ready[a], n)
                    for k in range(KB):
                        last = pe.matmul(ps_gu[a][:, 0:2 * F], rowsT[:, k, a * P:(a + 1) * P], gate_up[half][:, k, :],
                                         start=k == 0, stop=k == KB - 1)
                    last.then_inc(gu_in_psum[a], 1)
                transpose_rows(n + 1)
                for a in range(SUB):
                    pe.wait_ge(hidden_ready[a], n + 1)
                    pe.wait_ge(hT_ready[a], n)
                    for b in range(FB):
                        last = pe.transpose(ps_hT[a][0:FS, b * P:(b + 1) * P], hidden[:, a, b * FS:(b + 1) * FS], ident)
                    last.then_inc(hT_in_psum[a], 1)
                for a in range(SUB):
                    pe.wait_ge(hT_ready[a], n + 1)
                    pe.wait_ge(out_ready[a], n)
                    for b in range(FB):
                        last = pe.matmul(ps_out[a][:, 0:D], hiddenT[:, a, b, :], down[half][:, b, :],
                                         start=b == 0, stop=b == FB - 1)
                    last.then_inc(out_in_psum[a], 1)

            def expert_done(half, pair, e):
                pe.transpose(ps_hT[1][0:FS, 2 * P:3 * P], ident[:, 0:FS], ident).then_inc(weights_used[half], 1)

            transpose_rows(0)
            for_blocks(pe, body, after_expert=expert_done)

        @block.scalar
        def _(act):
            def copy_rowsT(n):
                act.wait_ge(rowsT_in_psum, n + 1)
                act.activation(rowsT[:], ps_rowsT[:], ACT.Copy).then_inc(rowsT_ready, 1)

            def body(n, half, pair, e, i):
                for a in range(SUB):
                    act.wait_ge(gu_in_psum[a], n + 1)
                    act.activation(silu[:, a, :], ps_gu[a][:, 0:F], ACT.Silu).then_inc(silu_ready[a], 1)
                copy_rowsT(n + 1)

            copy_rowsT(0)
            for_blocks(act, body)

        @block.gpsimd
        def _(pool):
            pool.memset(tick[:], 0.0).then_inc(tick_ready, 1)
            pool.wait_ge(tick_ready, 1)

            def body(n, half, pair, e, i):
                for a in range(SUB):
                    pool.wait_ge(out_ready[a], n + 1)
                    pool.wait_ge(tick_ready, n * SUB + a + 1)
                    pool.tensor_tensor(tick[:, 1:2], tick[:, 0:1], tick[:, 0:1], ALU.mult).then_inc(tick_ready, 1)
                    pool.indirect_dma_start(results, bass.IndirectOffsetOnAxis(ap=number[a][:], axis=0), out[a][:],
                                            None, bounds_check=results.shape[0] - 1, oob_is_err=False)\
                        .then_inc(scattered[a], 16)

            for_blocks(pool, body)
            blocks_in_all = pool.value_load(plan[0:1, 0, E - 1:E], min_val=1, max_val=MAXB) + \
                pool.value_load(plan[0:1, 1, E - 1:E], min_val=0, max_val=MAXB * E)
            for a in range(SUB):
                pool.wait_ge(scattered[a], blocks_in_all * 16)

        @block.vector
        def _(dve):
            def take_tags(n):
                dve.wait_ge(rows_loaded, n * 16 + 16)
                dve.tensor_copy(tags_next[:], rows[:, :, D:W]).then_inc(tags_taken, 1)

            def body(n, half, pair, e, i):
                dve.wait_ge(out_ready[SUB - 1], n)
                dve.wait_ge(tags_taken, n + 1)
                dve.tensor_copy(tags[:], tags_next[:]).then_inc(tags_ready, 1)
                for a in range(SUB):
                    dve.wait_ge(silu_ready[a], n + 1)
                    dve.tensor_tensor(hidden[:, a, :], silu[:, a, :], ps_gu[a][:, F:2 * F], ALU.mult)\
                       .then_inc(hidden_ready[a], 1)
                dve.wait_ge(tags_ready, n + 1)
                take_tags(n + 1)
                for a in range(SUB):
                    dve.wait_ge(hT_in_psum[a], n + 1)
                    dve.tensor_copy(hiddenT[:, a, :, :].rearrange("p b t -> p (b t)"), ps_hT[a][0:FS, 0:FB * P])\
                       .then_inc(hT_ready[a], 1)
                for a in range(SUB):
                    dve.wait_ge(scattered[a], n * 16)
                    dve.tensor_copy(number[a][:], tags[:, a, 1:2])
                    dve.wait_ge(out_in_psum[a], n + 1)
                    dve.tensor_scalar(out[a][:], ps_out[a][:, 0:D], tags[:, a, 0:1], None, ALU.mult)\
                       .then_inc(out_ready[a], 1)

            take_tags(0)
            for_blocks(dve, body)


def combination_stage(nc, eps, base, results, out):
    B, N, D = base.shape
    NBUF = 4
    res_in = results.rearrange("(b p k) c -> b p k c", p=P, k=TOP_K)

    with ExitStack() as ctx:
        s = Scope(nc, ctx, "co_")
        res, bas = s.sb("res", [P, NBUF, TOP_K, D]), s.sb("bas", [P, NBUF, D])
        summed, normed = s.sb("summed", [P, 2, D]), s.sb("normed", [P, 2, D])
        stats, agg = s.sb("stats", [P, 1, 6]), s.sb("agg", [P, 1, 2])
        std, rstd, tick = s.sb("std", [P, 1]), s.sb("rstd", [P, 1]), s.sb("tick", [P, 1])
        loaded = [s.sem(f"loaded{n}") for n in range(NBUF)]
        tile_summed = [s.sem(f"tile_summed{n}") for n in range(NBUF)]
        stored = [s.sem(f"stored{n}") for n in range(2)]
        sum_steps, ln_steps, std_ready, normed_ready = (
            s.sem(n) for n in ("sum_steps", "ln_steps", "std_ready", "normed_ready"))

        block = ctx.enter_context(nc.Block())

        @block.sync
        def _(sp):
            with sp.Fori(0, B // NBUF) as turn:
                for n in range(NBUF):
                    b = turn * NBUF + n
                    sp.wait_ge(tile_summed[n], turn)
                    sp.dma_start(res[:, n], res_in[bass.ds(b, 1)].rearrange("b p k c -> p (b k) c"))\
                      .then_inc(loaded[n], 16)
                    sp.dma_start(bas[:, n], base[bass.ds(b, 1)].rearrange("b p c -> p (b c)")).then_inc(loaded[n], 16)

        @block.scalar
        def _(act):
            with act.Fori(0, B // 2) as pair:
                for half in range(2):
                    b = pair * 2 + half
                    layer_norm_std(act, agg, std, eps, ln_steps, std_ready, b)
                    act.wait_ge(normed_ready, b + 1)
                    act.dma_start(out[bass.ds(b, 1)].rearrange("b p c -> p (b c)"), normed[:, half])\
                       .then_inc(stored[half], 16)
            for half in range(2):
                act.wait_ge(stored[half], 16 * (B // 2))

        @block.vector
        def _(dve):
            with dve.Fori(0, B // NBUF) as turn:
                for n in range(NBUF):
                    b = turn * NBUF + n
                    half = n % 2
                    dve.wait_ge(loaded[n], turn * 32 + 32)
                    dve.wait_ge(ln_steps, b * 3)
                    dve.tensor_reduce(summed[:, half], res[:, n].rearrange("p k c -> p c k"), AX.X, ALU.add)\
                       .then_inc(sum_steps, 1)
                    dve.wait_ge(sum_steps, b + 1)
                    dve.tensor_tensor(summed[:, half], summed[:, half], bas[:, n], ALU.add).then_inc(tile_summed[n], 1)
                    dve.wait_ge(tile_summed[n], turn + 1)
                    dve.wait_ge(stored[half], (turn * 2 + n // 2) * 16)
                    layer_norm(dve, summed[:, half:half + 1], normed[:, half:half + 1], stats, agg, std, rstd,
                               ln_steps, std_ready, b, tick[:]).then_inc(normed_ready, 1)


def build(nc, x, skip, context, w_qkv, w_gates, w_out, k, wg_router, w_gate, w_up, w_down, ws_gate, ws_up,
          ws_down, out):
    B, N, D = x.shape
    E = w_gate.shape[0]
    capacity = CAP_FACTOR * (B * N * TOP_K // E)
    x1 = nc.dram_tensor("x1", [B, N, D], F32).ap()
    x2 = nc.dram_tensor("x2", [B, N, D], F32).ap()
    base = nc.dram_tensor("base", [B, N, D], F32).ap()
    padded_kernels = nc.dram_tensor("padded_kernels", [P, k.shape[0], P + k.shape[1]], F32).ap()
    queues = nc.dram_tensor("queues", [E * capacity, D + 2], F32).ap()
    results = nc.dram_tensor("results", [B * N * TOP_K, D], F32).ap()

    with ExitStack() as ctx:
        s = Scope(nc, ctx, "")
        identity, eps = s.sb("identity", [P, P]), s.sb("eps", [P, 1])
        plan = s.sb("plan", [1, 2, E], I32)
        filler, zero_row = s.sb("filler", [P, D + 2]), s.sb("zero_row", [P, D])
        ones_written, identity_ready, fillers_ready = (
            s.sem(n) for n in ("ones_written", "identity_ready", "fillers_ready"))

        with nc.Block() as block:
            @block.gpsimd
            def _(pool):
                pool.memset(identity[:], 1.0).then_inc(ones_written, 1)
                pool.wait_ge(ones_written, 1)
                pool.affine_select(out=identity[:], in_=identity[:], compare_op=ALU.is_equal, fill=0.0, base=0,
                                   pattern=[[-1, P]], channel_multiplier=1).then_inc(identity_ready, 1)

            @block.vector
            def _(dve):
                dve.memset(eps[:], LN_EPS)
                dve.memset(filler[:, 0:D + 1], 0.0)
                dve.memset(filler[:, D + 1:D + 2], float(FAR))
                dve.memset(zero_row[:], 0.0)

        attention_stage(nc, identity[:], eps[:], x, w_qkv, w_gates, w_out, x1, [(queues, filler), (results, zero_row)])
        convolution_stage(nc, identity[:], eps[:], x1, context, k, skip, padded_kernels, x2)
        routing_stage(nc, identity[:], x2, wg_router, ws_gate, ws_up, ws_down, queues, base, plan[:])
        expert_stage(nc, identity[:], queues, w_gate, w_up, w_down, plan[:], results)
        combination_stage(nc, eps[:], base, results, out)


_INS = ["x", "fside_S2_0", "ctx_2048", "L0_attn_w_qkv", "L0_attn_w_gates", "L0_attn_w_out", "L0_xattn_k",
        "L0_ffn_wg_router", "L0_ffn_w_gate", "L0_ffn_w_up", "L0_ffn_w_down", "L0_ffn_ws_gate", "L0_ffn_ws_up",
        "L0_ffn_ws_down"]
_OUTS = [((16, 128, 256), "float32")]


def kernel(**inputs):
    import numpy as _np
    import concourse.bacc as _bacc
    from concourse import mybir as _mybir
    from concourse.bass_utils import run_bass_kernel_spmd as _run

    nc = _bacc.Bacc("TRN2", target_bir_lowering=False, num_devices=1)
    arrays, args = {}, []
    for name in _INS:
        a = _np.ascontiguousarray(inputs[name])
        arrays[f"in_{name}_dram"] = a
        args.append(nc.dram_tensor(f"in_{name}_dram", a.shape, _mybir.dt.from_np(a.dtype), kind="ExternalInput").ap())
    for i, (shape, dtype) in enumerate(_OUTS):
        dt = _mybir.dt.from_np(_np.dtype(dtype))
        args.append(nc.dram_tensor(f"out_{i}_dram", shape, dt, kind="ExternalOutput").ap())
    build(nc, *args)
    r = _run(nc, [arrays], core_ids=[0])
    return r.results[0]["out_0_dram"]
```

```python
from contextlib import ExitStack

import concourse.bass as bass
from concourse import mybir

F32 = mybir.dt.float32
F32R = mybir.dt.float32r
U32 = mybir.dt.uint32
I32 = mybir.dt.int32
ALU = mybir.AluOpType
ACT = mybir.ActivationFunctionType
AX = mybir.AxisListType

P = 128
LN_EPS = 1e-5
GB = 4


class Scope:

    def __init__(self, nc, ctx, prefix):
        self.nc, self.ctx, self.prefix = nc, ctx, prefix

    def sb(self, name, shape, dt=F32):
        return self.ctx.enter_context(self.nc.sbuf_tensor(self.prefix + name, shape, dt))

    def ps(self, name, shape, dt=F32):
        return self.ctx.enter_context(self.nc.psum_tensor(self.prefix + name, shape, dt))

    def sem(self, name):
        return self.ctx.enter_context(self.nc.semaphore(self.prefix + name))


def split3(pe, out, lhs, rhs, first, last):
    pe.matmul(out, lhs[0], rhs[0], start=first, stop=False, skip_group_check=True)
    pe.matmul(out, lhs[0], rhs[1], start=False, stop=False, skip_group_check=True)
    return pe.matmul(out, lhs[1], rhs[0], start=False, stop=last, skip_group_check=True)


def layer_norm(dve, x, out, stats, agg, std, rstd, steps, std_ready, n_before, tick):
    count = x.shape[1]
    for n in range(count):
        last = dve.bn_stats(stats[:, n, :], x[:, n, :])
    last.then_inc(steps, 1)
    carried_wait(dve, steps, 3 * n_before + 1, tick)
    for n in range(count):
        last = dve.bn_aggr(agg[:, n, :], stats[:, n, :])
    last.then_inc(steps, 1)
    dve.wait_ge(std_ready, n_before + 1)
    dve.reciprocal(rstd[:], std[:]).then_inc(steps, 1)
    dve.wait_ge(steps, 3 * n_before + 3)
    for n in range(count):
        last = dve.tensor_scalar(out[:, n, :], x[:, n, :], agg[:, n, 0:1], rstd[:, n:n + 1],
                                 ALU.subtract, ALU.mult)
    return last


def layer_norm_std(act, agg, std, eps, steps, std_ready, n_before):
    act.wait_ge(steps, 3 * n_before + 2)
    act.activation(std[:], agg[:, :, 1], ACT.Sqrt, bias=eps).then_inc(std_ready, 1)


def carried_wait(dve, sem, value, tick):
    dve.wait_ge(sem, value)
    dve.memset(tick, 0.0)


def attention_stage(nc, ident, eps, x, w_qkv, w_gates, w_out, x1, fills, copies):
    B, N, D = x.shape
    H = w_gates.shape[1]
    DH = w_qkv.shape[1] // (3 * H)
    G = B // GB
    KB = D // P
    SOFTCAP, SCALE = 50.0, DH ** -0.5
    HG = 4
    VW = DH + 2
    T = GB * N
    NV = H
    EARLY = GB
    CH = 512
    NCH = w_qkv.shape[1] // CH
    WOH = 4
    LN_END = 2
    NRAW = 3
    assert (N, DH, T, HG * DH, H // HG, WOH * D, KB * CH) == (P, P, 512, 512, GB, 1024, 1024)

    x_in = x.rearrange("b p c -> p b c")
    x1_out = x1.rearrange("b p c -> p b c")
    w_in = w_qkv.rearrange("(k p) n -> p k n", p=P)
    wg_in = w_gates.rearrange("(k p) n -> p k n", p=P)
    wo_in = w_out.rearrange("(h p) c -> p h c", p=P)

    with ExitStack() as ctx:
        s = Scope(nc, ctx, "at_")
        w_hi, w_lo = s.sb("w_hi", [P, KB, 3 * H * DH], F32R), s.sb("w_lo", [P, KB, 3 * H * DH], F32R)
        wo_hi, wo_lo = s.sb("wo_hi", [P, H, D], F32R), s.sb("wo_lo", [P, H, D], F32R)
        wg_hi, wg_lo = s.sb("wg_hi", [P, KB, H], F32R), s.sb("wg_lo", [P, KB, H], F32R)
        raw, wg_raw = s.sb("raw", [P, NRAW, 1024]), s.sb("wg_raw", [P, KB, H])
        xT_hi, xT_lo = s.sb("xT_hi", [P, KB, T], F32R), s.sb("xT_lo", [P, KB, T], F32R)
        qT, kT = s.sb("qT", [P, T]), s.sb("kT", [P, T])
        v = s.sb("v", [P, 2, GB, HG, VW])
        capped = s.sb("capped", [P, T])
        probs = s.sb("probs", [P, 2, T])
        o_norm = s.sb("o_norm", [P, GB, DH])
        oT_hi, oT_lo = s.sb("oT_hi", [P, T], F32R), s.sb("oT_lo", [P, T], F32R)
        gate_exp, gate_den = s.sb("gate_exp", [P, GB, H]), s.sb("gate_den", [P, GB, H])
        o_den, o_scale = s.sb("o_den", [P, GB]), s.sb("o_scale", [P, GB])
        stats, agg = s.sb("stats", [P, GB, 6]), s.sb("agg", [P, GB, 2])
        tick = s.sb("tick", [P, 1])
        causal = s.sb("causal", [P, N])
        std, rstd = s.sb("std", [P, GB]), s.sb("rstd", [P, GB])
        x_for_T = s.sb("x_for_T", [P, GB, D])
        x_res, x_out = (raw[:, n, :].rearrange("p (b c) -> p b c", b=GB) for n in range(2))

        ps_qv, ps_k, ps_s, ps_oT = (s.ps(n, [P, T]) for n in ("ps_qv", "ps_k", "ps_s", "ps_oT"))
        ps_o, ps_acc = s.ps("ps_o", [P, GB, D]), s.ps("ps_acc", [P, GB, D])
        ps_xT = (ps_qv, ps_k)
        ps_gate = ps_s[:, 0:GB * H].rearrange("p (b h) -> p b h", b=GB)

        raw_loaded = [s.sem(f"raw_loaded{n}") for n in range(NRAW)]
        gates_loaded, hi_split, lo_split, ones_ready, causal_ready = (
            s.sem(n) for n in ("gates_loaded", "hi_split", "lo_split", "ones_ready", "causal_ready"))
        filled = s.sem("filled")
        x_for_T_loaded, x_res_loaded, x1_stored = (s.sem(n) for n in ("x_for_T_loaded", "x_res_loaded", "x1_stored"))
        xT_in_psum, xT_hi_ready, xT_lo_ready = (s.sem(n) for n in ("xT_in_psum", "xT_hi_ready", "xT_lo_ready"))
        q_in_psum, q_ready = s.sem("q_in_psum"), s.sem("q_ready")
        k_in_psum, k_ready = s.sem("k_in_psum"), s.sem("k_ready")
        v_in_psum, v_ready = s.sem("v_in_psum"), s.sem("v_ready")
        gate_in_psum, gate_exp_ready, gate_ready = (s.sem(n) for n in ("gate_in_psum", "gate_exp_ready", "gate_ready"))
        s_in_psum, capped_ready, exp_ready, probs_ready = (
            s.sem(n) for n in ("s_in_psum", "capped_ready", "exp_ready", "probs_ready"))
        o_in_psum, o_steps, o_ready = (s.sem(n) for n in ("o_in_psum", "o_steps", "o_ready"))
        oT_in_psum, oT_hi_ready, oT_lo_ready = (s.sem(n) for n in ("oT_in_psum", "oT_hi_ready", "oT_lo_ready"))
        acc_in_psum, sum_ready, ln_steps, std_ready, x1_ready = (
            s.sem(n) for n in ("acc_in_psum", "sum_ready", "ln_steps", "std_ready", "x1_ready"))

        def columns(kind, hg):
            c = kind * (H // HG) + hg
            cols = slice(c * CH, (c + 1) * CH)
            return w_in[:, :, cols], w_hi[:, :, cols], w_lo[:, :, cols], KB

        def out_rows(hg):
            heads = slice(hg * WOH, (hg + 1) * WOH)
            return wo_in[:, heads, :], wo_hi[:, heads, :], wo_lo[:, heads, :], WOH

        chunks = [columns(2, 0), columns(0, 0), columns(1, 0)]
        for hg in range(1, H // HG):
            chunks += [columns(2, hg), out_rows(hg - 1), columns(0, hg), columns(1, hg)]
        chunks.append(out_rows(H // HG - 1))
        AT_ONCE = 4

        def raw_chunk(n, k):
            return raw[:, n % NRAW, :].rearrange("p (k c) -> p k c", k=k)

        def for_groups(eng, group):
            group(0, True, False)
            with eng.Fori(1, G - 1) as g:
                group(g, False, False)
            group(G - 1, False, True)

        block = ctx.enter_context(nc.Block())

        @block.sync
        def _(sp):
            sp.dma_start(x_for_T[:], x_in[:, 0:GB, :]).then_inc(x_for_T_loaded, 16)
            sp.dma_start(wg_raw[:], wg_in).then_inc(gates_loaded, 16)
            for n, (src, _, _, k) in enumerate(chunks):
                if n >= NRAW:
                    sp.wait_ge(hi_split, n - NRAW + 2)
                    sp.wait_ge(lo_split, n - NRAW + 2)
                sp.dma_start(raw_chunk(n, k), src).then_inc(raw_loaded[n % NRAW], 16)
            sp.wait_ge(hi_split, len(chunks) + 1)
            sp.wait_ge(lo_split, len(chunks) + 1)

            for dst, src in copies:
                sp.dma_start(dst, src).then_inc(filled, 16)

            FR = 12

            def fill(g):
                for dst, row in fills:
                    width = dst.shape[1]
                    share = dst.shape[0] // G
                    for n in range(share // (P * FR)):
                        sp.dma_start(dst[bass.ds(g * share + n * P * FR, P * FR), :]
                                     .rearrange("(p r) w -> p r w", p=P),
                                     row[:].unsqueeze(1).broadcast_to([P, FR, width])).then_inc(filled, 16)

            def group(g, first, last):
                if not first:
                    sp.wait_ge(sum_ready, g)
                sp.dma_start(x_res, x_in[:, bass.ds(g * GB, GB), :]).then_inc(x_res_loaded, 16)
                if not last:
                    sp.wait_ge(xT_in_psum, g + 1)
                    sp.dma_start(x_for_T[:], x_in[:, bass.ds(g * GB + GB, GB), :]).then_inc(x_for_T_loaded, 16)
                fill(g)
                if not first:
                    store(g - 1)

            def store(g):
                sp.wait_ge(x1_ready, g + 1)
                sp.dma_start(x1_out[:, bass.ds(g * GB, GB), :], x_out).then_inc(x1_stored, 16)

            for_groups(sp, group)
            store(G - 1)
            sp.wait_ge(x1_stored, 16 * G)
            sp.wait_ge(filled, 16 * (len(copies) + sum(dst.shape[0] // (P * FR) for dst, _ in fills)))

        @block.tensor
        def _(pe):
            pe.wait_ge(ones_ready, 1)

            def wait_for_chunks(count):
                pe.wait_ge(hi_split, count + 1)
                pe.wait_ge(lo_split, count + 1)

            def project(out, w_cols):
                for k in range(KB):
                    last = split3(pe, out, (w_hi[:, k, w_cols], w_lo[:, k, w_cols]),
                                  (xT_hi[:, k, :], xT_lo[:, k, :]), k == 0, k == KB - 1)
                return last

            def v_piece(out, hg, b):
                cols = slice((2 * H + hg * HG) * DH, (2 * H + (hg + 1) * HG) * DH)
                tok = slice(b * N, (b + 1) * N)
                for k in range(KB):
                    last = split3(pe, out, (xT_hi[:, k, tok], xT_lo[:, k, tok]),
                                  (w_hi[:, k, cols], w_lo[:, k, cols]), k == 0, k == KB - 1)
                return last

            def transposes(g):
                pe.wait_ge(x_for_T_loaded, g * 16 + 16)
                for k in range(KB):
                    for b in range(GB):
                        last = pe.transpose(ps_xT[k][:, b * N:(b + 1) * N], x_for_T[:, b, k * P:(k + 1) * P], ident)
                last.then_inc(xT_in_psum, 1)

            def first_v(g, n):
                if n == 0:
                    pe.wait_ge(xT_hi_ready, g + 1)
                    pe.wait_ge(xT_lo_ready, g + 1)
                if n >= 2:
                    pe.wait_ge(v_ready, g * NV + n - 1)
                v_piece((ps_qv, ps_k)[n % 2][:], 0, n).then_inc(v_in_psum, 1)

            def gates(g):
                for b in range(GB):
                    tok = slice(b * N, (b + 1) * N)
                    for k in range(KB):
                        last = split3(pe, ps_gate[:, b, :], (xT_hi[:, k, tok], xT_lo[:, k, tok]),
                                      (wg_hi[:, k, :], wg_lo[:, k, :]), k == 0, k == KB - 1)
                last.then_inc(gate_in_psum, 1)

            def group(g, first_group, last_group):
                made = EARLY
                for h in range(H + 2):
                    if first_group and h == 1:
                        wait_for_chunks(AT_ONCE)
                    if first_group and h >= 2 and AT_ONCE + h - 2 < len(chunks):
                        wait_for_chunks(AT_ONCE + h - 1)
                    if h == H and not last_group:
                        pe.wait_ge(k_ready, g * H + H)
                        transposes(g + 1)
                    if h == H + 1 and not last_group:
                        first_v(g + 1, 0)
                    if h < H:
                        pe.wait_ge(v_ready, g * NV + made)
                        project(ps_qv[:], slice(h * DH, (h + 1) * DH)).then_inc(q_in_psum, 1)
                    if h >= 2:
                        pe.wait_ge(o_ready, g * H + h - 1)
                        pe.wait_ge(oT_hi_ready, g * H + h - 2)
                        pe.wait_ge(oT_lo_ready, g * H + h - 2)
                        for b in range(GB):
                            last = pe.transpose(ps_oT[:, b * N:(b + 1) * N], o_norm[:, b, :], ident)
                        last.then_inc(oT_in_psum, 1)
                    if h < H:
                        pe.wait_ge(k_ready, g * H + h)
                        project(ps_k[:], slice((H + h) * DH, (H + h + 1) * DH)).then_inc(k_in_psum, 1)
                    if h < H:
                        pe.wait_ge(q_ready, g * H + h + 1)
                    if 1 <= h <= NV - EARLY:
                        v_piece(ps_qv[:], (h - 1) // GB + 1, (h - 1) % GB).then_inc(v_in_psum, 1)
                        made += 1
                    if h < H:
                        pe.wait_ge(k_ready, g * H + h + 1)
                        pe.wait_ge(capped_ready, g * H + h)
                        if h == 0:
                            pe.wait_ge(gate_exp_ready, g + 1)
                        for b in range(GB):
                            tok = slice(b * N, (b + 1) * N)
                            last = pe.matmul(ps_s[:, tok], kT[:, tok], qT[:, tok], start=True, stop=True,
                                             skip_group_check=True)
                        last.then_inc(s_in_psum, 1)
                    if 1 <= h <= H:
                        pe.wait_ge(probs_ready, g * H + h)
                        pe.wait_ge(v_ready, g * NV + ((h - 1) // HG + 1) * GB)
                        pe.wait_ge(o_ready, g * H + h - 1)
                        for b in range(GB):
                            last = pe.matmul(ps_o[:, b, 0:VW], probs[:, (h - 1) % 2, b * N:(b + 1) * N],
                                             v[:, (h - 1) // HG % 2, b, (h - 1) % HG, :], start=True, stop=True,
                                             skip_group_check=True)
                        last.then_inc(o_in_psum, 1)
                    if h == H + 1 and not last_group:
                        first_v(g + 1, 1)
                    if h >= 2:
                        pe.wait_ge(oT_hi_ready, g * H + h - 1)
                        pe.wait_ge(oT_lo_ready, g * H + h - 1)
                        if h == 2:
                            pe.wait_ge(sum_ready, g)
                        for b in range(GB):
                            tok = slice(b * N, (b + 1) * N)
                            last = split3(pe, ps_acc[:, b, :], (oT_hi[:, tok], oT_lo[:, tok]),
                                          (wo_hi[:, h - 2, :], wo_lo[:, h - 2, :]), h == 2 and b % 2 == 0,
                                          h == H + 1)
                last.then_inc(acc_in_psum, 1)
                if not last_group:
                    first_v(g + 1, 2)
                    gates(g + 1)
                    first_v(g + 1, 3)

            transposes(0)
            wait_for_chunks(1)
            for n in range(EARLY - 1):
                first_v(0, n)
            gates(0)
            first_v(0, EARLY - 1)
            wait_for_chunks(AT_ONCE - 1)
            for_groups(pe, group)

        @block.scalar
        def _(act):
            def split_chunk(n):
                _, hi, _, k = chunks[n]
                act.wait_ge(raw_loaded[n % NRAW], 16 * (n // NRAW + 1))
                act.activation(hi, raw_chunk(n, k), ACT.Copy).then_inc(hi_split, 1)

            def standard_deviations(g):
                act.wait_ge(ln_steps, 3 * g + 2)
                act.activation(std[:], agg[:, :, 1], ACT.Sqrt, bias=eps).then_inc(std_ready, 1)

            def split_xT(g):
                act.wait_ge(xT_in_psum, g + 1)
                for k in range(KB):
                    last = act.activation(xT_hi[:, k, :], ps_xT[k][:], ACT.Copy)
                last.then_inc(xT_hi_ready, 1)

            def gates(g):
                act.wait_ge(gate_in_psum, g + 1)
                if not (isinstance(g, int) and g == 0):
                    act.wait_ge(gate_ready, g)
                act.activation(gate_exp[:], ps_gate, ACT.Exp, scale=-1.0).then_inc(gate_exp_ready, 1)

            def group(g, first_group, last_group):
                for h in range(H + 2):
                    if h == H and not last_group:
                        split_xT(g + 1)
                    if h < H:
                        act.wait_ge(q_in_psum, g * H + h + 1)
                        act.activation(qT[:], ps_qv[:], ACT.Copy).then_inc(q_ready, 1)
                    if h >= 2:
                        act.wait_ge(oT_in_psum, g * H + h - 1)
                        act.activation(oT_hi[:], ps_oT[:], ACT.Copy).then_inc(oT_hi_ready, 1)
                    if h < H:
                        act.wait_ge(s_in_psum, g * H + h + 1)
                        act.wait_ge(exp_ready, g * H + h)
                        act.activation(capped[:], ps_s[:], ACT.Tanh, scale=SCALE / SOFTCAP).then_inc(capped_ready, 1)
                        act.wait_ge(capped_ready, g * H + h + 1)
                        if h >= 2:
                            act.wait_ge(o_in_psum, g * H + h - 1)
                        else:
                            act.wait_ge(o_in_psum, g * H)
                        act.activation(probs[:, h % 2, :], capped[:], ACT.Exp, scale=SOFTCAP).then_inc(exp_ready, 1)
                    if first_group and AT_ONCE + h < len(chunks):
                        split_chunk(AT_ONCE + h)
                    if h == LN_END and not first_group:
                        standard_deviations(g - 1)
                if last_group:
                    standard_deviations(g)
                else:
                    gates(g + 1)

            split_xT(0)
            act.wait_ge(gates_loaded, 16)
            act.activation(wg_hi[:], wg_raw[:], ACT.Copy).then_inc(hi_split, 1)
            for n in range(AT_ONCE):
                split_chunk(n)
            gates(0)
            for_groups(act, group)

        @block.gpsimd
        def _(pool):
            pool.wait_ge(ones_ready, 2)
            pool.affine_select(out=causal[:], in_=causal[:], compare_op=ALU.is_ge, fill=0.0, base=0,
                               pattern=[[1, N]], channel_multiplier=-1).then_inc(causal_ready, 1)
            pool.wait_ge(causal_ready, 1)
            with pool.Fori(0, G) as g:
                for h in range(H):
                    pool.wait_ge(exp_ready, g * H + h + 1)
                    half = probs[:, h % 2, :].rearrange("p (b i) -> p b i", b=GB)
                    pool.tensor_tensor(half, half, causal[:].unsqueeze(1).broadcast_to([P, GB, N]), ALU.mult)\
                        .then_inc(probs_ready, 1)

        @block.vector
        def _(dve):
            dve.memset(v[:, :, :, :, DH:VW], 1.0).then_inc(ones_ready, 1)
            dve.memset(causal[:], 1.0).then_inc(ones_ready, 1)
            def split_chunk(n):
                _, hi, lo, k = chunks[n]
                dve.wait_ge(hi_split, n + 2)
                dve.tensor_tensor(lo, raw_chunk(n, k), hi.bitcast(F32), ALU.subtract).then_inc(lo_split, 1)

            def layer_norm_end(g):
                dve.wait_ge(std_ready, g + 1)
                dve.reciprocal(rstd[:], std[:]).then_inc(ln_steps, 1)
                dve.wait_ge(ln_steps, 3 * g + 3)
                for b in range(GB):
                    last = dve.tensor_scalar(x_out[:, b, :], x_out[:, b, :], agg[:, b, 0:1], rstd[:, b:b + 1],
                                             ALU.subtract, ALU.mult)
                last.then_inc(x1_ready, 1)

            def v_copy(bank, hg, b):
                dve.tensor_copy(v[:, hg % 2, b, :, 0:DH],
                                bank[:].rearrange("p (h d) -> p h d", h=HG)).then_inc(v_ready, 1)

            def split_xT(g):
                dve.wait_ge(xT_hi_ready, g + 1)
                for k in range(KB):
                    last = dve.tensor_tensor(xT_lo[:, k, :], ps_xT[k][:], xT_hi[:, k, :].bitcast(F32), ALU.subtract)
                last.then_inc(xT_lo_ready, 1)

            def first_v(g, n):
                dve.wait_ge(v_in_psum, g * NV + n + 1)
                v_copy((ps_qv, ps_k)[n % 2], 0, n)

            def gates(g):
                dve.wait_ge(gate_exp_ready, g + 1)
                dve.tensor_scalar(gate_den[:], gate_exp[:], 1.0, None, ALU.add).then_inc(gate_ready, 1)

            def group(g, first_group, last_group):
                made = EARLY
                for h in range(H + 2):
                    if h == H and not last_group:
                        split_xT(g + 1)
                    if h >= 2:
                        dve.wait_ge(oT_hi_ready, g * H + h - 1)
                        dve.tensor_tensor(oT_lo[:], ps_oT[:], oT_hi[:].bitcast(F32), ALU.subtract)\
                           .then_inc(oT_lo_ready, 1)
                    if h < H:
                        dve.wait_ge(k_in_psum, g * H + h + 1)
                        dve.tensor_copy(kT[:], ps_k[:]).then_inc(k_ready, 1)
                    if 1 <= h <= NV - EARLY:
                        made += 1
                        dve.wait_ge(v_in_psum, g * NV + made)
                        v_copy(ps_qv, (h - 1) // GB + 1, (h - 1) % GB)
                    if 1 <= h <= H:
                        dve.wait_ge(o_in_psum, g * H + h)
                        if h == 1:
                            dve.wait_ge(gate_ready, g + 1)
                        dve.tensor_tensor(o_den[:], ps_o[:, :, DH], gate_den[:, :, h - 1], ALU.mult)\
                           .then_inc(o_steps, 1)
                        dve.wait_ge(o_steps, g * 2 * H + 2 * h - 1)
                        dve.reciprocal(o_scale[:], o_den[:]).then_inc(o_steps, 1)
                        dve.wait_ge(o_steps, g * 2 * H + 2 * h)
                        if h >= 2:
                            dve.wait_ge(oT_in_psum, g * H + h - 1)
                        dve.tensor_tensor(o_norm[:], ps_o[:, :, 0:DH],
                                          o_scale[:].unsqueeze(2).broadcast_to([P, GB, DH]), ALU.mult)\
                           .then_inc(o_ready, 1)
                    if first_group and AT_ONCE + h < len(chunks):
                        split_chunk(AT_ONCE + h)
                    if h == LN_END + 1 and not first_group:
                        layer_norm_end(g - 1)
                    if h == H and not last_group:
                        first_v(g + 1, 0)
                dve.wait_ge(acc_in_psum, g + 1)
                dve.wait_ge(x_res_loaded, g * 16 + 16)
                if first_group:
                    dve.wait_ge(lo_split, len(chunks) + 1)
                else:
                    dve.wait_ge(x1_stored, g * 16)
                dve.tensor_tensor(x_out, ps_acc[:], x_res, ALU.add).then_inc(sum_ready, 1)
                if not last_group:
                    first_v(g + 1, 1)
                dve.wait_ge(sum_ready, g + 1)
                for b in range(GB):
                    last = dve.bn_stats(stats[:, b, :], x_out[:, b, :])
                last.then_inc(ln_steps, 1)
                if not last_group:
                    first_v(g + 1, 2)
                carried_wait(dve, ln_steps, 3 * g + 1, tick[:])
                for b in range(GB):
                    last = dve.bn_aggr(agg[:, b, :], stats[:, b, :])
                last.then_inc(ln_steps, 1)
                if last_group:
                    layer_norm_end(g)
                else:
                    first_v(g + 1, 3)
                    gates(g + 1)

            split_xT(0)
            dve.wait_ge(hi_split, 1)
            dve.tensor_tensor(wg_lo[:], wg_raw[:], wg_hi[:].bitcast(F32), ALU.subtract).then_inc(lo_split, 1)
            split_chunk(0)
            for n in range(EARLY):
                first_v(0, n)
                if n < AT_ONCE - 1:
                    split_chunk(n + 1)
            gates(0)
            for_groups(dve, group)


def convolution_stage(nc, ident, eps, x1, ctx_in, skip_in, padded_kernels, x2):
    B, C, L = x1.shape
    H = padded_kernels.shape[1]
    NI = C // H
    G = B // GB
    LB = L // P
    NT = LB * GB
    TH = 4
    NY = 4
    RESULT, SKIP, ADD_X, ADD_SKIP, ADD_BOTH, STATS, MEANS, RSTD, TRANSPOSES = 3, 4, 2, 4, 9, 7, 8, 10, 9
    assert (C, LB, GB * NI * NI) == (P, 2, 256)

    x1_src = x1.rearrange("b p c -> p b c")
    ctx_src = ctx_in.rearrange("b p c -> p b c")
    row = H * (P + L)
    toeplitz_src = bass.AP(padded_kernels.tensor, P, [[row - 1, P], [P + L, H], [1, L]])

    with ExitStack() as ctx:
        s = Scope(nc, ctx, "cv_")
        toeplitz = s.sb("toeplitz", [P, H, L])
        same_head, skip = s.sb("same_head", [P, P]), s.sb("skip", [P, 1])
        skip_sum = s.sb("skip_sum", [P, P])
        x_for_T, c_for_T = s.sb("x_for_T", [P, GB, L]), s.sb("c_for_T", [P, GB, L])
        x_res, c_res = s.sb("x_res", [P, GB * L]), s.sb("c_res", [P, GB * L])
        product, skipped = s.sb("product", [P, GB * L]), s.sb("skipped", [P, GB * L])
        total = s.sb("total", [P, GB, L])
        vT, cT = s.sb("vT", [P, 2, NT, C]), s.sb("cT", [P, 2, NT, C])
        pairs = s.sb("pairs", [P, NY, NT, NI, NI])
        weighted = s.sb("weighted", [P, 2, NT, NI, NI])
        outT = s.sb("outT", [P, LB, GB, C])
        stats, agg = s.sb("stats", [P, GB, 6]), s.sb("agg", [P, GB, 2])
        std, rstd, shift = s.sb("std", [P, GB]), s.sb("rstd", [P, GB]), s.sb("shift", [P, GB])
        tick = s.sb("tick", [P, 1])
        ps_v, ps_c = s.ps("ps_v", [P, GB * L]), s.ps("ps_c", [P, GB * L])
        ps_y = [s.ps(f"ps_y{n}", [P, NT, NI, NI]) for n in range(NY)]

        toeplitz_loaded, skip_loaded = [s.sem(f"toeplitz_loaded{n}") for n in range(H // TH)], s.sem("skip_loaded")
        band_steps, same_head_ready, skip_sum_ready = (s.sem(n) for n in ("band_steps", "same_head_ready",
                                                                          "skip_sum_ready"))
        xT_loaded, cT_loaded, x_res_loaded, c_res_loaded = (
            s.sem(n) for n in ("xT_loaded", "cT_loaded", "x_res_loaded", "c_res_loaded"))
        v_in_psum, c_in_psum, vT_ready, cT_ready = (s.sem(n) for n in ("v_in_psum", "c_in_psum", "vT_ready", "cT_ready"))
        pairs_ready, y_in_psum, weighted_ready, head_out = (
            s.sem(n) for n in ("pairs_ready", "y_in_psum", "weighted_ready", "head_out"))
        product_ready, result_in_psum, skip_in_psum = (s.sem(n) for n in ("product_ready", "result_in_psum", "skip_in_psum"))
        x_added, skip_ready, sum_ready = s.sem("x_added"), s.sem("skip_ready"), s.sem("sum_ready")
        stats_ready, means_ready, std_ready, rstd_ready, shift_ready, x2_ready = (s.sem(n) for n in (
            "stats_ready", "means_ready", "std_ready", "rstd_ready", "shift_ready", "x2_ready"))

        def for_groups(eng, group, end):
            group(0, True, False)
            with eng.Fori(1, G - 1) as g:
                group(g, False, False)
            group(G - 1, False, True)
            end(G - 1)

        block = ctx.enter_context(nc.Block())

        @block.sync
        def _(sp):
            def load_for_T(g):
                sp.dma_start(x_for_T[:], x1_src[:, bass.ds(g * GB, GB), :]).then_inc(xT_loaded, 16)
                sp.dma_start(c_for_T[:], ctx_src[:, bass.ds(g * GB, GB), :]).then_inc(cT_loaded, 16)

            def load_res(g):
                sp.dma_start(x_res[:].rearrange("p (b l) -> p b l", b=GB), x1_src[:, bass.ds(g * GB, GB), :])\
                  .then_inc(x_res_loaded, 16)
                sp.dma_start(c_res[:].rearrange("p (b l) -> p b l", b=GB), ctx_src[:, bass.ds(g * GB, GB), :])\
                  .then_inc(c_res_loaded, 16)

            def group(g, first, last):
                if not last:
                    sp.wait_ge(c_in_psum, g + 1)
                    load_for_T(g + 1)
                if not first:
                    sp.wait_ge(x_added, g)
                    sp.wait_ge(skip_ready, g)
                    load_res(g)

            load_for_T(0)
            sp.dma_start(skip[:], skip_in.rearrange("(p a) -> p a", a=1)).then_inc(skip_loaded, 16)
            for n in range(H // TH):
                heads = slice(n * TH, (n + 1) * TH)
                sp.dma_start(toeplitz[:, heads], toeplitz_src[:, heads]).then_inc(toeplitz_loaded[n], 16)
            load_res(0)
            for_groups(sp, group, lambda g: None)

        @block.tensor
        def _(pe):
            def transposes(g):
                for src, loaded, bank, done in ((x_for_T, xT_loaded, ps_v, v_in_psum),
                                                (c_for_T, cT_loaded, ps_c, c_in_psum)):
                    pe.wait_ge(loaded, g * 16 + 16)
                    for lb in range(LB):
                        for b in range(GB):
                            last = pe.transpose(bank[:, (lb * GB + b) * C:(lb * GB + b + 1) * C],
                                                src[:, b, lb * P:(lb + 1) * P], ident)
                    last.then_inc(done, 1)

            def result_end(g):
                pe.wait_ge(vT_ready, g + 1)
                pe.wait_ge(head_out, g * H + H)
                for b in range(GB):
                    for lb in range(LB):
                        last = pe.transpose(ps_v[:, b * L + lb * P:b * L + (lb + 1) * P], outT[:, lb, b, :], ident)
                last.then_inc(result_in_psum, 1)

            def skip_end(g):
                pe.wait_ge(product_ready, g + 1)
                pe.wait_ge(cT_ready, g + 1)
                for n in range(2):
                    half = slice(n * 512, (n + 1) * 512)
                    last = pe.matmul(ps_c[:, half], skip_sum[:], product[:, half], start=True, stop=True)
                last.then_inc(skip_in_psum, 1)

            def group(g, first, last_group):
                for h in range(H):
                    if first and h % TH == 0:
                        pe.wait_ge(toeplitz_loaded[h // TH], 16)
                    pe.wait_ge(pairs_ready, g * H + h + 1)
                    if not (first and h < NY):
                        pe.wait_ge(weighted_ready, g * H + h - NY + 1)
                    y = ps_y[h % NY]
                    half = NT // 2
                    pe.matmul(y[:], toeplitz[:, h, 0:P], pairs[:, h % NY], start=True, stop=False, skip_group_check=True)
                    pe.matmul(y[:, half:2 * half], toeplitz[:, h, P:L], pairs[:, h % NY, 0:half], start=False,
                              stop=True, skip_group_check=True).then_inc(y_in_psum, 1)
                    if h == RESULT and not first:
                        result_end(g - 1)
                    if h == SKIP and not first:
                        skip_end(g - 1)
                    if h == TRANSPOSES and not last_group:
                        if not first:
                            pe.wait_ge(x_added, g)
                            pe.wait_ge(skip_ready, g)
                        transposes(g + 1)

            def end(g):
                result_end(g)
                skip_end(g)

            transposes(0)
            pe.wait_ge(skip_sum_ready, 1)
            for_groups(pe, group, end)

        @block.scalar
        def _(act):
            def copies(g):
                act.wait_ge(v_in_psum, g + 1)
                act.activation(vT[:, bass.ds(g % 2, 1)].rearrange("p a n c -> p (a n c)"), ps_v[:], ACT.Copy)\
                   .then_inc(vT_ready, 1)
                act.wait_ge(c_in_psum, g + 1)
                act.activation(cT[:, bass.ds(g % 2, 1)].rearrange("p a n c -> p (a n c)"), ps_c[:], ACT.Copy)\
                   .then_inc(cT_ready, 1)

            def end(g):
                act.wait_ge(means_ready, g + 1)
                act.activation(std[:], agg[:, :, 1], ACT.Sqrt, bias=eps).then_inc(std_ready, 1)
                act.wait_ge(shift_ready, g + 1)
                for b in range(GB):
                    last = act.activation(x2[:, bass.ds(g * GB + b, 1), :].rearrange("p b l -> p (b l)"), total[:, b, :],
                                          ACT.Identity, bias=shift[:, b:b + 1],
                                          scale=rstd[:, b:b + 1])
                last.then_inc(x2_ready, 1)

            def group(g, first, last):
                if not last:
                    copies(g + 1)
                if not first:
                    end(g - 1)

            copies(0)
            for_groups(act, group, end)

        @block.gpsimd
        def _(pool):
            pool.memset(same_head[:], 1.0).then_inc(band_steps, 1)
            pool.wait_ge(band_steps, 1)
            grid = same_head[:].rearrange("p (h j) -> p h j", h=H)
            pool.affine_select(out=grid, in_=grid, compare_op=ALU.is_ge, fill=0.0, base=0,
                               pattern=[[-NI, H], [0, NI]], channel_multiplier=1).then_inc(band_steps, 1)
            pool.wait_ge(band_steps, 2)
            pool.affine_select(out=grid, in_=grid, compare_op=ALU.is_ge, fill=0.0, base=NI - 1,
                               pattern=[[NI, H], [0, NI]], channel_multiplier=-1).then_inc(same_head_ready, 1)

            def make_product(g):
                pool.wait_ge(x_res_loaded, g * 16 + 16)
                pool.wait_ge(c_res_loaded, g * 16 + 16)
                if not (isinstance(g, int) and g == 0):
                    pool.wait_ge(skip_in_psum, g)
                pool.tensor_tensor(product[:], x_res[:], c_res[:], ALU.mult).then_inc(product_ready, 1)

            def group(g, first, last):
                pool.wait_ge(vT_ready, g + 1)
                pool.wait_ge(cT_ready, g + 1)
                full = [P, NT, NI, NI]
                for h in range(H):
                    if not (first and h < NY):
                        pool.wait_ge(y_in_psum, g * H + h - NY + 1)
                    ch = slice(h * NI, (h + 1) * NI)
                    v_h = vT[:, bass.ds(g % 2, 1), :, ch].rearrange("p a n i -> p (a n) i").unsqueeze(3)
                    c_h = cT[:, bass.ds(g % 2, 1), :, ch].rearrange("p a n i -> p (a n) i").unsqueeze(2)
                    pool.tensor_tensor(pairs[:, h % NY], v_h.broadcast_to(full), c_h.broadcast_to(full), ALU.mult)\
                        .then_inc(pairs_ready, 1)
                    if h == ADD_BOTH and not first:
                        end(g - 1)
                    if h == H - 3:
                        make_product(g)

            def end(g):
                pool.wait_ge(x_added, g + 1)
                pool.wait_ge(skip_ready, g + 1)
                flat = total[:].rearrange("p b l -> p (b l)")
                pool.tensor_tensor(flat, flat, skipped[:], ALU.add).then_inc(sum_ready, 1)

            for_groups(pool, group, end)

        @block.vector
        def _(dve):
            def add_x(g):
                dve.wait_ge(result_in_psum, g + 1)
                dve.wait_ge(x_res_loaded, g * 16 + 16)
                if not (isinstance(g, int) and g == 0):
                    dve.wait_ge(x2_ready, g)
                dve.tensor_tensor(total[:].rearrange("p b l -> p (b l)"), ps_v[:], x_res[:], ALU.add)\
                   .then_inc(x_added, 1)

            def multiply_skip(g):
                if not (isinstance(g, int) and g == 0):
                    dve.wait_ge(sum_ready, g)
                dve.wait_ge(skip_in_psum, g + 1)
                dve.wait_ge(c_res_loaded, g * 16 + 16)
                dve.tensor_tensor(skipped[:], ps_c[:], c_res[:], ALU.mult).then_inc(skip_ready, 1)

            def statistics(g):
                dve.wait_ge(sum_ready, g + 1)
                for b in range(GB):
                    last = dve.bn_stats(stats[:, b, :], total[:, b, :])
                last.then_inc(stats_ready, 1)

            def means(g):
                if not (isinstance(g, int) and g == 0):
                    dve.wait_ge(x2_ready, g)
                carried_wait(dve, stats_ready, g + 1, tick[:])
                for b in range(GB):
                    last = dve.bn_aggr(agg[:, b, :], stats[:, b, :])
                last.then_inc(means_ready, 1)

            def scale_and_shift(g):
                dve.wait_ge(std_ready, g + 1)
                dve.reciprocal(rstd[:], std[:]).then_inc(rstd_ready, 1)
                dve.wait_ge(rstd_ready, g + 1)
                dve.scalar_tensor_tensor(out=shift[:], in0=agg[:, :, 0], scalar=-1.0, in1=rstd[:], op0=ALU.mult,
                                         op1=ALU.mult).then_inc(shift_ready, 1)

            parts = {ADD_X: add_x, ADD_SKIP: multiply_skip, STATS: statistics, MEANS: means, RSTD: scale_and_shift}

            def end(g):
                for part in parts.values():
                    part(g)

            def group(g, first, last):
                full = [P, NT, NI, NI]
                dve.wait_ge(cT_ready, g + 1)
                for h in range(H + 1):
                    if h < H:
                        ch = slice(h * NI, (h + 1) * NI)
                        c_i = cT[:, bass.ds(g % 2, 1), :, ch].rearrange("p a n i -> p (a n) i").unsqueeze(3)
                        if not (first and h < 2):
                            dve.wait_ge(head_out, g * H + h - 1)
                        dve.wait_ge(y_in_psum, g * H + h + 1)
                        dve.tensor_tensor(weighted[:, h % 2], ps_y[h % NY][:], c_i.broadcast_to(full), ALU.mult)\
                           .then_inc(weighted_ready, 1)
                    if h >= 1:
                        ch = slice((h - 1) * NI, h * NI)
                        if h == 1 and not first:
                            dve.wait_ge(result_in_psum, g)
                        dve.wait_ge(weighted_ready, g * H + h)
                        dve.tensor_reduce(outT[:].rearrange("p a b c -> p (a b) c")[:, :, ch],
                                          weighted[:, (h - 1) % 2].rearrange("p n i j -> p n j i"),
                                          AX.X, ALU.add).then_inc(head_out, 1)
                    if h in parts and not first:
                        parts[h](g - 1)

            dve.wait_ge(skip_loaded, 16)
            dve.wait_ge(same_head_ready, 1)
            dve.tensor_scalar(skip_sum[:], same_head[:], skip[:], None, ALU.mult).then_inc(skip_sum_ready, 1)
            for_groups(dve, group, end)


TOP_K = 6
CAP_FACTOR = 2
BLOCK = 256
FAR = 1 << 20


def routing_stage(nc, ident, x2_nat, wg_router, ws_gate, ws_up, ws_down, queues, base, plan):
    _, B, D = x2_nat.shape
    N = P
    E = wg_router.shape[0]
    F = ws_gate.shape[1]
    KB = D // P
    CAP = (queues.shape[0] - BLOCK) // E
    W = D + 2
    T = GB * N
    NCHUNK = B // GB
    NROWS = 4
    FB = [(f, min(P, F - f)) for f in range(0, F, P)]
    assert CAP == CAP_FACTOR * (B * N * TOP_K // E) and CAP == 3 * BLOCK and B * E == 512

    with ExitStack() as ctx:
        s = Scope(nc, ctx, "rt_")
        x2T = s.sb("x2T", [P, KB, B * N])
        router, routerT = s.sb("router", [E, D]), s.sb("routerT", [P, KB, E])
        gate_w, up_w, down_w = s.sb("gate_w", [P, KB, F]), s.sb("up_w", [P, KB, F]), s.sb("down_w", [P, len(FB), D])
        silu, hidden = s.sb("silu", [P, 2, T]), s.sb("hidden", [P, 2, T])
        sharedT = s.sb("sharedT", [P, KB, T])
        logits, top, top_i = s.sb("logits", [P, B, E]), s.sb("top", [P, B, 8]), s.sb("top_i", [P, B, 8], U32)
        shifted, top_shifted = s.sb("shifted", [P, B, E]), s.sb("top_shifted", [P, B, 8])
        expd, top_expd = s.sb("expd", [P, B, E]), s.sb("top_expd", [P, B, 8])
        norm, top_p = s.sb("norm", [P, B]), s.sb("top_p", [P, B, TOP_K])
        top_sum = s.sb("top_sum", [P, B])
        chosen, expert_no = s.sb("chosen", [P, B, TOP_K]), s.sb("expert_no", [P, E])
        top_no = s.sb("top_no", [P, B, TOP_K])
        one_hot, picked = s.sb("one_hot", [P, B, TOP_K, E]), s.sb("picked", [P, GB, TOP_K, E])
        member = s.sb("member", [P, B, E])
        earlier, ones = s.sb("earlier", [P, P]), s.sb("ones", [P, P])
        before = s.sb("before", [P, B + 1, E])
        place, over, queue_start = s.sb("place", [P, B, E]), s.sb("over", [P, B, E]), s.sb("queue_start", [P, E])
        place_k, place_i = s.sb("place_k", [P, B, TOP_K]), s.sb("place_i", [P, B, TOP_K], U32)
        tags = s.sb("tags", [P, B, TOP_K, 2])
        rows = [s.sb(f"rows{n}", [P, TOP_K, W]) for n in range(NROWS)]
        rows_i = [s.sb(f"rows_i{n}", [P, TOP_K], U32) for n in range(NROWS)]
        pairs = s.sb("pairs", [1, E])
        packed = s.sb("packed", [1, E // 4])
        pairs_sum, one_row = s.sb("pairs_sum", [1, E]), s.sb("one_row", [1, E])

        ps_g = [s.ps(f"ps_g{n}", [P, T]) for n in range(2)]
        ps_u = [s.ps(f"ps_u{n}", [P, T]) for n in range(2)]
        ps_yT, ps_y = s.ps("ps_yT", [P, KB, T]), s.ps("ps_y", [P, 2, D])
        ps_places = s.ps("ps_places", [P, 2, GB, E])
        ps_x2T = [(ps_g[0], ps_g[1]), (ps_u[0], ps_u[1])]
        ps_logits = [ps_yT[:, k, 0:GB * E] for k in range(2)]
        ps_router = ps_places[:].rearrange("p a b e -> p (a b e)")[:, 0:KB * E]

        router_loaded, weights_loaded = s.sem("router_loaded"), s.sem("weights_loaded")
        constants, iotas = s.sem("constants"), s.sem("iotas")
        x2T_in_psum, x2T_ready = s.sem("x2T_in_psum"), s.sem("x2T_ready")
        routerT_in_psum, routerT_ready = s.sem("routerT_in_psum"), s.sem("routerT_ready")
        logits_copied, places_read = s.sem("logits_copied"), s.sem("places_read")
        logits_in_psum, shifted_ready, exp_ready = s.sem("logits_in_psum"), s.sem("shifted_ready"), s.sem("exp_ready")
        steps, member_ready, places_in_psum = s.sem("steps"), s.sem("member_ready"), s.sem("places_in_psum")
        rows_ready = [s.sem(f"rows_ready{n}") for n in range(NROWS)]
        rows_scattered = [s.sem(f"rows_scattered{n}") for n in range(NROWS)]
        gu_in_psum, silu_ready, hidden_ready, yT_in_psum, yT_ready, y_in_psum, summed_ready = (s.sem(n) for n in (
            "gu_in_psum", "silu_ready", "hidden_ready", "yT_in_psum", "yT_ready", "y_in_psum", "summed_ready"))

        find_at = {0: 1}
        for c in range(2, NCHUNK):
            find_at[GB * (c - 1) - 2] = c

        block = ctx.enter_context(nc.Block())

        @block.sync
        def _(sp):
            sp.dma_start(router[:], wg_router).then_inc(router_loaded, 16)
            sp.dma_start(gate_w[:], ws_gate.rearrange("(k p) f -> p k f", p=P)).then_inc(weights_loaded, 16)
            sp.dma_start(up_w[:], ws_up.rearrange("(k p) f -> p k f", p=P)).then_inc(weights_loaded, 16)
            for n, (f, size) in enumerate(FB):
                sp.dma_start(down_w[0:size, n, :], ws_down[f:f + size, :]).then_inc(weights_loaded, 16)

        @block.tensor
        def _(pe):
            pe.wait_ge(router_loaded, 16)
            for k in range(KB):
                last = pe.transpose(ps_router[:, k * E:(k + 1) * E], router[:, k * P:(k + 1) * P], ident[0:E, 0:E])
            last.then_inc(routerT_in_psum, 1)

            def transposes(c):
                if c >= 2:
                    pe.wait_ge(x2T_ready, c - 1)
                for k in range(KB):
                    for b in range(GB):
                        last = pe.transpose(ps_x2T[c % 2][k][:, b * N:(b + 1) * N],
                                            x2_nat[:, c * GB + b, k * P:(k + 1) * P], ident)
                last.then_inc(x2T_in_psum, 1)

            def chunk_logits(c):
                pe.wait_ge(routerT_ready, 1)
                pe.wait_ge(x2T_ready, c + 1)
                if c >= 2:
                    pe.wait_ge(logits_copied, c - 1)
                for b in range(GB):
                    for k in range(KB):
                        last = pe.matmul(ps_logits[c % 2][:, b * E:(b + 1) * E],
                                         x2T[:, k, (c * GB + b) * N:(c * GB + b + 1) * N], routerT[:, k, :],
                                         start=k == 0, stop=k == KB - 1, skip_group_check=True)
                last.then_inc(logits_in_psum, 1)

            def places(c):
                pe.wait_ge(member_ready, c + 1)
                if c == 0:
                    pe.wait_ge(constants, 5)
                else:
                    pe.wait_ge(places_read, c)
                members = member[:, c * GB:(c + 1) * GB, :].rearrange("p b e -> p (b e)")
                for n, w in enumerate((earlier, ones)):
                    last = pe.matmul(ps_places[:, n].rearrange("p b e -> p (b e)"), w[:], members, start=True,
                                     stop=True, skip_group_check=True)
                last.then_inc(places_in_psum, 1)

            transposes(0)
            chunk_logits(0)
            transposes(1)
            places(0)
            for c in range(1, NCHUNK):
                chunk_logits(c)
                if c + 1 < NCHUNK:
                    transposes(c + 1)
            pe.wait_ge(weights_loaded, 16 * (2 + len(FB)))

            def gate_up(n):
                c, (f, size) = n // len(FB), FB[n % len(FB)]
                if n >= 2:
                    pe.wait_ge(hidden_ready, n - 1)
                for bank, w in ((ps_g[n % 2], gate_w), (ps_u[n % 2], up_w)):
                    for k in range(KB):
                        last = pe.matmul(bank[0:size, :], w[:, k, f:f + size], x2T[:, k, c * T:(c + 1) * T],
                                         start=k == 0, stop=k == KB - 1)
                last.then_inc(gu_in_psum, 1)

            def down(n):
                c, fb = n // len(FB), n % len(FB)
                size = FB[fb][1]
                pe.wait_ge(hidden_ready, n + 1)
                if n == 0:
                    pe.wait_ge(logits_copied, NCHUNK)
                elif fb == 0:
                    pe.wait_ge(yT_ready, c)
                for k in range(KB):
                    last = pe.matmul(ps_yT[:, k, :], down_w[0:size, fb, k * P:(k + 1) * P],
                                     hidden[0:size, n % 2, :], start=fb == 0, stop=fb == len(FB) - 1)
                if fb == len(FB) - 1:
                    last.then_inc(yT_in_psum, 1)

            def back(c, half):
                pe.wait_ge(yT_ready, c + 1)
                if c or half:
                    pe.wait_ge(summed_ready, 2 * c + half)
                for b in range(2):
                    for k in range(KB):
                        tok = slice((half * 2 + b) * N, (half * 2 + b + 1) * N)
                        last = pe.transpose(ps_y[:, b, k * P:(k + 1) * P], sharedT[:, k, tok], ident)
                last.then_inc(y_in_psum, 1)

            total = NCHUNK * len(FB)
            gate_up(0)
            gate_up(1)
            for n in range(total):
                if n == 0:
                    places(find_at[0])
                elif n + 1 in find_at:
                    places(find_at[n + 1])
                down(n)
                if n + 2 < total:
                    gate_up(n + 2)
                if n >= len(FB) and n % len(FB) < 2:
                    back(n // len(FB) - 1, n % len(FB))
            back(NCHUNK - 1, 0)
            back(NCHUNK - 1, 1)

        def copy_result(act, c):
            act.wait_ge(yT_in_psum, c + 1)
            if c >= 1:
                act.wait_ge(y_in_psum, 2 * c)
            act.activation(sharedT[:], ps_yT[:], ACT.Copy).then_inc(yT_ready, 1)

        @block.scalar
        def _(act):
            act.wait_ge(routerT_in_psum, 1)
            act.activation(routerT[:].rearrange("p k e -> p (k e)"), ps_router, ACT.Copy)\
               .then_inc(routerT_ready, 1)
            def copy_x2T(c):
                act.wait_ge(x2T_in_psum, c + 1)
                for k in range(KB):
                    last = act.activation(x2T[:, k, c * T:(c + 1) * T], ps_x2T[c % 2][k][:], ACT.Copy)
                last.then_inc(x2T_ready, 1)

            copy_x2T(0)
            for c in range(NCHUNK):
                if c + 1 < NCHUNK:
                    copy_x2T(c + 1)
                seqs = slice(c * GB, (c + 1) * GB)
                act.wait_ge(shifted_ready, 2 * c + 2)
                act.activation(expd[:, seqs], shifted[:, seqs], ACT.Exp).then_inc(exp_ready, 1)
                act.activation(top_expd[:, seqs], top_shifted[:, seqs], ACT.Exp).then_inc(exp_ready, 1)
            for n in range(NCHUNK * len(FB)):
                c, size = n // len(FB), FB[n % len(FB)][1]
                act.wait_ge(gu_in_psum, n + 1)
                if n >= 2:
                    act.wait_ge(hidden_ready, n - 1)
                act.activation(silu[0:size, n % 2, :], ps_g[n % 2][0:size, :], ACT.Silu).then_inc(silu_ready, 1)
                if n % len(FB) == 0 and n:
                    copy_result(act, c - 1)
            copy_result(act, NCHUNK - 1)

        @block.gpsimd
        def _(pool):
            pool.memset(earlier[:], 1.0).then_inc(iotas, 1)
            pool.wait_ge(iotas, 1)
            pool.affine_select(out=earlier[:], in_=earlier[:], compare_op=ALU.is_gt, fill=0.0, base=0,
                               pattern=[[1, P]], channel_multiplier=-1).then_inc(constants, 1)
            pool.memset(ones[:], 1.0).then_inc(constants, 1)
            pool.iota(expert_no[:], [[1, E]], base=0, channel_multiplier=0,
                      allow_small_or_imprecise_dtypes=True).then_inc(constants, 1)
            pool.iota(queue_start[:], [[CAP, E]], base=0, channel_multiplier=0,
                      allow_small_or_imprecise_dtypes=True).then_inc(constants, 1)
            pool.iota(tags[:, :, :, 1], [[N * TOP_K, B], [1, TOP_K]], base=0, channel_multiplier=TOP_K,
                      allow_small_or_imprecise_dtypes=True).then_inc(constants, 1)
            for b in range(B):
                turn, buf = divmod(b, NROWS)
                pool.wait_ge(rows_ready[buf], turn + 1)
                for k in range(TOP_K):
                    pool.indirect_dma_start(queues, bass.IndirectOffsetOnAxis(ap=rows_i[buf][:, k:k + 1], axis=0),
                                            rows[buf][:, k, :], None, bounds_check=E * CAP - 1,
                                            oob_is_err=False).then_inc(rows_scattered[buf], 16)
            for buf in range(NROWS):
                pool.wait_ge(rows_scattered[buf], 16 * TOP_K * (B // NROWS))

        @block.vector
        def _(dve):
            count = [0]

            def step(instruction):
                count[0] += 1
                instruction.then_inc(steps, 1)
                dve.wait_ge(steps, count[0])

            def over_k(ap):
                return ap.unsqueeze(2).broadcast_to([P, GB, TOP_K, E])

            def over_choices(ap):
                return ap.unsqueeze(2).broadcast_to([P, GB, TOP_K])

            def choose(c):
                seqs = slice(c * GB, (c + 1) * GB)
                dve.wait_ge(logits_in_psum, c + 1)
                dve.tensor_copy(logits[:, seqs].rearrange("p b e -> p (b e)"), ps_logits[c % 2]).then_inc(logits_copied, 1)
                dve.wait_ge(logits_copied, c + 1)
                for b in range(c * GB, (c + 1) * GB):
                    last = dve.max(top[:, b, :], logits[:, b, :])
                step(last)
                for b in range(c * GB, (c + 1) * GB):
                    last = dve.max_index(top_i[:, b, :], top[:, b, :], logits[:, b, :])
                step(last)
                dve.tensor_tensor(shifted[:, seqs], logits[:, seqs], top[:, seqs, 0:1].broadcast_to([P, GB, E]),
                                  ALU.subtract).then_inc(shifted_ready, 1)
                dve.tensor_tensor(top_shifted[:, seqs], top[:, seqs], top[:, seqs, 0:1].broadcast_to([P, GB, 8]),
                                  ALU.subtract).then_inc(shifted_ready, 1)
                step(dve.tensor_copy(top_no[:, seqs], top_i[:, seqs, 0:TOP_K]))
                if c == 0:
                    dve.wait_ge(constants, 5)
                hot = one_hot[:, seqs].rearrange("p b k e -> p (b k) e")
                number = top_no[:, seqs].rearrange("p b k -> p (b k)").unsqueeze(2)
                step(dve.tensor_tensor(hot, expert_no[:].unsqueeze(1).broadcast_to([P, GB * TOP_K, E]),
                                       number.broadcast_to([P, GB * TOP_K, E]), ALU.is_equal))
                dve.tensor_reduce(member[:, seqs], one_hot[:, seqs].rearrange("p b k e -> p b e k"), AX.X, ALU.add)\
                   .then_inc(member_ready, 1)

            def weigh(c):
                seqs = slice(c * GB, (c + 1) * GB)
                dve.wait_ge(exp_ready, 2 * c + 2)
                step(dve.tensor_reduce(norm[:, seqs], expd[:, seqs], AX.X, ALU.add))
                step(dve.reciprocal(norm[:, seqs], norm[:, seqs]))
                step(dve.tensor_tensor(top_p[:, seqs], top_expd[:, seqs, 0:TOP_K], over_choices(norm[:, seqs]), ALU.mult))
                step(dve.tensor_reduce(top_sum[:, seqs], top_p[:, seqs], AX.X, ALU.add))
                step(dve.tensor_scalar(top_sum[:, seqs], top_sum[:, seqs], 1e-20, None, ALU.add))
                step(dve.reciprocal(top_sum[:, seqs], top_sum[:, seqs]))
                step(dve.tensor_tensor(tags[:, seqs, :, 0], top_p[:, seqs], over_choices(top_sum[:, seqs]), ALU.mult))

            def find_places(c):
                seqs = slice(c * GB, (c + 1) * GB)
                dve.wait_ge(places_in_psum, c + 1)
                for b in range(GB):
                    at = c * GB + b
                    step(dve.tensor_tensor(before[:, at + 1, :], before[:, at, :], ps_places[:, 1, b, :], ALU.add))
                dve.tensor_tensor(place[:, seqs], ps_places[:, 0], before[:, seqs, :], ALU.add).then_inc(places_read, 1)
                dve.wait_ge(places_read, c + 1)
                step(dve.tensor_scalar(over[:, seqs], place[:, seqs], float(CAP), float(FAR), ALU.is_ge, ALU.mult))
                step(dve.tensor_tensor(place[:, seqs], place[:, seqs], over[:, seqs], ALU.add))
                step(dve.tensor_tensor(place[:, seqs], place[:, seqs], queue_start[:].unsqueeze(1)
                                       .broadcast_to([P, GB, E]), ALU.add))
                step(dve.tensor_tensor(picked[:], one_hot[:, seqs], over_k(place[:, seqs]), ALU.mult))
                step(dve.tensor_reduce(place_k[:, seqs].rearrange("p b k -> p (b k)"),
                                       picked[:].rearrange("p b k e -> p (b k) e"), AX.X, ALU.add))
                step(dve.tensor_copy(place_i[:, seqs], place_k[:, seqs]))

            def make_plan():
                total = before[0:1, B, :]
                step(dve.tensor_scalar(pairs[:], total, float(2 * BLOCK), 1.0, ALU.is_gt, ALU.add))
                step(dve.tensor_tensor_scan(pairs_sum[:], one_row[:], pairs[:], 0.0, ALU.mult, ALU.add))
                step(dve.tensor_tensor(pairs_sum[:], pairs_sum[:], pairs[:], ALU.subtract))
                of4 = pairs[:].rearrange("a (q w) -> a q w", w=4)
                sum4 = pairs_sum[:].rearrange("a (q w) -> a q w", w=4)
                step(dve.tensor_copy(packed[:], sum4[:, :, 0]))
                for w in (3, 2, 1, 0):
                    step(dve.scalar_tensor_tensor(out=packed[:], in0=packed[:], scalar=4.0, in1=of4[:, :, w],
                                                  op0=ALU.mult, op1=ALU.add))
                step(dve.tensor_copy(plan, packed[:]))

            def make_rows(b):
                turn, buf = divmod(b, NROWS)
                if turn >= 1:
                    dve.wait_ge(rows_scattered[buf], 16 * TOP_K * turn)
                dve.tensor_copy(rows[buf][:, :, 0:D], x2_nat[:, b, :].unsqueeze(1).broadcast_to([P, TOP_K, D]))
                dve.tensor_copy(rows[buf][:, :, D:W], tags[:, b])
                dve.tensor_copy(rows_i[buf][:], place_i[:, b, :]).then_inc(rows_ready[buf], 1)

            def make_hidden(n):
                size = FB[n % len(FB)][1]
                dve.wait_ge(silu_ready, n + 1)
                dve.tensor_tensor(hidden[0:size, n % 2, :], silu[0:size, n % 2, :], ps_u[n % 2][0:size, :], ALU.mult)\
                   .then_inc(hidden_ready, 1)

            def make_sum(c, half):
                dve.wait_ge(y_in_psum, 2 * c + half + 1)
                seqs = slice(c * GB + 2 * half, c * GB + 2 * half + 2)
                dve.tensor_tensor(base[:, seqs, :], ps_y[:], x2_nat[:, seqs, :], ALU.add).then_inc(summed_ready, 1)

            step(dve.memset(before[:, 0, :], 0.0))
            step(dve.memset(one_row[:], 1.0))
            choose(0)
            weigh(0)
            find_places(0)
            make_rows(0)
            make_rows(1)
            choose(1)
            choose(2)
            make_rows(2)
            choose(3)
            make_rows(3)
            for n in range(NCHUNK * len(FB)):
                b = GB + n
                if n in find_at:
                    weigh(find_at[n])
                    find_places(find_at[n])
                make_hidden(n)
                make_rows(b)
                if n >= len(FB) and n % len(FB) < 2:
                    make_sum(n // len(FB) - 1, n % len(FB))
            make_sum(NCHUNK - 1, 0)
            make_sum(NCHUNK - 1, 1)
            make_plan()


def expert_stage(nc, ident, queues, w_gate, w_up, w_down, plan, results):
    E, D, F = w_gate.shape
    KB = D // P
    MAXB = (queues.shape[0] // BLOCK - 1) // E
    MAXPAIRS = 2
    SUB = BLOCK // P
    FT = F - P
    HALF = P // 2
    W = D + 2
    NW = 4
    AHEAD = 2
    assert 0 < FT <= HALF and SUB == 2 and KB * BLOCK == 512 and E % NW == 0

    with ExitStack() as ctx:
        s = Scope(nc, ctx, "ex_")
        rows = s.sb("rows", [P, SUB, W])
        rowsT_hi, rowsT_lo = s.sb("rowsT_hi", [P, KB, BLOCK], F32R), s.sb("rowsT_lo", [P, KB, BLOCK], F32R)
        gate_up = [s.sb(f"gate_up{n}", [P, KB, 2, F]) for n in range(NW)]
        down = [s.sb(f"down{n}", [P, D]) for n in range(NW)]
        down_tail = [s.sb(f"down_tail{n}", [FT, D]) for n in range(NW)]
        main, tail = ([[s.sb(f"{name}_{part}{n}", shape, F32R) for part in ("hi", "lo")] for n in range(NW)]
                      for name, shape in (("main", [P, KB, 2, P]), ("tail", [P, KB, 2, HALF])))
        down_split, down_tail_split = ([s.sb(f"{name}_{part}", [rows_, NW, D], F32R) for part in ("hi", "lo")]
                                       for name, rows_ in (("down", P), ("down_tail", FT)))
        zeros, far = s.sb("zeros", [P, 2, BLOCK]), s.sb("far", [P, SUB, 2])
        silu, hidden = s.sb("silu", [P, 2, BLOCK]), s.sb("hidden", [P, 2, BLOCK])
        hidden_hi, hidden_lo = ([s.sb(f"{name}{h}", [P, 2, BLOCK], F32R) for h in range(2)]
                                for name in ("hidden_hi", "hidden_lo"))
        tags_next, tags_now, tags = (s.sb(n, [P, SUB, 2]) for n in ("tags_next", "tags_now", "tags"))
        number = [[s.sb(f"number{h}{n}", [P, 1], U32) for n in range(SUB)] for h in range(2)]
        out = [[s.sb(f"out{h}{n}", [P, D]) for n in range(SUB)] for h in range(2)]
        tick = s.sb("tick", [P, 3])
        size = (FT, P)

        ps_rowsT = s.ps("ps_rowsT", [P, KB, BLOCK])
        ps_gate, ps_up, ps_tail = (s.ps(n, [P, 512]) for n in ("ps_gate", "ps_up", "ps_tail"))
        ps_out = [s.ps(f"ps_out{n}", [P, 512]) for n in range(SUB)]
        ps_unused = s.ps("ps_unused", [P, 512])
        gate_sum = (ps_tail[0:FT, 0:BLOCK], ps_gate[:, 0:BLOCK])
        up_sum = (ps_tail[HALF:HALF + FT, 0:BLOCK], ps_up[:, 0:BLOCK])

        rows_loaded, rowsT_in_psum, rowsT_hi_ready, rowsT_lo_ready, tags_taken = (
            s.sem(n) for n in ("rows_loaded", "rowsT_in_psum", "rowsT_hi_ready", "rowsT_lo_ready", "tags_taken"))
        weights_loaded = [s.sem(f"weights_loaded{n}") for n in range(NW)]
        hi_split, lo_split, weights_used = (s.sem(n) for n in ("hi_split", "lo_split", "weights_used"))
        constants_ready, pads_ready = s.sem("constants_ready"), s.sem("pads_ready")
        sums_in_psum, silu_ready, hidden_ready, hidden_hi_ready, hidden_lo_ready = (
            s.sem(n) for n in ("sums_in_psum", "silu_ready", "hidden_ready", "hidden_hi_ready", "hidden_lo_ready"))
        out_in_psum = [s.sem(f"out_in_psum{n}") for n in range(SUB)]
        out_ready = [s.sem(f"out_ready{n}") for n in range(SUB)]
        scattered = [[s.sem(f"scattered{h}{n}") for n in range(SUB)] for h in range(2)]
        tags_shifted, tags_ready, tick_ready = (s.sem(n) for n in ("tags_shifted", "tags_ready", "tick_ready"))

        def read_plan(eng, turn):
            word = eng.value_load(plan[0:1, bass.ds(turn, 1)], min_val=0, max_val=MAXPAIRS * E * 4 ** NW)
            return word // 4 ** NW, [word // 4 ** w % 4 for w in range(NW)]

        def count_pairs(eng):
            start, counts = read_plan(eng, E // NW - 1)
            return start + sum(counts[1:], counts[0])

        def for_blocks(eng, body, after_expert=None):
            with eng.Fori(0, E // NW) as turn:
                start, counts = read_plan(eng, turn)
                for w in range(NW):
                    with eng.Fori(0, counts[w]) as q:
                        for h in range(2):
                            body(start + q, h, w, turn, q)
                    if after_expert:
                        after_expert(w, turn)
                    start = start + counts[w]

        def split_parts(w):
            return [(gate_up[w][:, :, :, 0:P], [t[:] for t in main[w]]),
                    (gate_up[w][:, :, :, P:F], [t[:, :, :, 0:FT] for t in tail[w]]),
                    (down[w][:], [t[:, w, :] for t in down_split]),
                    (down_tail[w][:], [t[:, w, :] for t in down_tail_split])]

        block = ctx.enter_context(nc.Block())

        @block.sync
        def _(sp):
            def load_rows(first_row):
                sp.dma_start(rows[:], queues[bass.ds(first_row, BLOCK), :].rearrange("(a p) w -> p a w", p=P))\
                  .then_inc(rows_loaded, 16)

            def load_weights(w, e):
                for src, k in ((w_gate, 0), (w_up, 1)):
                    sp.dma_start(gate_up[w][:, :, k, :], src[bass.ds(e, 1)].rearrange("e (k p) f -> p (e k) f", p=P))\
                      .then_inc(weights_loaded[w], 16)
                sp.dma_start(down[w][:], w_down[bass.ds(e, 1), 0:P, :].rearrange("e p c -> p (e c)"))\
                  .then_inc(weights_loaded[w], 16)
                sp.dma_start(down_tail[w][:], w_down[bass.ds(e, 1), P:F, :].rearrange("e p c -> p (e c)"))\
                  .then_inc(weights_loaded[w], 16)

            def body(m, h, w, turn, q):
                n = 2 * m + h
                e = turn * NW + w
                block = e * MAXB + 2 * q + h
                if h == 1:
                    block = block + q * (E * MAXB - MAXB - e * MAXB)
                sp.reg_mov(row_register, block * BLOCK)
                first_row = sp.snap(row_register, min_val=0, max_val=E * MAXB * BLOCK)
                sp.wait_ge(rowsT_in_psum, n)
                sp.wait_ge(tags_taken, n)
                load_rows(first_row)

            def next_weights(w, turn):
                e = turn * NW + w
                sp.wait_ge(hi_split, e + 1)
                sp.wait_ge(lo_split, e + 1)
                load_weights(w, (e + NW) % E)

            for w in range(NW):
                load_weights(w, w)
            row_register = nc.alloc_register(sp.engine, "first_row")
            for_blocks(sp, body, after_expert=next_weights)
            blocks_in_all = 2 * count_pairs(sp)
            sp.wait_ge(rowsT_in_psum, blocks_in_all)
            sp.wait_ge(tags_taken, blocks_in_all)
            load_rows(0)
            for w in range(NW):
                sp.wait_ge(weights_loaded[w], 64 * (E // NW + 1))

        @block.tensor
        def _(pe):
            def transpose_rows(n):
                pe.wait_ge(rows_loaded, n * 16 + 16)
                for k in range(KB):
                    for a in range(SUB):
                        last = pe.transpose(ps_rowsT[:, k, a * P:(a + 1) * P], rows[:, a, k * P:(k + 1) * P], ident)
                last.then_inc(rowsT_in_psum, 1)

            def body(m, h, w, turn, q):
                n = 2 * m + h
                def sums_hi(out, w_hi, w_lo):
                    for k in range(KB):
                        pe.matmul(out, w_hi[:, k], rowsT_hi[:, k, :], start=k == 0, stop=False)
                        pe.matmul(out, w_lo[:, k], rowsT_hi[:, k, :], start=False, stop=False)

                def sums_lo(out, w_hi):
                    for k in range(KB):
                        last = pe.matmul(out, w_hi[:, k], rowsT_lo[:, k, :], start=False, stop=k == KB - 1)
                    return last

                e = turn * NW + w
                w_hi, w_lo = main[w]
                wt_hi, wt_lo = (t[:].rearrange("p k a f -> p k (a f)") for t in tail[w])
                pe.wait_ge(rowsT_hi_ready, n + 1)
                pe.wait_ge(hi_split, e + 1)
                pe.wait_ge(lo_split, e + 1)
                pe.wait_ge(hidden_ready, n * 2)
                sums_hi(ps_tail[:, 0:BLOCK], wt_hi, wt_lo)
                pe.wait_ge(rowsT_lo_ready, n + 1)
                sums_lo(ps_tail[:, 0:BLOCK], wt_hi).then_inc(sums_in_psum, 1)
                for bank, k in ((ps_gate, 0), (ps_up, 1)):
                    sums_hi(bank[:, 0:BLOCK], w_hi[:, :, k, :], w_lo[:, :, k, :])
                    last = sums_lo(bank[:, 0:BLOCK], w_hi[:, :, k, :])
                last.then_inc(sums_in_psum, 1)
                transpose_rows(n + 1)
                down_products(n, 1 - h, w if h == 1 else (w + NW - 1 + q) % NW)

            def down_products(n, h, w):
                for a in range(SUB):
                    pe.wait_ge(out_ready[a], n)
                contraction = ((1, down_split), (0, down_tail_split))
                pe.wait_ge(hidden_hi_ready, n * 2 + 2)
                for f, parts in contraction:
                    for a in range(SUB):
                        for part in parts:
                            pe.matmul(ps_out[a][:, 0:D], hidden_hi[h][0:size[f], f, a * P:(a + 1) * P],
                                      part[:, bass.ds(w, 1), :], start=f == 1 and part is parts[0], stop=False)
                pe.wait_ge(hidden_lo_ready, n * 2 + 2)
                for f, (hi, _) in contraction:
                    for a in range(SUB):
                        last = pe.matmul(ps_out[a][:, 0:D], hidden_lo[h][0:size[f], f, a * P:(a + 1) * P],
                                         hi[:, bass.ds(w, 1), :], start=False, stop=f == 0)
                        if f == 0:
                            last.then_inc(out_in_psum[a], 1)

            def expert_done(w, turn):
                pe.transpose(ps_unused[0:HALF, 0:P], ident[:, 0:HALF], ident)\
                  .then_inc(weights_used, 1)

            transpose_rows(0)
            pe.wait_ge(pads_ready, 1)
            for_blocks(pe, body, after_expert=expert_done)
            down_products(2 * count_pairs(pe), 1, NW - 1)

        @block.scalar
        def _(act):
            def copy_rowsT(n):
                act.wait_ge(rowsT_in_psum, n + 1)
                act.activation(rowsT_hi[:], ps_rowsT[:], ACT.Copy).then_inc(rowsT_hi_ready, 1)

            def body(m, h, w, turn, q):
                n = 2 * m + h
                for f in range(2):
                    act.wait_ge(sums_in_psum, n * 2 + f + 1)
                    act.activation(silu[0:size[f], f, :], gate_sum[f], ACT.Silu).then_inc(silu_ready, 1)
                copy_rowsT(n + 1)
                act.wait_ge(out_in_psum[SUB - 1], n)
                for f in range(2):
                    act.wait_ge(hidden_ready, n * 2 + f + 1)
                    act.activation(hidden_hi[h][0:size[f], f, :], hidden[0:size[f], f, :], ACT.Copy)\
                       .then_inc(hidden_hi_ready, 1)

            def split_hi(w, turn):
                act.wait_ge(weights_loaded[w], turn * 64 + 64)
                for src, (hi, _) in split_parts(w):
                    last = act.activation(hi, src, ACT.Copy)
                last.then_inc(hi_split, 1)

            def split_ahead(w, turn):
                act.wait_ge(weights_used, turn * NW + w)
                split_hi((w + AHEAD) % NW, turn + (w + AHEAD) // NW)

            act.wait_ge(tick_ready, 1)
            act.activation(tick[:, 2:3], tick[:, 0:1], ACT.Silu)
            split_hi(0, 0)
            split_hi(1, 0)
            copy_rowsT(0)
            for_blocks(act, body, after_expert=split_ahead)

        @block.gpsimd
        def _(pool):
            pool.memset(tick[:], 0.0).then_inc(tick_ready, 1)
            pool.wait_ge(tick_ready, 1)
            pool.wait_ge(constants_ready, 1)
            for part in [t[:, k, :, FT:HALF] for w in range(NW) for t in tail[w] for k in range(KB)]:
                pool.tensor_copy(part, zeros[:, :, 0:HALF - FT])
            for part in down_split:
                pool.tensor_copy(part[:, NW - 1, :], zeros[:, 0, :])
            for part in down_tail_split:
                last = pool.tensor_copy(part[:, NW - 1, :], zeros[0:FT, 0, :])
            last.then_inc(pads_ready, 1)

            def split_lo(w, e):
                pool.wait_ge(hi_split, e + 1)
                for src, (hi, lo) in split_parts(w):
                    last = pool.tensor_tensor(lo, src, hi.bitcast(F32), ALU.subtract)
                last.then_inc(lo_split, 1)

            split_lo(0, 0)
            split_lo(1, 1)

            def body(m, h, w, turn, q):
                n = 2 * m + h
                results_out(n, 1 - h)

            def results_out(n, h):
                for a in range(SUB):
                    pool.wait_ge(out_ready[a], n + 1)
                    pool.wait_ge(tick_ready, n * SUB + a + 1)
                    pool.tensor_tensor(tick[:, 1:2], tick[:, 0:1], tick[:, 0:1], ALU.mult).then_inc(tick_ready, 1)
                    pool.indirect_dma_start(results, bass.IndirectOffsetOnAxis(ap=number[h][a][:], axis=0), out[h][a][:],
                                            None, bounds_check=results.shape[0] - 1, oob_is_err=False)\
                        .then_inc(scattered[h][a], 16)

            for_blocks(pool, body, after_expert=lambda w, turn: split_lo((w + AHEAD) % NW, turn * NW + w + AHEAD))
            pairs = count_pairs(pool)
            results_out(2 * pairs, 1)
            for a in range(SUB):
                pool.wait_ge(scattered[0][a], pairs * 16)
                pool.wait_ge(scattered[1][a], pairs * 16 + 16)

        @block.vector
        def _(dve):
            def take_tags(n):
                dve.wait_ge(rows_loaded, n * 16 + 16)
                dve.tensor_copy(tags_next[:], rows[:, :, D:W]).then_inc(tags_taken, 1)

            def subtract_rowsT(n):
                dve.wait_ge(rowsT_hi_ready, n + 1)
                dve.tensor_tensor(rowsT_lo[:], ps_rowsT[:], rowsT_hi[:].bitcast(F32), ALU.subtract)\
                   .then_inc(rowsT_lo_ready, 1)

            def shift_tags(n):
                dve.wait_ge(out_ready[SUB - 1], n)
                dve.wait_ge(tags_shifted, n + 1)
                dve.tensor_copy(tags[:], tags_now[:]).then_inc(tags_ready, 1)

            def results_out(m, h):
                n = 2 * m + h
                number_h, out_h = number[1 - h], out[1 - h]
                for a in range(SUB):
                    dve.wait_ge(scattered[1 - h][a], m * 16)
                    dve.tensor_copy(number_h[a][:], tags[:, a, 1:2])
                    dve.wait_ge(out_in_psum[a], n + 1)
                    dve.tensor_scalar(out_h[a][:], ps_out[a][:, 0:D], tags[:, a, 0:1], None, ALU.mult)\
                       .then_inc(out_ready[a], 1)

            def body(m, h, w, turn, q):
                n = 2 * m + h
                shift_tags(n)
                dve.wait_ge(tags_ready, n + 1)
                dve.wait_ge(tags_taken, n + 1)
                dve.tensor_copy(tags_now[:], tags_next[:]).then_inc(tags_shifted, 1)
                dve.wait_ge(tags_shifted, n + 2)
                take_tags(n + 1)
                for f in range(2):
                    dve.wait_ge(silu_ready, n * 2 + f + 1)
                    dve.tensor_tensor(hidden[0:size[f], f, :], silu[0:size[f], f, :], up_sum[f], ALU.mult)\
                       .then_inc(hidden_ready, 1)
                subtract_rowsT(n + 1)
                for f in range(2):
                    dve.wait_ge(hidden_hi_ready, n * 2 + f + 3)
                    dve.tensor_tensor(hidden_lo[h][0:size[f], f, :], hidden[0:size[f], f, :],
                                      hidden_hi[h][0:size[f], f, :].bitcast(F32), ALU.subtract)\
                       .then_inc(hidden_lo_ready, 1)
                results_out(m, h)

            dve.memset(zeros[:], 0.0).then_inc(constants_ready, 1)
            dve.memset(far[:], float(FAR)).then_inc(constants_ready, 1)
            dve.wait_ge(constants_ready, 2)
            dve.tensor_copy(tags_now[:], far[:]).then_inc(tags_shifted, 1)
            for f in range(2):
                dve.tensor_copy(hidden_hi[1][:, f, :], zeros[:, f, :]).then_inc(hidden_hi_ready, 1)
                dve.tensor_copy(hidden_lo[1][:, f, :], zeros[:, f, :]).then_inc(hidden_lo_ready, 1)
            take_tags(0)
            subtract_rowsT(0)
            for_blocks(dve, body)
            pairs = count_pairs(dve)
            shift_tags(2 * pairs)
            dve.wait_ge(tags_ready, 2 * pairs + 1)
            results_out(pairs, 0)


def combination_stage(nc, eps, base, results, out):
    _, B, D = base.shape
    NBUF = 4
    res_in = results.rearrange("(b p k) c -> b p k c", p=P, k=TOP_K)

    with ExitStack() as ctx:
        s = Scope(nc, ctx, "co_")
        res = s.sb("res", [P, NBUF, TOP_K, D])
        summed, normed = s.sb("summed", [P, 2, D]), s.sb("normed", [P, 2, D])
        stats, agg = s.sb("stats", [P, 1, 6]), s.sb("agg", [P, 1, 2])
        std, rstd, tick = s.sb("std", [P, 1]), s.sb("rstd", [P, 1]), s.sb("tick", [P, 1])
        loaded = [s.sem(f"loaded{n}") for n in range(NBUF)]
        tile_summed = [s.sem(f"tile_summed{n}") for n in range(NBUF)]
        stored = [s.sem(f"stored{n}") for n in range(2)]
        sum_steps, ln_steps, std_ready, normed_ready = (
            s.sem(n) for n in ("sum_steps", "ln_steps", "std_ready", "normed_ready"))

        block = ctx.enter_context(nc.Block())

        @block.sync
        def _(sp):
            with sp.Fori(0, B // NBUF) as turn:
                for n in range(NBUF):
                    b = turn * NBUF + n
                    sp.wait_ge(tile_summed[n], turn)
                    sp.dma_start(res[:, n], res_in[bass.ds(b, 1)].rearrange("b p k c -> p (b k) c"))\
                      .then_inc(loaded[n], 16)

        @block.scalar
        def _(act):
            with act.Fori(0, B // 2) as pair:
                for half in range(2):
                    b = pair * 2 + half
                    layer_norm_std(act, agg, std, eps, ln_steps, std_ready, b)
                    act.wait_ge(normed_ready, b + 1)
                    act.dma_start(out[bass.ds(b, 1)].rearrange("b p c -> p (b c)"), normed[:, half])\
                       .then_inc(stored[half], 16)
            for half in range(2):
                act.wait_ge(stored[half], 16 * (B // 2))

        @block.vector
        def _(dve):
            with dve.Fori(0, B // NBUF) as turn:
                for n in range(NBUF):
                    b = turn * NBUF + n
                    half = n % 2
                    dve.wait_ge(loaded[n], turn * 16 + 16)
                    dve.wait_ge(ln_steps, b * 3)
                    dve.tensor_reduce(summed[:, half], res[:, n].rearrange("p k c -> p c k"), AX.X, ALU.add)\
                       .then_inc(sum_steps, 1)
                    dve.wait_ge(sum_steps, b + 1)
                    dve.tensor_tensor(summed[:, half], summed[:, half],
                                      base[:, bass.ds(b, 1), :].rearrange("p b c -> p (b c)"), ALU.add).then_inc(tile_summed[n], 1)
                    dve.wait_ge(tile_summed[n], turn + 1)
                    dve.wait_ge(stored[half], (turn * 2 + n // 2) * 16)
                    layer_norm(dve, summed[:, half:half + 1], normed[:, half:half + 1], stats, agg, std, rstd,
                               ln_steps, std_ready, b, tick[:]).then_inc(normed_ready, 1)


def build(nc, x, skip, context, w_qkv, w_gates, w_out, k, wg_router, w_gate, w_up, w_down, ws_gate, ws_up,
          ws_down, out):
    B, N, D = x.shape
    E = w_gate.shape[0]
    capacity = CAP_FACTOR * (B * N * TOP_K // E)
    x1 = nc.dram_tensor("x1", [B, N, D], F32).ap()
    padded_kernels = nc.dram_tensor("padded_kernels", [P, k.shape[0], P + k.shape[1]], F32).ap()
    queues = nc.dram_tensor("queues", [E * capacity + BLOCK, D + 2], F32).ap()
    results = nc.dram_tensor("results", [B * N * TOP_K, D], F32).ap()

    with ExitStack() as ctx:
        s = Scope(nc, ctx, "")
        identity, eps = s.sb("identity", [P, P]), s.sb("eps", [P, 1])
        plan = s.sb("plan", [1, E // 4], I32)
        filler, zero_row = s.sb("filler", [P, D + 2]), s.sb("zero_row", [P, D])
        ones_written, identity_ready, fillers_ready = (
            s.sem(n) for n in ("ones_written", "identity_ready", "fillers_ready"))

        with nc.Block() as block:
            @block.gpsimd
            def _(pool):
                pool.memset(identity[:], 1.0).then_inc(ones_written, 1)
                pool.wait_ge(ones_written, 1)
                pool.affine_select(out=identity[:], in_=identity[:], compare_op=ALU.is_equal, fill=0.0, base=0,
                                   pattern=[[-1, P]], channel_multiplier=1).then_inc(identity_ready, 1)

            @block.vector
            def _(dve):
                dve.memset(eps[:], LN_EPS)
                dve.memset(filler[:, 0:D + 1], 0.0)
                dve.memset(filler[:, D + 1:D + 2], float(FAR))
                dve.memset(zero_row[:], 0.0)

        H, L = k.shape
        pads = (padded_kernels[:, :, 0:P], zero_row[:, 0:P].unsqueeze(1).broadcast_to([P, H, P]))
        kernels = (padded_kernels[:, :, P:P + L], k.unsqueeze(0).broadcast_to([P, H, L]))
        empty_block = (queues[E * capacity:, :].rearrange("(p r) w -> p r w", p=P),
                       filler[:].unsqueeze(1).broadcast_to([P, BLOCK // P, D + 2]))
        attention_stage(nc, identity[:], eps[:], x, w_qkv, w_gates, w_out, x1,
                        [(queues[0:E * capacity, :], filler), (results, zero_row)], [pads, kernels, empty_block])
        x2 = s.sb("x2", [P, B, D])
        convolution_stage(nc, identity[:], eps[:], x1, context, skip, padded_kernels, x2[:])
        base = s.sb("base", [P, B, D])
        routing_stage(nc, identity[:], x2[:], wg_router, ws_gate, ws_up, ws_down, queues, base[:], plan[:])
        expert_stage(nc, identity[:], queues, w_gate, w_up, w_down, plan[:], results)
        combination_stage(nc, eps[:], base[:], results, out)


_INS = ["x", "fside_S2_0", "ctx_2048", "L0_attn_w_qkv", "L0_attn_w_gates", "L0_attn_w_out", "L0_xattn_k",
        "L0_ffn_wg_router", "L0_ffn_w_gate", "L0_ffn_w_up", "L0_ffn_w_down", "L0_ffn_ws_gate", "L0_ffn_ws_up",
        "L0_ffn_ws_down"]
_OUTS = [((16, 128, 256), "float32")]


def kernel(**inputs):
    import numpy as _np
    import concourse.bacc as _bacc
    from concourse import mybir as _mybir
    from concourse.bass_utils import run_bass_kernel_spmd as _run

    nc = _bacc.Bacc("TRN2", target_bir_lowering=False, num_devices=1)
    arrays, args = {}, []
    for name in _INS:
        a = _np.ascontiguousarray(inputs[name])
        arrays[f"in_{name}_dram"] = a
        args.append(nc.dram_tensor(f"in_{name}_dram", a.shape, _mybir.dt.from_np(a.dtype), kind="ExternalInput").ap())
    for i, (shape, dtype) in enumerate(_OUTS):
        dt = _mybir.dt.from_np(_np.dtype(dtype))
        args.append(nc.dram_tensor(f"out_{i}_dram", shape, dt, kind="ExternalOutput").ap())
    build(nc, *args)
    r = _run(nc, [arrays], core_ids=[0])
    return r.results[0]["out_0_dram"]
```

```python
from contextlib import ExitStack

import concourse.bass as bass
from concourse import mybir

F32 = mybir.dt.float32
F32R = mybir.dt.float32r
U32 = mybir.dt.uint32
I32 = mybir.dt.int32
ALU = mybir.AluOpType
ACT = mybir.ActivationFunctionType
AX = mybir.AxisListType

P = 128
LN_EPS = 1e-5
GB = 4


class Scope:

    def __init__(self, nc, ctx, prefix):
        self.nc, self.ctx, self.prefix = nc, ctx, prefix

    def sb(self, name, shape, dt=F32):
        return self.ctx.enter_context(self.nc.sbuf_tensor(self.prefix + name, shape, dt))

    def ps(self, name, shape, dt=F32):
        return self.ctx.enter_context(self.nc.psum_tensor(self.prefix + name, shape, dt))

    def sem(self, name):
        return self.ctx.enter_context(self.nc.semaphore(self.prefix + name))


def split3(pe, out, lhs, rhs, first, last):
    pe.matmul(out, lhs[0], rhs[0], start=first, stop=False, skip_group_check=True)
    pe.matmul(out, lhs[0], rhs[1], start=False, stop=False, skip_group_check=True)
    return pe.matmul(out, lhs[1], rhs[0], start=False, stop=last, skip_group_check=True)


def layer_norm(dve, x, out, stats, agg, std, rstd, steps, std_ready, n_before, tick):
    count = x.shape[1]
    for n in range(count):
        last = dve.bn_stats(stats[:, n, :], x[:, n, :])
    last.then_inc(steps, 1)
    carried_wait(dve, steps, 3 * n_before + 1, tick)
    for n in range(count):
        last = dve.bn_aggr(agg[:, n, :], stats[:, n, :])
    last.then_inc(steps, 1)
    dve.wait_ge(std_ready, n_before + 1)
    dve.reciprocal(rstd[:], std[:]).then_inc(steps, 1)
    dve.wait_ge(steps, 3 * n_before + 3)
    for n in range(count):
        last = dve.tensor_scalar(out[:, n, :], x[:, n, :], agg[:, n, 0:1], rstd[:, n:n + 1],
                                 ALU.subtract, ALU.mult)
    return last


def layer_norm_std(act, agg, std, eps, steps, std_ready, n_before):
    act.wait_ge(steps, 3 * n_before + 2)
    act.activation(std[:], agg[:, :, 1], ACT.Sqrt, bias=eps).then_inc(std_ready, 1)


def carried_wait(dve, sem, value, tick):
    dve.wait_ge(sem, value)
    dve.memset(tick, 0.0)


class MixTiles:

    def __init__(self, s, ctx_in, D):
        self.ctx_in = ctx_in
        self.x, self.c = s.sb("x", [P, GB, D]), s.sb("c", [P, GB, D])
        self.x1_out = s.sb("x1_out", [P, GB, D])
        self.x_loaded, self.c_loaded = s.sem("x_loaded"), s.sem("c_loaded")
        self.x1_stored = s.sem("x1_stored")

    def load(self, sp, x1, g):
        sp.dma_start(self.x[:], x1.rearrange("b p c -> p b c")[:, bass.ds(g * GB, GB), :]).then_inc(self.x_loaded, 16)
        sp.dma_start(self.c[:], self.ctx_in.rearrange("b p c -> p b c")[:, bass.ds(g * GB, GB), :])\
          .then_inc(self.c_loaded, 16)


def attention_stage(nc, ident, eps, x, w_qkv, w_gates, w_out, x1, mix, fills, copies):
    B, N, D = x.shape
    H = w_gates.shape[1]
    DH = w_qkv.shape[1] // (3 * H)
    G = B // GB
    KB = D // P
    SOFTCAP, SCALE = 50.0, DH ** -0.5
    HG = 4
    VW = DH + 2
    T = GB * N
    NV = H
    EARLY = GB
    CH = 512
    WOH = 4
    LN_END = 2
    NRAW = 3
    assert (N, DH, T, HG * DH, H // HG, WOH * D, KB * CH) == (P, P, 512, 512, GB, 1024, 1024)

    x_in = x.rearrange("b p c -> p b c")
    x1_out = x1.rearrange("b p c -> p b c")
    w_in = w_qkv.rearrange("(k p) n -> p k n", p=P)
    wg_in = w_gates.rearrange("(k p) n -> p k n", p=P)
    wo_in = w_out.rearrange("(h p) c -> p h c", p=P)

    with ExitStack() as ctx:
        s = Scope(nc, ctx, "at_")
        w_hi, w_lo = s.sb("w_hi", [P, KB, 3 * H * DH], F32R), s.sb("w_lo", [P, KB, 3 * H * DH], F32R)
        wo_hi, wo_lo = s.sb("wo_hi", [P, H, D], F32R), s.sb("wo_lo", [P, H, D], F32R)
        wg_hi, wg_lo = s.sb("wg_hi", [P, KB, H], F32R), s.sb("wg_lo", [P, KB, H], F32R)
        raw = [s.sb("raw", [P, GB, D]), mix.x1_out, mix.c]
        wg_raw = s.sb("wg_raw", [P, KB, H])
        xT_hi, xT_lo = s.sb("xT_hi", [P, KB, T], F32R), s.sb("xT_lo", [P, KB, T], F32R)
        qT, kT = s.sb("qT", [P, T]), s.sb("kT", [P, T])
        v = s.sb("v", [P, 2, GB, HG, VW])
        capped = s.sb("capped", [P, T])
        probs = s.sb("probs", [P, 2, T])
        o_norm = s.sb("o_norm", [P, GB, DH])
        oT_hi, oT_lo = s.sb("oT_hi", [P, T], F32R), s.sb("oT_lo", [P, T], F32R)
        gate_exp, gate_den = s.sb("gate_exp", [P, GB, H]), s.sb("gate_den", [P, GB, H])
        o_den, o_scale = s.sb("o_den", [P, GB]), s.sb("o_scale", [P, GB])
        stats, agg = s.sb("stats", [P, GB, 6]), s.sb("agg", [P, GB, 2])
        tick = s.sb("tick", [P, 1])
        causal = s.sb("causal", [P, N])
        std, rstd = s.sb("std", [P, GB]), s.sb("rstd", [P, GB])
        x_for_T = mix.x
        x_res, x_out = raw[0][:], raw[1][:]

        ps_qv, ps_k, ps_s, ps_oT = (s.ps(n, [P, T]) for n in ("ps_qv", "ps_k", "ps_s", "ps_oT"))
        ps_o, ps_acc = s.ps("ps_o", [P, GB, D]), s.ps("ps_acc", [P, GB, D])
        ps_xT = (ps_qv, ps_k)
        ps_gate = ps_s[:, 0:GB * H].rearrange("p (b h) -> p b h", b=GB)

        raw_loaded = [s.sem(f"raw_loaded{n}") for n in range(NRAW)]
        gates_loaded, hi_split, lo_split, ones_ready, causal_ready = (
            s.sem(n) for n in ("gates_loaded", "hi_split", "lo_split", "ones_ready", "causal_ready"))
        filled = s.sem("filled")
        x_for_T_loaded, x_res_loaded = s.sem("x_for_T_loaded"), s.sem("x_res_loaded")
        xT_in_psum, xT_hi_ready, xT_lo_ready = (s.sem(n) for n in ("xT_in_psum", "xT_hi_ready", "xT_lo_ready"))
        q_in_psum, q_ready = s.sem("q_in_psum"), s.sem("q_ready")
        k_in_psum, k_ready = s.sem("k_in_psum"), s.sem("k_ready")
        v_in_psum, v_ready = s.sem("v_in_psum"), s.sem("v_ready")
        gate_in_psum, gate_exp_ready, gate_ready = (s.sem(n) for n in ("gate_in_psum", "gate_exp_ready", "gate_ready"))
        s_in_psum, capped_ready, exp_ready, probs_ready = (
            s.sem(n) for n in ("s_in_psum", "capped_ready", "exp_ready", "probs_ready"))
        o_in_psum, o_steps, o_ready = (s.sem(n) for n in ("o_in_psum", "o_steps", "o_ready"))
        oT_in_psum, oT_hi_ready, oT_lo_ready = (s.sem(n) for n in ("oT_in_psum", "oT_hi_ready", "oT_lo_ready"))
        acc_in_psum, sum_ready, ln_steps, std_ready, x1_ready = (
            s.sem(n) for n in ("acc_in_psum", "sum_ready", "ln_steps", "std_ready", "x1_ready"))

        def columns(kind, hg):
            c = kind * (H // HG) + hg
            cols = slice(c * CH, (c + 1) * CH)
            return w_in[:, :, cols], w_hi[:, :, cols], w_lo[:, :, cols], KB

        def out_rows(hg):
            heads = slice(hg * WOH, (hg + 1) * WOH)
            return wo_in[:, heads, :], wo_hi[:, heads, :], wo_lo[:, heads, :], WOH

        chunks = [columns(2, 0), columns(0, 0), columns(1, 0)]
        for hg in range(1, H // HG):
            chunks += [columns(2, hg), out_rows(hg - 1), columns(0, hg), columns(1, hg)]
        chunks.append(out_rows(H // HG - 1))
        AT_ONCE = 4

        def raw_chunk(n, k):
            return raw[n % NRAW][:].rearrange("p b c -> p (b c)").rearrange("p (k c) -> p k c", k=k)

        def for_groups(eng, group):
            group(0, True, False)
            with eng.Fori(1, G - 1) as g:
                group(g, False, False)
            group(G - 1, False, True)

        block = ctx.enter_context(nc.Block())

        @block.sync
        def _(sp):
            sp.dma_start(x_for_T[:], x_in[:, 0:GB, :]).then_inc(x_for_T_loaded, 16)
            sp.dma_start(wg_raw[:], wg_in).then_inc(gates_loaded, 16)
            for n, (src, _, _, k) in enumerate(chunks):
                if n >= NRAW:
                    sp.wait_ge(hi_split, n - NRAW + 2)
                    sp.wait_ge(lo_split, n - NRAW + 2)
                sp.dma_start(raw_chunk(n, k), src).then_inc(raw_loaded[n % NRAW], 16)
            sp.wait_ge(hi_split, len(chunks) + 1)
            sp.wait_ge(lo_split, len(chunks) + 1)

            for dst, src in copies:
                sp.dma_start(dst, src).then_inc(filled, 16)

            FR = 12

            def fill(g):
                for dst, row in fills:
                    width = dst.shape[1]
                    share = dst.shape[0] // G
                    for n in range(share // (P * FR)):
                        sp.dma_start(dst[bass.ds(g * share + n * P * FR, P * FR), :]
                                     .rearrange("(p r) w -> p r w", p=P),
                                     row[:].unsqueeze(1).broadcast_to([P, FR, width])).then_inc(filled, 16)

            def group(g, first, last):
                if not first:
                    sp.wait_ge(sum_ready, g)
                sp.dma_start(x_res, x_in[:, bass.ds(g * GB, GB), :]).then_inc(x_res_loaded, 16)
                if not last:
                    sp.wait_ge(xT_in_psum, g + 1)
                    sp.dma_start(x_for_T[:], x_in[:, bass.ds(g * GB + GB, GB), :]).then_inc(x_for_T_loaded, 16)
                fill(g)
                if not first:
                    store(g - 1)

            def store(g):
                sp.wait_ge(x1_ready, g + 1)
                sp.dma_start(x1_out[:, bass.ds(g * GB, GB), :], x_out).then_inc(mix.x1_stored, 16)

            for_groups(sp, group)
            sp.wait_ge(xT_in_psum, G)
            sp.wait_ge(mix.x1_stored, 16 * (G - 1))
            mix.load(sp, x1, 0)
            store(G - 1)
            sp.wait_ge(filled, 16 * (len(copies) + sum(dst.shape[0] // (P * FR) for dst, _ in fills)))

        @block.tensor
        def _(pe):
            pe.wait_ge(ones_ready, 1)

            def wait_for_chunks(count):
                pe.wait_ge(hi_split, count + 1)
                pe.wait_ge(lo_split, count + 1)

            def project(out, w_cols):
                for k in range(KB):
                    last = split3(pe, out, (w_hi[:, k, w_cols], w_lo[:, k, w_cols]),
                                  (xT_hi[:, k, :], xT_lo[:, k, :]), k == 0, k == KB - 1)
                return last

            def v_piece(out, hg, b):
                cols = slice((2 * H + hg * HG) * DH, (2 * H + (hg + 1) * HG) * DH)
                tok = slice(b * N, (b + 1) * N)
                for k in range(KB):
                    last = split3(pe, out, (xT_hi[:, k, tok], xT_lo[:, k, tok]),
                                  (w_hi[:, k, cols], w_lo[:, k, cols]), k == 0, k == KB - 1)
                return last

            def transposes(g):
                pe.wait_ge(x_for_T_loaded, g * 16 + 16)
                for k in range(KB):
                    for b in range(GB):
                        last = pe.transpose(ps_xT[k][:, b * N:(b + 1) * N], x_for_T[:, b, k * P:(k + 1) * P], ident)
                last.then_inc(xT_in_psum, 1)

            def first_v(g, n):
                if n == 0:
                    pe.wait_ge(xT_hi_ready, g + 1)
                    pe.wait_ge(xT_lo_ready, g + 1)
                if n >= 2:
                    pe.wait_ge(v_ready, g * NV + n - 1)
                v_piece((ps_qv, ps_k)[n % 2][:], 0, n).then_inc(v_in_psum, 1)

            def gates(g):
                for b in range(GB):
                    tok = slice(b * N, (b + 1) * N)
                    for k in range(KB):
                        last = split3(pe, ps_gate[:, b, :], (xT_hi[:, k, tok], xT_lo[:, k, tok]),
                                      (wg_hi[:, k, :], wg_lo[:, k, :]), k == 0, k == KB - 1)
                last.then_inc(gate_in_psum, 1)

            def group(g, first_group, last_group):
                made = EARLY
                for h in range(H + 2):
                    if first_group and h == 1:
                        wait_for_chunks(AT_ONCE)
                    if first_group and h >= 2 and AT_ONCE + h - 2 < len(chunks):
                        wait_for_chunks(AT_ONCE + h - 1)
                    if h == H and not last_group:
                        pe.wait_ge(k_ready, g * H + H)
                        transposes(g + 1)
                    if h == H + 1 and not last_group:
                        first_v(g + 1, 0)
                    if h < H:
                        pe.wait_ge(v_ready, g * NV + made)
                        project(ps_qv[:], slice(h * DH, (h + 1) * DH)).then_inc(q_in_psum, 1)
                    if h >= 2:
                        pe.wait_ge(o_ready, g * H + h - 1)
                        pe.wait_ge(oT_hi_ready, g * H + h - 2)
                        pe.wait_ge(oT_lo_ready, g * H + h - 2)
                        for b in range(GB):
                            last = pe.transpose(ps_oT[:, b * N:(b + 1) * N], o_norm[:, b, :], ident)
                        last.then_inc(oT_in_psum, 1)
                    if h < H:
                        pe.wait_ge(k_ready, g * H + h)
                        project(ps_k[:], slice((H + h) * DH, (H + h + 1) * DH)).then_inc(k_in_psum, 1)
                    if h < H:
                        pe.wait_ge(q_ready, g * H + h + 1)
                    if 1 <= h <= NV - EARLY:
                        v_piece(ps_qv[:], (h - 1) // GB + 1, (h - 1) % GB).then_inc(v_in_psum, 1)
                        made += 1
                    if h < H:
                        pe.wait_ge(k_ready, g * H + h + 1)
                        pe.wait_ge(capped_ready, g * H + h)
                        if h == 0:
                            pe.wait_ge(gate_exp_ready, g + 1)
                        for b in range(GB):
                            tok = slice(b * N, (b + 1) * N)
                            last = pe.matmul(ps_s[:, tok], kT[:, tok], qT[:, tok], start=True, stop=True,
                                             skip_group_check=True)
                        last.then_inc(s_in_psum, 1)
                    if 1 <= h <= H:
                        pe.wait_ge(probs_ready, g * H + h)
                        pe.wait_ge(v_ready, g * NV + ((h - 1) // HG + 1) * GB)
                        pe.wait_ge(o_ready, g * H + h - 1)
                        for b in range(GB):
                            last = pe.matmul(ps_o[:, b, 0:VW], probs[:, (h - 1) % 2, b * N:(b + 1) * N],
                                             v[:, (h - 1) // HG % 2, b, (h - 1) % HG, :], start=True, stop=True,
                                             skip_group_check=True)
                        last.then_inc(o_in_psum, 1)
                    if h == H + 1 and not last_group:
                        first_v(g + 1, 1)
                    if h >= 2:
                        pe.wait_ge(oT_hi_ready, g * H + h - 1)
                        pe.wait_ge(oT_lo_ready, g * H + h - 1)
                        if h == 2:
                            pe.wait_ge(sum_ready, g)
                        for b in range(GB):
                            tok = slice(b * N, (b + 1) * N)
                            last = split3(pe, ps_acc[:, b, :], (oT_hi[:, tok], oT_lo[:, tok]),
                                          (wo_hi[:, h - 2, :], wo_lo[:, h - 2, :]), h == 2 and b % 2 == 0,
                                          h == H + 1)
                last.then_inc(acc_in_psum, 1)
                if not last_group:
                    first_v(g + 1, 2)
                    gates(g + 1)
                    first_v(g + 1, 3)

            transposes(0)
            wait_for_chunks(1)
            for n in range(EARLY - 1):
                first_v(0, n)
            gates(0)
            first_v(0, EARLY - 1)
            wait_for_chunks(AT_ONCE - 1)
            for_groups(pe, group)

        @block.scalar
        def _(act):
            def split_chunk(n):
                _, hi, _, k = chunks[n]
                act.wait_ge(raw_loaded[n % NRAW], 16 * (n // NRAW + 1))
                act.activation(hi, raw_chunk(n, k), ACT.Copy).then_inc(hi_split, 1)

            def standard_deviations(g):
                act.wait_ge(ln_steps, 3 * g + 2)
                act.activation(std[:], agg[:, :, 1], ACT.Sqrt, bias=eps).then_inc(std_ready, 1)

            def split_xT(g):
                act.wait_ge(xT_in_psum, g + 1)
                for k in range(KB):
                    last = act.activation(xT_hi[:, k, :], ps_xT[k][:], ACT.Copy)
                last.then_inc(xT_hi_ready, 1)

            def gates(g):
                act.wait_ge(gate_in_psum, g + 1)
                if not (isinstance(g, int) and g == 0):
                    act.wait_ge(gate_ready, g)
                act.activation(gate_exp[:], ps_gate, ACT.Exp, scale=-1.0).then_inc(gate_exp_ready, 1)

            def group(g, first_group, last_group):
                for h in range(H + 2):
                    if h == H and not last_group:
                        split_xT(g + 1)
                    if h < H:
                        act.wait_ge(q_in_psum, g * H + h + 1)
                        act.activation(qT[:], ps_qv[:], ACT.Copy).then_inc(q_ready, 1)
                    if h >= 2:
                        act.wait_ge(oT_in_psum, g * H + h - 1)
                        act.activation(oT_hi[:], ps_oT[:], ACT.Copy).then_inc(oT_hi_ready, 1)
                    if h < H:
                        act.wait_ge(s_in_psum, g * H + h + 1)
                        act.wait_ge(exp_ready, g * H + h)
                        act.activation(capped[:], ps_s[:], ACT.Tanh, scale=SCALE / SOFTCAP).then_inc(capped_ready, 1)
                        act.wait_ge(capped_ready, g * H + h + 1)
                        if h >= 2:
                            act.wait_ge(o_in_psum, g * H + h - 1)
                        else:
                            act.wait_ge(o_in_psum, g * H)
                        act.activation(probs[:, h % 2, :], capped[:], ACT.Exp, scale=SOFTCAP).then_inc(exp_ready, 1)
                    if first_group and AT_ONCE + h < len(chunks):
                        split_chunk(AT_ONCE + h)
                    if h == LN_END and not first_group:
                        standard_deviations(g - 1)
                if last_group:
                    standard_deviations(g)
                else:
                    gates(g + 1)

            split_xT(0)
            act.wait_ge(gates_loaded, 16)
            act.activation(wg_hi[:], wg_raw[:], ACT.Copy).then_inc(hi_split, 1)
            for n in range(AT_ONCE):
                split_chunk(n)
            gates(0)
            for_groups(act, group)

        @block.gpsimd
        def _(pool):
            pool.wait_ge(ones_ready, 2)
            pool.affine_select(out=causal[:], in_=causal[:], compare_op=ALU.is_ge, fill=0.0, base=0,
                               pattern=[[1, N]], channel_multiplier=-1).then_inc(causal_ready, 1)
            pool.wait_ge(causal_ready, 1)
            with pool.Fori(0, G) as g:
                for h in range(H):
                    pool.wait_ge(exp_ready, g * H + h + 1)
                    half = probs[:, h % 2, :].rearrange("p (b i) -> p b i", b=GB)
                    pool.tensor_tensor(half, half, causal[:].unsqueeze(1).broadcast_to([P, GB, N]), ALU.mult)\
                        .then_inc(probs_ready, 1)

        @block.vector
        def _(dve):
            dve.memset(v[:, :, :, :, DH:VW], 1.0).then_inc(ones_ready, 1)
            dve.memset(causal[:], 1.0).then_inc(ones_ready, 1)
            def split_chunk(n):
                _, hi, lo, k = chunks[n]
                dve.wait_ge(hi_split, n + 2)
                dve.tensor_tensor(lo, raw_chunk(n, k), hi.bitcast(F32), ALU.subtract).then_inc(lo_split, 1)

            def layer_norm_end(g):
                dve.wait_ge(std_ready, g + 1)
                dve.reciprocal(rstd[:], std[:]).then_inc(ln_steps, 1)
                dve.wait_ge(ln_steps, 3 * g + 3)
                for b in range(GB):
                    last = dve.tensor_scalar(x_out[:, b, :], x_out[:, b, :], agg[:, b, 0:1], rstd[:, b:b + 1],
                                             ALU.subtract, ALU.mult)
                last.then_inc(x1_ready, 1)

            def v_copy(bank, hg, b):
                dve.tensor_copy(v[:, hg % 2, b, :, 0:DH],
                                bank[:].rearrange("p (h d) -> p h d", h=HG)).then_inc(v_ready, 1)

            def split_xT(g):
                dve.wait_ge(xT_hi_ready, g + 1)
                for k in range(KB):
                    last = dve.tensor_tensor(xT_lo[:, k, :], ps_xT[k][:], xT_hi[:, k, :].bitcast(F32), ALU.subtract)
                last.then_inc(xT_lo_ready, 1)

            def first_v(g, n):
                dve.wait_ge(v_in_psum, g * NV + n + 1)
                v_copy((ps_qv, ps_k)[n % 2], 0, n)

            def gates(g):
                dve.wait_ge(gate_exp_ready, g + 1)
                dve.tensor_scalar(gate_den[:], gate_exp[:], 1.0, None, ALU.add).then_inc(gate_ready, 1)

            def group(g, first_group, last_group):
                made = EARLY
                for h in range(H + 2):
                    if h == H and not last_group:
                        split_xT(g + 1)
                    if h >= 2:
                        dve.wait_ge(oT_hi_ready, g * H + h - 1)
                        dve.tensor_tensor(oT_lo[:], ps_oT[:], oT_hi[:].bitcast(F32), ALU.subtract)\
                           .then_inc(oT_lo_ready, 1)
                    if h < H:
                        dve.wait_ge(k_in_psum, g * H + h + 1)
                        dve.tensor_copy(kT[:], ps_k[:]).then_inc(k_ready, 1)
                    if 1 <= h <= NV - EARLY:
                        made += 1
                        dve.wait_ge(v_in_psum, g * NV + made)
                        v_copy(ps_qv, (h - 1) // GB + 1, (h - 1) % GB)
                    if 1 <= h <= H:
                        dve.wait_ge(o_in_psum, g * H + h)
                        if h == 1:
                            dve.wait_ge(gate_ready, g + 1)
                        dve.tensor_tensor(o_den[:], ps_o[:, :, DH], gate_den[:, :, h - 1], ALU.mult)\
                           .then_inc(o_steps, 1)
                        dve.wait_ge(o_steps, g * 2 * H + 2 * h - 1)
                        dve.reciprocal(o_scale[:], o_den[:]).then_inc(o_steps, 1)
                        dve.wait_ge(o_steps, g * 2 * H + 2 * h)
                        if h >= 2:
                            dve.wait_ge(oT_in_psum, g * H + h - 1)
                        dve.tensor_tensor(o_norm[:], ps_o[:, :, 0:DH],
                                          o_scale[:].unsqueeze(2).broadcast_to([P, GB, DH]), ALU.mult)\
                           .then_inc(o_ready, 1)
                    if first_group and AT_ONCE + h < len(chunks):
                        split_chunk(AT_ONCE + h)
                    if h == LN_END + 1 and not first_group:
                        layer_norm_end(g - 1)
                    if h == H and not last_group:
                        first_v(g + 1, 0)
                dve.wait_ge(acc_in_psum, g + 1)
                dve.wait_ge(x_res_loaded, g * 16 + 16)
                if first_group:
                    dve.wait_ge(lo_split, len(chunks) + 1)
                else:
                    dve.wait_ge(mix.x1_stored, g * 16)
                dve.tensor_tensor(x_out, ps_acc[:], x_res, ALU.add).then_inc(sum_ready, 1)
                if not last_group:
                    first_v(g + 1, 1)
                dve.wait_ge(sum_ready, g + 1)
                for b in range(GB):
                    last = dve.bn_stats(stats[:, b, :], x_out[:, b, :])
                last.then_inc(ln_steps, 1)
                if not last_group:
                    first_v(g + 1, 2)
                carried_wait(dve, ln_steps, 3 * g + 1, tick[:])
                for b in range(GB):
                    last = dve.bn_aggr(agg[:, b, :], stats[:, b, :])
                last.then_inc(ln_steps, 1)
                if last_group:
                    layer_norm_end(g)
                else:
                    first_v(g + 1, 3)
                    gates(g + 1)

            split_xT(0)
            dve.wait_ge(hi_split, 1)
            dve.tensor_tensor(wg_lo[:], wg_raw[:], wg_hi[:].bitcast(F32), ALU.subtract).then_inc(lo_split, 1)
            split_chunk(0)
            for n in range(EARLY):
                first_v(0, n)
                if n < AT_ONCE - 1:
                    split_chunk(n + 1)
            gates(0)
            for_groups(dve, group)


def convolution_stage(nc, ident, eps, x1, ctx_in, skip_in, padded_kernels, x2, mix):
    B, C, L = x1.shape
    H = padded_kernels.shape[1]
    NI = C // H
    G = B // GB
    LB = L // P
    NT = LB * GB
    TH = 4
    NY = 4
    RESULT, SKIP, ADD_X, ADD_SKIP, ADD_BOTH, STATS, MEANS, RSTD, TRANSPOSES = 3, 4, 2, 4, 9, 7, 8, 10, 9
    assert (C, LB, GB * NI * NI) == (P, 2, 256)

    x1_src = x1.rearrange("b p c -> p b c")
    ctx_src = ctx_in.rearrange("b p c -> p b c")
    row = H * (P + L)
    toeplitz_src = bass.AP(padded_kernels.tensor, P, [[row - 1, P], [P + L, H], [1, L]])

    with ExitStack() as ctx:
        s = Scope(nc, ctx, "cv_")
        toeplitz = s.sb("toeplitz", [P, H, L])
        same_head, skip = s.sb("same_head", [P, P]), s.sb("skip", [P, 1])
        skip_sum = s.sb("skip_sum", [P, P])
        x_res, c_res = s.sb("x_res", [P, GB * L]), s.sb("c_res", [P, GB * L])
        product, skipped = s.sb("product", [P, GB * L]), s.sb("skipped", [P, GB * L])
        total = s.sb("total", [P, GB, L])
        vT, cT = s.sb("vT", [P, 2, NT, C]), s.sb("cT", [P, 2, NT, C])
        pairs = s.sb("pairs", [P, NY, NT, NI, NI])
        weighted = s.sb("weighted", [P, 2, NT, NI, NI])
        outT = s.sb("outT", [P, LB, GB, C])
        stats, agg = s.sb("stats", [P, GB, 6]), s.sb("agg", [P, GB, 2])
        std, rstd, shift = s.sb("std", [P, GB]), s.sb("rstd", [P, GB]), s.sb("shift", [P, GB])
        tick = s.sb("tick", [P, 1])
        ps_v, ps_c = s.ps("ps_v", [P, GB * L]), s.ps("ps_c", [P, GB * L])
        ps_y = [s.ps(f"ps_y{n}", [P, NT, NI, NI]) for n in range(NY)]

        toeplitz_loaded, skip_loaded = [s.sem(f"toeplitz_loaded{n}") for n in range(H // TH)], s.sem("skip_loaded")
        band_steps, same_head_ready, skip_sum_ready = (s.sem(n) for n in ("band_steps", "same_head_ready",
                                                                          "skip_sum_ready"))
        x_res_loaded, c_res_loaded = s.sem("x_res_loaded"), s.sem("c_res_loaded")
        v_in_psum, c_in_psum, vT_ready, cT_ready = (s.sem(n) for n in ("v_in_psum", "c_in_psum", "vT_ready", "cT_ready"))
        pairs_ready, y_in_psum, weighted_ready, head_out = (
            s.sem(n) for n in ("pairs_ready", "y_in_psum", "weighted_ready", "head_out"))
        product_ready, result_in_psum, skip_in_psum = (s.sem(n) for n in ("product_ready", "result_in_psum", "skip_in_psum"))
        x_added, skip_ready, sum_ready = s.sem("x_added"), s.sem("skip_ready"), s.sem("sum_ready")
        stats_ready, means_ready, std_ready, rstd_ready, shift_ready, x2_ready = (s.sem(n) for n in (
            "stats_ready", "means_ready", "std_ready", "rstd_ready", "shift_ready", "x2_ready"))

        def for_groups(eng, group, end):
            group(0, True, False)
            with eng.Fori(1, G - 1) as g:
                group(g, False, False)
            group(G - 1, False, True)
            end(G - 1)

        block = ctx.enter_context(nc.Block())

        @block.sync
        def _(sp):
            def load_res(g):
                sp.dma_start(x_res[:].rearrange("p (b l) -> p b l", b=GB), x1_src[:, bass.ds(g * GB, GB), :])\
                  .then_inc(x_res_loaded, 16)
                sp.dma_start(c_res[:].rearrange("p (b l) -> p b l", b=GB), ctx_src[:, bass.ds(g * GB, GB), :])\
                  .then_inc(c_res_loaded, 16)

            def group(g, first, last):
                if not last:
                    sp.wait_ge(c_in_psum, g + 1)
                    mix.load(sp, x1, g + 1)
                if not first:
                    sp.wait_ge(x_added, g)
                    sp.wait_ge(skip_ready, g)
                    load_res(g)

            sp.dma_start(skip[:], skip_in.rearrange("(p a) -> p a", a=1)).then_inc(skip_loaded, 16)
            for n in range(H // TH):
                heads = slice(n * TH, (n + 1) * TH)
                sp.dma_start(toeplitz[:, heads], toeplitz_src[:, heads]).then_inc(toeplitz_loaded[n], 16)
            sp.wait_ge(mix.x1_stored, 16 * G)
            load_res(0)
            for_groups(sp, group, lambda g: None)

        @block.tensor
        def _(pe):
            def transposes(g):
                for src, loaded, bank, done in ((mix.x, mix.x_loaded, ps_v, v_in_psum),
                                                (mix.c, mix.c_loaded, ps_c, c_in_psum)):
                    pe.wait_ge(loaded, g * 16 + 16)
                    for lb in range(LB):
                        for b in range(GB):
                            last = pe.transpose(bank[:, (lb * GB + b) * C:(lb * GB + b + 1) * C],
                                                src[:, b, lb * P:(lb + 1) * P], ident)
                    last.then_inc(done, 1)

            def result_end(g):
                pe.wait_ge(vT_ready, g + 1)
                pe.wait_ge(head_out, g * H + H)
                for b in range(GB):
                    for lb in range(LB):
                        last = pe.transpose(ps_v[:, b * L + lb * P:b * L + (lb + 1) * P], outT[:, lb, b, :], ident)
                last.then_inc(result_in_psum, 1)

            def skip_end(g):
                pe.wait_ge(product_ready, g + 1)
                pe.wait_ge(cT_ready, g + 1)
                for n in range(2):
                    half = slice(n * 512, (n + 1) * 512)
                    last = pe.matmul(ps_c[:, half], skip_sum[:], product[:, half], start=True, stop=True)
                last.then_inc(skip_in_psum, 1)

            def group(g, first, last_group):
                for h in range(H):
                    if first and h % TH == 0:
                        pe.wait_ge(toeplitz_loaded[h // TH], 16)
                    pe.wait_ge(pairs_ready, g * H + h + 1)
                    if not (first and h < NY):
                        pe.wait_ge(weighted_ready, g * H + h - NY + 1)
                    y = ps_y[h % NY]
                    half = NT // 2
                    pe.matmul(y[:], toeplitz[:, h, 0:P], pairs[:, h % NY], start=True, stop=False, skip_group_check=True)
                    pe.matmul(y[:, half:2 * half], toeplitz[:, h, P:L], pairs[:, h % NY, 0:half], start=False,
                              stop=True, skip_group_check=True).then_inc(y_in_psum, 1)
                    if h == RESULT and not first:
                        result_end(g - 1)
                    if h == SKIP and not first:
                        skip_end(g - 1)
                    if h == TRANSPOSES and not last_group:
                        if not first:
                            pe.wait_ge(x_added, g)
                            pe.wait_ge(skip_ready, g)
                        transposes(g + 1)

            def end(g):
                skip_end(g)
                result_end(g)

            transposes(0)
            pe.wait_ge(skip_sum_ready, 1)
            for_groups(pe, group, end)

        @block.scalar
        def _(act):
            def copies(g):
                act.wait_ge(v_in_psum, g + 1)
                act.activation(vT[:, bass.ds(g % 2, 1)].rearrange("p a n c -> p (a n c)"), ps_v[:], ACT.Copy)\
                   .then_inc(vT_ready, 1)
                act.wait_ge(c_in_psum, g + 1)
                act.activation(cT[:, bass.ds(g % 2, 1)].rearrange("p a n c -> p (a n c)"), ps_c[:], ACT.Copy)\
                   .then_inc(cT_ready, 1)

            def end(g):
                act.wait_ge(means_ready, g + 1)
                act.activation(std[:], agg[:, :, 1], ACT.Sqrt, bias=eps).then_inc(std_ready, 1)
                act.wait_ge(shift_ready, g + 1)
                for b in range(GB):
                    last = act.activation(x2[:, bass.ds(g * GB + b, 1), :].rearrange("p b l -> p (b l)"), total[:, b, :],
                                          ACT.Identity, bias=shift[:, b:b + 1],
                                          scale=rstd[:, b:b + 1])
                last.then_inc(x2_ready, 1)

            def group(g, first, last):
                if not last:
                    copies(g + 1)
                if not first:
                    end(g - 1)

            copies(0)
            for_groups(act, group, end)

        @block.gpsimd
        def _(pool):
            pool.memset(same_head[:], 1.0).then_inc(band_steps, 1)
            pool.wait_ge(band_steps, 1)
            grid = same_head[:].rearrange("p (h j) -> p h j", h=H)
            pool.affine_select(out=grid, in_=grid, compare_op=ALU.is_ge, fill=0.0, base=0,
                               pattern=[[-NI, H], [0, NI]], channel_multiplier=1).then_inc(band_steps, 1)
            pool.wait_ge(band_steps, 2)
            pool.affine_select(out=grid, in_=grid, compare_op=ALU.is_ge, fill=0.0, base=NI - 1,
                               pattern=[[NI, H], [0, NI]], channel_multiplier=-1).then_inc(same_head_ready, 1)

            def make_product(g):
                pool.wait_ge(x_res_loaded, g * 16 + 16)
                pool.wait_ge(c_res_loaded, g * 16 + 16)
                if not (isinstance(g, int) and g == 0):
                    pool.wait_ge(skip_in_psum, g)
                pool.tensor_tensor(product[:], x_res[:], c_res[:], ALU.mult).then_inc(product_ready, 1)

            def group(g, first, last):
                pool.wait_ge(vT_ready, g + 1)
                pool.wait_ge(cT_ready, g + 1)
                full = [P, NT, NI, NI]
                for h in range(H):
                    if not (first and h < NY):
                        pool.wait_ge(y_in_psum, g * H + h - NY + 1)
                    ch = slice(h * NI, (h + 1) * NI)
                    v_h = vT[:, bass.ds(g % 2, 1), :, ch].rearrange("p a n i -> p (a n) i").unsqueeze(3)
                    c_h = cT[:, bass.ds(g % 2, 1), :, ch].rearrange("p a n i -> p (a n) i").unsqueeze(2)
                    pool.tensor_tensor(pairs[:, h % NY], v_h.broadcast_to(full), c_h.broadcast_to(full), ALU.mult)\
                        .then_inc(pairs_ready, 1)
                    if h == ADD_BOTH and not first:
                        end(g - 1)
                    if h == H - 3:
                        make_product(g)

            def end(g):
                pool.wait_ge(x_added, g + 1)
                pool.wait_ge(skip_ready, g + 1)
                flat = total[:].rearrange("p b l -> p (b l)")
                pool.tensor_tensor(flat, flat, skipped[:], ALU.add).then_inc(sum_ready, 1)

            for_groups(pool, group, lambda g: None)

        @block.vector
        def _(dve):
            def add_x(g):
                dve.wait_ge(result_in_psum, g + 1)
                dve.wait_ge(x_res_loaded, g * 16 + 16)
                if not (isinstance(g, int) and g == 0):
                    dve.wait_ge(x2_ready, g)
                dve.tensor_tensor(total[:].rearrange("p b l -> p (b l)"), ps_v[:], x_res[:], ALU.add)\
                   .then_inc(x_added, 1)

            def multiply_skip(g):
                if not (isinstance(g, int) and g == 0):
                    dve.wait_ge(sum_ready, g)
                dve.wait_ge(skip_in_psum, g + 1)
                dve.wait_ge(c_res_loaded, g * 16 + 16)
                dve.tensor_tensor(skipped[:], ps_c[:], c_res[:], ALU.mult).then_inc(skip_ready, 1)

            def statistics(g):
                dve.wait_ge(sum_ready, g + 1)
                for b in range(GB):
                    last = dve.bn_stats(stats[:, b, :], total[:, b, :])
                last.then_inc(stats_ready, 1)

            def means(g):
                if not (isinstance(g, int) and g == 0):
                    dve.wait_ge(x2_ready, g)
                carried_wait(dve, stats_ready, g + 1, tick[:])
                for b in range(GB):
                    last = dve.bn_aggr(agg[:, b, :], stats[:, b, :])
                last.then_inc(means_ready, 1)

            def scale_and_shift(g):
                dve.wait_ge(std_ready, g + 1)
                dve.reciprocal(rstd[:], std[:]).then_inc(rstd_ready, 1)
                dve.wait_ge(rstd_ready, g + 1)
                dve.scalar_tensor_tensor(out=shift[:], in0=agg[:, :, 0], scalar=-1.0, in1=rstd[:], op0=ALU.mult,
                                         op1=ALU.mult).then_inc(shift_ready, 1)

            parts = {ADD_X: add_x, ADD_SKIP: multiply_skip, STATS: statistics, MEANS: means, RSTD: scale_and_shift}

            def end(g):
                multiply_skip(g)
                add_x(g)
                dve.wait_ge(skip_ready, g + 1)
                dve.wait_ge(x_added, g + 1)
                flat = total[:].rearrange("p b l -> p (b l)")
                dve.tensor_tensor(flat, flat, skipped[:], ALU.add).then_inc(sum_ready, 1)
                for part in (statistics, means, scale_and_shift):
                    part(g)

            def group(g, first, last):
                full = [P, NT, NI, NI]
                dve.wait_ge(cT_ready, g + 1)
                for h in range(H + 1):
                    if h < H:
                        ch = slice(h * NI, (h + 1) * NI)
                        c_i = cT[:, bass.ds(g % 2, 1), :, ch].rearrange("p a n i -> p (a n) i").unsqueeze(3)
                        if not (first and h < 2):
                            dve.wait_ge(head_out, g * H + h - 1)
                        dve.wait_ge(y_in_psum, g * H + h + 1)
                        dve.tensor_tensor(weighted[:, h % 2], ps_y[h % NY][:], c_i.broadcast_to(full), ALU.mult)\
                           .then_inc(weighted_ready, 1)
                    if h >= 1:
                        ch = slice((h - 1) * NI, h * NI)
                        if h == 1 and not first:
                            dve.wait_ge(result_in_psum, g)
                        dve.wait_ge(weighted_ready, g * H + h)
                        dve.tensor_reduce(outT[:].rearrange("p a b c -> p (a b) c")[:, :, ch],
                                          weighted[:, (h - 1) % 2].rearrange("p n i j -> p n j i"),
                                          AX.X, ALU.add).then_inc(head_out, 1)
                    if h in parts and not first:
                        parts[h](g - 1)

            dve.wait_ge(skip_loaded, 16)
            dve.wait_ge(same_head_ready, 1)
            dve.tensor_scalar(skip_sum[:], same_head[:], skip[:], None, ALU.mult).then_inc(skip_sum_ready, 1)
            for_groups(dve, group, end)


TOP_K = 6
CAP_FACTOR = 2
BLOCK = 256
FAR = 1 << 20


def routing_stage(nc, ident, x2_nat, router, ws_gate, ws_up, ws_down, queues, base, plan, weights, zeros):
    _, B, D = x2_nat.shape
    N = P
    E = router.shape[0]
    F = ws_gate.shape[1]
    KB = D // P
    CAP = (queues.shape[0] - BLOCK) // E
    W = D + 2
    T = GB * N
    NCHUNK = B // GB
    NROWS = 4
    FB = [(f, min(P, F - f)) for f in range(0, F, P)]
    assert CAP == CAP_FACTOR * (B * N * TOP_K // E) and CAP == 3 * BLOCK and B * E == 512

    with ExitStack() as ctx:
        s = Scope(nc, ctx, "rt_")
        x2T = s.sb("x2T", [P, KB, B * N])
        routerT, tick = s.sb("routerT", [P, KB, E]), s.sb("tick", [P, 1])
        gate_w, up_w, down_w = s.sb("gate_w", [P, KB, F]), s.sb("up_w", [P, KB, F]), s.sb("down_w", [P, len(FB), D])
        silu, hidden = s.sb("silu", [P, 2, T]), s.sb("hidden", [P, 2, T])
        sharedT = s.sb("sharedT", [P, KB, T])
        logits, top, top_i = s.sb("logits", [P, B, E]), s.sb("top", [P, B, 8]), s.sb("top_i", [P, B, 8], U32)
        shifted, top_shifted = s.sb("shifted", [P, B, E]), s.sb("top_shifted", [P, B, 8])
        expd, top_expd = s.sb("expd", [P, B, E]), s.sb("top_expd", [P, B, 8])
        norm, top_p = s.sb("norm", [P, B]), s.sb("top_p", [P, B, TOP_K])
        top_sum = s.sb("top_sum", [P, B])
        expert_no = s.sb("expert_no", [P, E])
        top_no = s.sb("top_no", [P, B, TOP_K])
        one_hot, picked = s.sb("one_hot", [P, B, TOP_K, E]), s.sb("picked", [P, GB, TOP_K, E])
        member = s.sb("member", [P, B, E])
        earlier, ones = s.sb("earlier", [P, P]), s.sb("ones", [P, P])
        before = s.sb("before", [P, B + 1, E])
        place, over, queue_start = s.sb("place", [P, B, E]), s.sb("over", [P, B, E]), s.sb("queue_start", [P, E])
        place_k, place_i = s.sb("place_k", [P, B, TOP_K]), s.sb("place_i", [P, B, TOP_K], U32)
        tags = s.sb("tags", [P, B, TOP_K, 2])
        rows = [s.sb(f"rows{n}", [P, TOP_K, W]) for n in range(NROWS)]
        rows_i = [s.sb(f"rows_i{n}", [P, TOP_K], U32) for n in range(NROWS)]
        pairs = s.sb("pairs", [1, E])
        packed = s.sb("packed", [1, E // 4])
        pairs_sum, one_row = s.sb("pairs_sum", [1, E]), s.sb("one_row", [1, E])

        ps_g = [s.ps(f"ps_g{n}", [P, T]) for n in range(2)]
        ps_u = [s.ps(f"ps_u{n}", [P, T]) for n in range(2)]
        ps_yT, ps_y = s.ps("ps_yT", [P, KB, T]), s.ps("ps_y", [P, 2, D])
        ps_places = s.ps("ps_places", [P, 2, GB, E])
        ps_x2T = [(ps_g[0], ps_g[1]), (ps_u[0], ps_u[1])]
        ps_logits = [ps_yT[:, k, 0:GB * E] for k in range(2)]
        ps_router = ps_places[:].rearrange("p a b e -> p (a b e)")[:, 0:KB * E]

        weights_loaded = s.sem("weights_loaded")
        constants, iotas = s.sem("constants"), s.sem("iotas")
        x2T_in_psum, x2T_ready = s.sem("x2T_in_psum"), s.sem("x2T_ready")
        routerT_in_psum, routerT_ready = s.sem("routerT_in_psum"), s.sem("routerT_ready")
        logits_copied, places_read = s.sem("logits_copied"), s.sem("places_read")
        logits_in_psum, shifted_ready, exp_ready = s.sem("logits_in_psum"), s.sem("shifted_ready"), s.sem("exp_ready")
        steps, member_ready, places_in_psum = s.sem("steps"), s.sem("member_ready"), s.sem("places_in_psum")
        rows_ready = [s.sem(f"rows_ready{n}") for n in range(NROWS)]
        rows_scattered = [s.sem(f"rows_scattered{n}") for n in range(NROWS)]
        gu_in_psum, silu_ready, hidden_ready, yT_in_psum, yT_ready, y_in_psum, summed_ready = (s.sem(n) for n in (
            "gu_in_psum", "silu_ready", "hidden_ready", "yT_in_psum", "yT_ready", "y_in_psum", "summed_ready"))

        find_at = {0: 1}
        for c in range(2, NCHUNK):
            find_at[GB * (c - 1) - 2] = c

        block = ctx.enter_context(nc.Block())

        @block.sync
        def _(sp):
            sp.dma_start(gate_w[:], ws_gate.rearrange("(k p) f -> p k f", p=P)).then_inc(weights_loaded, 16)
            sp.dma_start(up_w[:], ws_up.rearrange("(k p) f -> p k f", p=P)).then_inc(weights_loaded, 16)
            for n, (f, size) in enumerate(FB):
                sp.dma_start(down_w[0:size, n, :], ws_down[f:f + size, :]).then_inc(weights_loaded, 16)
            sp.wait_ge(weights.gaps_zeroed, 1)
            for w in range(len(weights.loaded)):
                weights.load(sp, w, w)

        @block.tensor
        def _(pe):
            for k in range(KB):
                last = pe.transpose(ps_router[:, k * E:(k + 1) * E], router[:, k * P:(k + 1) * P], ident[0:E, 0:E])
            last.then_inc(routerT_in_psum, 1)

            def transposes(c):
                if c >= 2:
                    pe.wait_ge(x2T_ready, c - 1)
                for k in range(KB):
                    for b in range(GB):
                        last = pe.transpose(ps_x2T[c % 2][k][:, b * N:(b + 1) * N],
                                            x2_nat[:, c * GB + b, k * P:(k + 1) * P], ident)
                last.then_inc(x2T_in_psum, 1)

            def chunk_logits(c):
                pe.wait_ge(routerT_ready, 1)
                pe.wait_ge(x2T_ready, c + 1)
                if c >= 2:
                    pe.wait_ge(logits_copied, c - 1)
                for b in range(GB):
                    for k in range(KB):
                        last = pe.matmul(ps_logits[c % 2][:, b * E:(b + 1) * E],
                                         x2T[:, k, (c * GB + b) * N:(c * GB + b + 1) * N], routerT[:, k, :],
                                         start=k == 0, stop=k == KB - 1, skip_group_check=True)
                last.then_inc(logits_in_psum, 1)

            def places(c):
                pe.wait_ge(member_ready, c + 1)
                if c == 0:
                    pe.wait_ge(constants, 5)
                else:
                    pe.wait_ge(places_read, c)
                members = member[:, c * GB:(c + 1) * GB, :].rearrange("p b e -> p (b e)")
                for n, w in enumerate((earlier, ones)):
                    last = pe.matmul(ps_places[:, n].rearrange("p b e -> p (b e)"), w[:], members, start=True,
                                     stop=True, skip_group_check=True)
                last.then_inc(places_in_psum, 1)

            transposes(0)
            chunk_logits(0)
            transposes(1)
            places(0)
            for c in range(1, NCHUNK):
                chunk_logits(c)
                if c + 1 < NCHUNK:
                    transposes(c + 1)
            pe.wait_ge(weights_loaded, 16 * (2 + len(FB)))

            def gate_up(n):
                c, (f, size) = n // len(FB), FB[n % len(FB)]
                if n >= 2:
                    pe.wait_ge(hidden_ready, n - 1)
                for bank, w in ((ps_g[n % 2], gate_w), (ps_u[n % 2], up_w)):
                    for k in range(KB):
                        last = pe.matmul(bank[0:size, :], w[:, k, f:f + size], x2T[:, k, c * T:(c + 1) * T],
                                         start=k == 0, stop=k == KB - 1)
                last.then_inc(gu_in_psum, 1)

            def down(n):
                c, fb = n // len(FB), n % len(FB)
                size = FB[fb][1]
                pe.wait_ge(hidden_ready, n + 1)
                if n == 0:
                    pe.wait_ge(logits_copied, NCHUNK)
                elif fb == 0:
                    pe.wait_ge(yT_ready, c)
                for k in range(KB):
                    last = pe.matmul(ps_yT[:, k, :], down_w[0:size, fb, k * P:(k + 1) * P],
                                     hidden[0:size, n % 2, :], start=fb == 0, stop=fb == len(FB) - 1)
                if fb == len(FB) - 1:
                    last.then_inc(yT_in_psum, 1)

            def back(c, half):
                pe.wait_ge(yT_ready, c + 1)
                if c or half:
                    pe.wait_ge(summed_ready, 2 * c + half)
                for b in range(2):
                    for k in range(KB):
                        tok = slice((half * 2 + b) * N, (half * 2 + b + 1) * N)
                        last = pe.transpose(ps_y[:, b, k * P:(k + 1) * P], sharedT[:, k, tok], ident)
                last.then_inc(y_in_psum, 1)

            total = NCHUNK * len(FB)
            gate_up(0)
            gate_up(1)
            for n in range(total):
                if n == 0:
                    places(find_at[0])
                elif n + 1 in find_at:
                    places(find_at[n + 1])
                down(n)
                if n + 2 < total:
                    gate_up(n + 2)
                if n >= len(FB) and n % len(FB) < 2:
                    back(n // len(FB) - 1, n % len(FB))
            back(NCHUNK - 1, 0)
            back(NCHUNK - 1, 1)

        def copy_result(act, c):
            act.wait_ge(yT_in_psum, c + 1)
            if c >= 1:
                act.wait_ge(y_in_psum, 2 * c)
            act.activation(sharedT[:], ps_yT[:], ACT.Copy).then_inc(yT_ready, 1)

        @block.scalar
        def _(act):
            act.activation(tick[:], zeros[:, 0:1], ACT.Exp)
            act.wait_ge(routerT_in_psum, 1)
            act.activation(routerT[:].rearrange("p k e -> p (k e)"), ps_router, ACT.Copy)\
               .then_inc(routerT_ready, 1)
            def copy_x2T(c):
                act.wait_ge(x2T_in_psum, c + 1)
                for k in range(KB):
                    last = act.activation(x2T[:, k, c * T:(c + 1) * T], ps_x2T[c % 2][k][:], ACT.Copy)
                last.then_inc(x2T_ready, 1)

            copy_x2T(0)
            for c in range(NCHUNK):
                if c + 1 < NCHUNK:
                    copy_x2T(c + 1)
                seqs = slice(c * GB, (c + 1) * GB)
                act.wait_ge(shifted_ready, 2 * c + 2)
                act.activation(expd[:, seqs], shifted[:, seqs], ACT.Exp).then_inc(exp_ready, 1)
                act.activation(top_expd[:, seqs], top_shifted[:, seqs], ACT.Exp).then_inc(exp_ready, 1)
            for n in range(NCHUNK * len(FB)):
                c, size = n // len(FB), FB[n % len(FB)][1]
                act.wait_ge(gu_in_psum, n + 1)
                if n >= 2:
                    act.wait_ge(hidden_ready, n - 1)
                act.activation(silu[0:size, n % 2, :], ps_g[n % 2][0:size, :], ACT.Silu).then_inc(silu_ready, 1)
                if n % len(FB) == 0 and n:
                    copy_result(act, c - 1)
            copy_result(act, NCHUNK - 1)
            for w in range(weights.AHEAD):
                weights.split_hi(act, w, 0)

        @block.gpsimd
        def _(pool):
            pool.memset(earlier[:], 1.0).then_inc(iotas, 1)
            pool.wait_ge(iotas, 1)
            pool.affine_select(out=earlier[:], in_=earlier[:], compare_op=ALU.is_gt, fill=0.0, base=0,
                               pattern=[[1, P]], channel_multiplier=-1).then_inc(constants, 1)
            pool.memset(ones[:], 1.0).then_inc(constants, 1)
            pool.iota(expert_no[:], [[1, E]], base=0, channel_multiplier=0,
                      allow_small_or_imprecise_dtypes=True).then_inc(constants, 1)
            pool.iota(queue_start[:], [[CAP, E]], base=0, channel_multiplier=0,
                      allow_small_or_imprecise_dtypes=True).then_inc(constants, 1)
            pool.iota(tags[:, :, :, 1], [[N * TOP_K, B], [1, TOP_K]], base=0, channel_multiplier=TOP_K,
                      allow_small_or_imprecise_dtypes=True).then_inc(constants, 1)
            weights.zero_pads(pool, zeros)
            for b in range(B):
                turn, buf = divmod(b, NROWS)
                pool.wait_ge(rows_ready[buf], turn + 1)
                for k in range(TOP_K):
                    pool.indirect_dma_start(queues, bass.IndirectOffsetOnAxis(ap=rows_i[buf][:, k:k + 1], axis=0),
                                            rows[buf][:, k, :], None, bounds_check=E * CAP - 1,
                                            oob_is_err=False).then_inc(rows_scattered[buf], 16)
            for buf in range(NROWS):
                pool.wait_ge(rows_scattered[buf], 16 * TOP_K * (B // NROWS))

        @block.vector
        def _(dve):
            count = [0]

            def step(instruction):
                count[0] += 1
                instruction.then_inc(steps, 1)
                dve.wait_ge(steps, count[0])

            def over_k(ap):
                return ap.unsqueeze(2).broadcast_to([P, GB, TOP_K, E])

            def over_choices(ap):
                return ap.unsqueeze(2).broadcast_to([P, GB, TOP_K])

            def choose(c):
                seqs = slice(c * GB, (c + 1) * GB)
                dve.wait_ge(logits_in_psum, c + 1)
                dve.tensor_copy(logits[:, seqs].rearrange("p b e -> p (b e)"), ps_logits[c % 2]).then_inc(logits_copied, 1)
                dve.wait_ge(logits_copied, c + 1)
                for b in range(c * GB, (c + 1) * GB):
                    last = dve.max(top[:, b, :], logits[:, b, :])
                step(last)
                for b in range(c * GB, (c + 1) * GB):
                    last = dve.max_index(top_i[:, b, :], top[:, b, :], logits[:, b, :])
                step(last)
                dve.tensor_tensor(shifted[:, seqs], logits[:, seqs], top[:, seqs, 0:1].broadcast_to([P, GB, E]),
                                  ALU.subtract).then_inc(shifted_ready, 1)
                dve.tensor_tensor(top_shifted[:, seqs], top[:, seqs], top[:, seqs, 0:1].broadcast_to([P, GB, 8]),
                                  ALU.subtract).then_inc(shifted_ready, 1)
                step(dve.tensor_copy(top_no[:, seqs], top_i[:, seqs, 0:TOP_K]))
                if c == 0:
                    dve.wait_ge(constants, 5)
                hot = one_hot[:, seqs].rearrange("p b k e -> p (b k) e")
                number = top_no[:, seqs].rearrange("p b k -> p (b k)").unsqueeze(2)
                step(dve.tensor_tensor(hot, expert_no[:].unsqueeze(1).broadcast_to([P, GB * TOP_K, E]),
                                       number.broadcast_to([P, GB * TOP_K, E]), ALU.is_equal))
                dve.tensor_reduce(member[:, seqs], one_hot[:, seqs].rearrange("p b k e -> p b e k"), AX.X, ALU.add)\
                   .then_inc(member_ready, 1)

            def weigh(c):
                seqs = slice(c * GB, (c + 1) * GB)
                dve.wait_ge(exp_ready, 2 * c + 2)
                step(dve.tensor_reduce(norm[:, seqs], expd[:, seqs], AX.X, ALU.add))
                step(dve.reciprocal(norm[:, seqs], norm[:, seqs]))
                step(dve.tensor_tensor(top_p[:, seqs], top_expd[:, seqs, 0:TOP_K], over_choices(norm[:, seqs]), ALU.mult))
                step(dve.tensor_reduce(top_sum[:, seqs], top_p[:, seqs], AX.X, ALU.add))
                step(dve.tensor_scalar(top_sum[:, seqs], top_sum[:, seqs], 1e-20, None, ALU.add))
                step(dve.reciprocal(top_sum[:, seqs], top_sum[:, seqs]))
                step(dve.tensor_tensor(tags[:, seqs, :, 0], top_p[:, seqs], over_choices(top_sum[:, seqs]), ALU.mult))

            def find_places(c):
                seqs = slice(c * GB, (c + 1) * GB)
                dve.wait_ge(places_in_psum, c + 1)
                for b in range(GB):
                    at = c * GB + b
                    step(dve.tensor_tensor(before[:, at + 1, :], before[:, at, :], ps_places[:, 1, b, :], ALU.add))
                dve.tensor_tensor(place[:, seqs], ps_places[:, 0], before[:, seqs, :], ALU.add).then_inc(places_read, 1)
                dve.wait_ge(places_read, c + 1)
                step(dve.tensor_scalar(over[:, seqs], place[:, seqs], float(CAP), float(FAR), ALU.is_ge, ALU.mult))
                step(dve.tensor_tensor(place[:, seqs], place[:, seqs], over[:, seqs], ALU.add))
                step(dve.tensor_tensor(place[:, seqs], place[:, seqs], queue_start[:].unsqueeze(1)
                                       .broadcast_to([P, GB, E]), ALU.add))
                step(dve.tensor_tensor(picked[:], one_hot[:, seqs], over_k(place[:, seqs]), ALU.mult))
                step(dve.tensor_reduce(place_k[:, seqs].rearrange("p b k -> p (b k)"),
                                       picked[:].rearrange("p b k e -> p (b k) e"), AX.X, ALU.add))
                step(dve.tensor_copy(place_i[:, seqs], place_k[:, seqs]))

            def make_plan():
                total = before[0:1, B, :]
                step(dve.tensor_scalar(pairs[:], total, float(2 * BLOCK), 1.0, ALU.is_gt, ALU.add))
                step(dve.tensor_tensor_scan(pairs_sum[:], one_row[:], pairs[:], 0.0, ALU.mult, ALU.add))
                step(dve.tensor_tensor(pairs_sum[:], pairs_sum[:], pairs[:], ALU.subtract))
                of4 = pairs[:].rearrange("a (q w) -> a q w", w=4)
                sum4 = pairs_sum[:].rearrange("a (q w) -> a q w", w=4)
                step(dve.tensor_copy(packed[:], sum4[:, :, 0]))
                for w in (3, 2, 1, 0):
                    step(dve.scalar_tensor_tensor(out=packed[:], in0=packed[:], scalar=4.0, in1=of4[:, :, w],
                                                  op0=ALU.mult, op1=ALU.add))
                step(dve.tensor_copy(plan, packed[:]))

            def make_rows(b):
                turn, buf = divmod(b, NROWS)
                if turn >= 1:
                    dve.wait_ge(rows_scattered[buf], 16 * TOP_K * turn)
                dve.tensor_copy(rows[buf][:, :, 0:D], x2_nat[:, b, :].unsqueeze(1).broadcast_to([P, TOP_K, D]))
                dve.tensor_copy(rows[buf][:, :, D:W], tags[:, b])
                dve.tensor_copy(rows_i[buf][:], place_i[:, b, :]).then_inc(rows_ready[buf], 1)

            def make_hidden(n):
                size = FB[n % len(FB)][1]
                dve.wait_ge(silu_ready, n + 1)
                dve.tensor_tensor(hidden[0:size, n % 2, :], silu[0:size, n % 2, :], ps_u[n % 2][0:size, :], ALU.mult)\
                   .then_inc(hidden_ready, 1)

            def make_sum(c, half):
                dve.wait_ge(y_in_psum, 2 * c + half + 1)
                seqs = slice(c * GB + 2 * half, c * GB + 2 * half + 2)
                dve.tensor_tensor(base[:, seqs, :], ps_y[:], x2_nat[:, seqs, :], ALU.add).then_inc(summed_ready, 1)

            weights.zero_gaps(dve)
            step(dve.memset(before[:, 0, :], 0.0))
            step(dve.memset(one_row[:], 1.0))
            choose(0)
            weigh(0)
            find_places(0)
            make_rows(0)
            make_rows(1)
            choose(1)
            choose(2)
            make_rows(2)
            choose(3)
            make_rows(3)
            for n in range(NCHUNK * len(FB)):
                b = GB + n
                if n in find_at:
                    weigh(find_at[n])
                    find_places(find_at[n])
                make_hidden(n)
                make_rows(b)
                if n >= len(FB) and n % len(FB) < 2:
                    make_sum(n // len(FB) - 1, n % len(FB))
            make_sum(NCHUNK - 1, 0)
            make_sum(NCHUNK - 1, 1)
            make_plan()
            for w in range(weights.AHEAD):
                dve.wait_ge(weights.hi_split, w + 1)
                weights.split_lo(dve, w, (0, 1)).then_inc(weights.lo_split, 1)
            weights.split_lo(dve, 0, (2, 3)).then_inc(weights.down_lo_split, 1)


NW = 4


class ExpertWeights:
    LOADS = 5 * 16
    AHEAD = 2

    def __init__(self, s, w_gate, w_up, w_down):
        self.w_gate, self.w_up, self.w_down = w_gate, w_up, w_down
        _, D, F = w_gate.shape
        KB = D // P
        FT = self.FT = F - P
        HALF = self.HALF = P // 2
        self.gate_up = [s.sb(f"gate_up{n}", [P, KB, 2, F]) for n in range(NW)]
        self.down = [s.sb(f"down{n}", [P, D]) for n in range(NW)]
        self.down_tail = [s.sb(f"down_tail{n}", [HALF + FT, D]) for n in range(NW)]
        self.main, self.tail = (
            [[s.sb(f"{name}_{part}{n}", shape, F32R) for part in ("hi", "lo")] for n in range(NW)]
            for name, shape in (("main", [P, KB, 2, P]), ("tail", [P, KB, 2, HALF])))
        self.down_split, self.down_tail_split = (
            [s.sb(f"{name}_{part}", [rows_, NW, D], F32R) for part, rows_ in (("hi", rows_hi), ("lo", rows_lo))]
            for name, rows_hi, rows_lo in (("down", P, P), ("down_tail", HALF + FT, FT)))
        self.loaded = [s.sem(f"weights_loaded{n}") for n in range(NW)]
        self.hi_split, self.lo_split = s.sem("hi_split"), s.sem("lo_split")
        self.down_lo_split = s.sem("down_lo_split")
        self.gaps_zeroed = s.sem("gaps_zeroed")

    def zero_gaps(self, dve):
        for t in self.down_tail:
            last = dve.memset(t[:], 0.0)
        last.then_inc(self.gaps_zeroed, 1)

    def zero_pads(self, pool, zeros):
        pad = self.HALF - self.FT
        for part in [t[:, k, :, self.FT:self.HALF] for parts in self.tail for t in parts for k in range(t.shape[1])]:
            pool.tensor_copy(part, zeros[:, 0:2 * pad].rearrange("p (a c) -> p a c", a=2))
        for part in self.down_split + self.down_tail_split:
            pool.tensor_copy(part[:, NW - 1, :], zeros[0:part.shape[0], :])

    def load(self, sp, w, e):
        F = P + self.FT
        for src, k in ((self.w_gate, 0), (self.w_up, 1)):
            sp.dma_start(self.gate_up[w][:, :, k, :], src[bass.ds(e, 1)].rearrange("e (k p) f -> p (e k) f", p=P))\
              .then_inc(self.loaded[w], 16)
        sp.dma_start(self.down[w][:], self.w_down[bass.ds(e, 1), 0:P, :].rearrange("e p c -> p (e c)"))\
          .then_inc(self.loaded[w], 16)
        for at in (0, self.HALF):
            sp.dma_start(self.down_tail[w][at:at + self.FT, :],
                         self.w_down[bass.ds(e, 1), P:F, :].rearrange("e p c -> p (e c)")).then_inc(self.loaded[w], 16)

    def parts(self, w):
        return [(self.gate_up[w][:, :, :, 0:P], [t[:] for t in self.main[w]]),
                (self.gate_up[w][:, :, :, P:], [t[:, :, :, 0:self.FT] for t in self.tail[w]]),
                (self.down[w][:], [t[:, w, :] for t in self.down_split]),
                (self.down_tail[w][:], [t[:, w, :] for t in self.down_tail_split])]

    def split_hi(self, act, w, turn):
        act.wait_ge(self.loaded[w], turn * self.LOADS + self.LOADS)
        for src, (hi, _) in self.parts(w):
            last = act.activation(hi, src, ACT.Copy)
        last.then_inc(self.hi_split, 1)

    def split_lo(self, eng, w, parts):
        for n in parts:
            src, (hi, lo) = self.parts(w)[n]
            rows_ = lo.shape[0]
            last = eng.tensor_tensor(lo, src[0:rows_], hi[0:rows_].bitcast(F32), ALU.subtract)
        return last


def expert_stage(nc, ident, queues, weights, plan, results):
    E, D, _ = weights.w_gate.shape
    KB = D // P
    MAXB = (queues.shape[0] // BLOCK - 1) // E
    MAXPAIRS = 2
    SUB = BLOCK // P
    FT, HALF, AHEAD = weights.FT, weights.HALF, weights.AHEAD
    W = D + 2
    assert 0 < FT <= HALF and SUB == 2 and KB * BLOCK == 512 and E % NW == 0

    with ExitStack() as ctx:
        s = Scope(nc, ctx, "ex_")
        rows = [s.sb(f"rows{h}", [P, SUB, W]) for h in range(2)]
        rowsT_hi, rowsT_lo = s.sb("rowsT_hi", [P, KB, BLOCK], F32R), s.sb("rowsT_lo", [P, KB, BLOCK], F32R)
        main, tail, down_split, down_tail_split = weights.main, weights.tail, weights.down_split, weights.down_tail_split
        zeros, far = s.sb("zeros", [P, 2, BLOCK]), s.sb("far", [P, SUB, 2])
        silu, hidden = s.sb("silu", [P, 2, BLOCK]), s.sb("hidden", [P, 2, BLOCK])
        hidden_hi = [s.sb(f"hidden_hi{h}", [P, 2, BLOCK], F32R) for h in range(2)]
        hidden_lo = [s.sb(f"hidden_lo{h}", [P, BLOCK], F32R) for h in range(2)]
        tags = [s.sb(f"tags{h}", [P, SUB, 2]) for h in range(2)]
        number = [s.sb(f"number{h}", [P, SUB], U32) for h in range(2)]
        out = [[s.sb(f"out{h}{n}", [P, D]) for n in range(SUB)] for h in range(2)]
        tick = s.sb("tick", [P, 3])
        size = (FT, P)

        ps_rowsT = s.ps("ps_rowsT", [P, KB, BLOCK])
        ps_gate, ps_up, ps_tail = (s.ps(n, [P, 512]) for n in ("ps_gate", "ps_up", "ps_tail"))
        ps_out = [s.ps(f"ps_out{n}", [P, 512]) for n in range(SUB)]
        ps_unused = s.ps("ps_unused", [P, 512])
        gate_sum = (ps_tail[0:FT, 0:BLOCK], ps_gate[:, 0:BLOCK])
        up_sum = (ps_tail[HALF:HALF + FT, 0:BLOCK], ps_up[:, 0:BLOCK])

        rows_loaded = [s.sem(f"rows_loaded{h}") for h in range(2)]
        rowsT_in_psum, rowsT_hi_ready, rowsT_lo_ready, tags_taken = (
            s.sem(n) for n in ("rowsT_in_psum", "rowsT_hi_ready", "rowsT_lo_ready", "tags_taken"))
        hi_split, lo_split, down_lo_split = weights.hi_split, weights.lo_split, weights.down_lo_split
        weights_used = s.sem("weights_used")
        constants_ready = s.sem("constants_ready")
        sums_in_psum, silu_ready, hidden_ready, hidden_hi_ready, hidden_lo_ready = (
            s.sem(n) for n in ("sums_in_psum", "silu_ready", "hidden_ready", "hidden_hi_ready", "hidden_lo_ready"))
        out_in_psum = [s.sem(f"out_in_psum{n}") for n in range(SUB)]
        out_ready = [s.sem(f"out_ready{n}") for n in range(SUB)]
        scattered = [[s.sem(f"scattered{h}{n}") for n in range(SUB)] for h in range(2)]
        number_ready, tick_ready = s.sem("number_ready"), s.sem("tick_ready")

        MAX_WORD = MAXPAIRS * E * 4 ** NW

        def read_plan(eng, turn):
            return unpack(eng.value_load(plan[0:1, bass.ds(turn, 1)], min_val=0, max_val=MAX_WORD))

        def unpack(word):
            return word // 4 ** NW, [word // 4 ** w % 4 for w in range(NW)]

        def count_pairs(eng):
            start, counts = read_plan(eng, E // NW - 1)
            return start + sum(counts[1:], counts[0])

        def next_block(m, h):
            return (m, 1) if h == 0 else (m + 1, 0)

        def for_blocks(eng, body, after_expert=None, read_turn=read_plan):
            with eng.Fori(0, E // NW) as turn:
                start, counts = read_turn(eng, turn)
                for w in range(NW):
                    with eng.Fori(0, counts[w]) as q:
                        for h in range(2):
                            body(start + q, h, w, turn, q)
                    if after_expert:
                        after_expert(w, turn, start)
                    start = start + counts[w]

        block = ctx.enter_context(nc.Block())

        @block.sync
        def _(sp):
            def load_rows(first_row, h):
                sp.dma_start(rows[h][:], queues[bass.ds(first_row, BLOCK), :].rearrange("(a p) w -> p a w", p=P))\
                  .then_inc(rows_loaded[h], 16)

            def body(m, h, w, turn, q):
                n = 2 * m + h
                e = turn * NW + w
                block = e * MAXB + 2 * q + h
                if h == 1:
                    block = block + q * (E * MAXB - MAXB - e * MAXB)
                sp.reg_mov(row_register, block * BLOCK)
                first_row = sp.snap(row_register, min_val=0, max_val=E * MAXB * BLOCK)
                sp.wait_ge(tags_taken, n)
                load_rows(first_row, h)
                if w == NW - 1 and h == 0:
                    read_next_word((turn + 1) % (E // NW))

            def next_weights(w, turn, start):
                e = turn * NW + w
                sp.wait_ge(hi_split, e + 1)
                sp.wait_ge(lo_split, e + 1)
                sp.wait_ge(down_lo_split, start + 1)
                weights.load(sp, w, (e + NW) % E)

            row_register = nc.alloc_register(sp.engine, "first_row")
            word_register = nc.alloc_register(sp.engine, "next_word")

            def read_next_word(turn):
                sp.reg_mov(word_register, sp.value_load(plan[0:1, bass.ds(turn, 1)], min_val=0, max_val=MAX_WORD))

            read_next_word(0)
            for_blocks(sp, body, after_expert=next_weights,
                       read_turn=lambda sp, turn: unpack(sp.snap(word_register, min_val=0, max_val=MAX_WORD)))
            blocks_in_all = 2 * count_pairs(sp)
            sp.wait_ge(tags_taken, blocks_in_all)
            load_rows(0, 0)
            for w in range(NW):
                sp.wait_ge(weights.loaded[w], weights.LOADS * (E // NW + 1))

        @block.tensor
        def _(pe):
            def transpose_rows(m, h):
                pe.wait_ge(rows_loaded[h], m * 16 + 16)
                for k in range(KB):
                    for a in range(SUB):
                        last = pe.transpose(ps_rowsT[:, k, a * P:(a + 1) * P], rows[h][:, a, k * P:(k + 1) * P], ident)
                last.then_inc(rowsT_in_psum, 1)

            def body(m, h, w, turn, q):
                n = 2 * m + h
                def sums_hi(out, w_hi, w_lo):
                    for k in range(KB):
                        pe.matmul(out, w_hi[:, k], rowsT_hi[:, k, :], start=k == 0, stop=False)
                        pe.matmul(out, w_lo[:, k], rowsT_hi[:, k, :], start=False, stop=False)

                def sums_lo(out, w_hi):
                    for k in range(KB):
                        last = pe.matmul(out, w_hi[:, k], rowsT_lo[:, k, :], start=False, stop=k == KB - 1)
                    return last

                e = turn * NW + w
                w_hi, w_lo = main[w]
                wt_hi, wt_lo = (t[:].rearrange("p k a f -> p k (a f)") for t in tail[w])
                pe.wait_ge(rowsT_hi_ready, n + 1)
                pe.wait_ge(hi_split, e + 1)
                pe.wait_ge(lo_split, e + 1)
                pe.wait_ge(down_lo_split, m + 1)
                pe.wait_ge(hidden_ready, n * 2)
                sums = ((ps_tail[:, 0:BLOCK], wt_hi, wt_lo),
                        (ps_gate[:, 0:BLOCK], w_hi[:, :, 0, :], w_lo[:, :, 0, :]),
                        (ps_up[:, 0:BLOCK], w_hi[:, :, 1, :], w_lo[:, :, 1, :]))
                for out, hi, lo in sums:
                    sums_hi(out, hi, lo)
                pe.wait_ge(rowsT_lo_ready, n + 1)
                for k, (out, hi, _) in enumerate(sums):
                    last = sums_lo(out, hi)
                    if k != 1:
                        last.then_inc(sums_in_psum, 1)
                transpose_rows(*next_block(m, h))
                down_products(n, 1 - h, w if h == 1 else (w + NW - 1 + q) % NW)

            def down_products(n, h, w):
                for a in range(SUB):
                    pe.wait_ge(out_ready[a], n)
                def products(f, hidden_part, rows_, weights):
                    for a in range(SUB):
                        last = pe.matmul(ps_out[a][:, 0:D], hidden_part[0:rows_, a * P:(a + 1) * P],
                                         weights[0:rows_, bass.ds(w, 1), :], start=f == "first", stop=f == "last")
                        if f == "last":
                            last.then_inc(out_in_psum[a], 1)

                pe.wait_ge(hidden_hi_ready, n * 2 + 2)
                hi, lo = down_split
                tail_hi, tail_lo = down_tail_split
                products("first", hidden_hi[h][:, 1, :], P, hi)
                products("", hidden_hi[h][:, 1, :], P, lo)
                products("", hidden_hi[h][:, 0, :], FT, tail_lo)
                pe.wait_ge(hidden_lo_ready, n * 2 + 2)
                products("", hidden_lo[h][:], P, hi)
                products("last", hidden_hi[h][:, 0, :], HALF + FT, tail_hi)

            def expert_done(w, turn, start):
                pe.transpose(ps_unused[0:HALF, 0:P], ident[:, 0:HALF], ident)\
                  .then_inc(weights_used, 1)

            transpose_rows(0, 0)
            for_blocks(pe, body, after_expert=expert_done)
            down_products(2 * count_pairs(pe), 1, NW - 1)

        @block.scalar
        def _(act):
            def copy_rowsT(n):
                act.wait_ge(rowsT_in_psum, n + 1)
                act.activation(rowsT_hi[:], ps_rowsT[:], ACT.Copy).then_inc(rowsT_hi_ready, 1)

            def results_out(m, h):
                n = 2 * m + h
                act.wait_ge(tags_taken, n + 1)
                for a in range(SUB):
                    act.wait_ge(scattered[1 - h][a], m * 16)
                    act.wait_ge(out_in_psum[a], n + 1)
                    act.activation(out[1 - h][a][:], ps_out[a][:, 0:D], ACT.Copy, scale=tags[1 - h][:, a, 0:1])\
                       .then_inc(out_ready[a], 1)

            def body(m, h, w, turn, q):
                n = 2 * m + h
                for f in range(2):
                    act.wait_ge(sums_in_psum, n * 2 + f + 1)
                    act.activation(silu[0:size[f], f, :], gate_sum[f], ACT.Silu).then_inc(silu_ready, 1)
                copy_rowsT(n + 1)
                act.wait_ge(out_in_psum[SUB - 1], n)
                for f in range(2):
                    act.wait_ge(hidden_ready, n * 2 + f + 1)
                    act.activation(hidden_hi[h][0:size[f], f, :], hidden[0:size[f], f, :], ACT.Copy)\
                       .then_inc(hidden_hi_ready, 1)
                results_out(m, h)

            def split_ahead(w, turn, start):
                act.wait_ge(weights_used, turn * NW + w)
                weights.split_hi(act, (w + AHEAD) % NW, turn + (w + AHEAD) // NW)

            act.wait_ge(constants_ready, 3)
            act.wait_ge(tick_ready, 1)
            act.activation(tick[:, 2:3], tick[:, 0:1], ACT.Silu)
            copy_rowsT(0)
            for_blocks(act, body, after_expert=split_ahead)
            results_out(count_pairs(act), 0)

        @block.gpsimd
        def _(pool):
            pool.memset(tick[:], 0.0).then_inc(tick_ready, 1)
            pool.wait_ge(tick_ready, 1)
            def split_lo(w, e):
                pool.wait_ge(hi_split, e + 1)
                weights.split_lo(pool, w, (0, 1)).then_inc(lo_split, 1)

            def body(m, h, w, turn, q):
                n = 2 * m + h
                results_out(n, 1 - h)

            def results_out(n, h):
                pool.wait_ge(number_ready, n + 1)
                for a in range(SUB):
                    pool.wait_ge(out_ready[a], n + 1)
                    pool.wait_ge(tick_ready, n * SUB + a + 1)
                    pool.tensor_tensor(tick[:, 1:2], tick[:, 0:1], tick[:, 0:1], ALU.mult).then_inc(tick_ready, 1)
                    pool.indirect_dma_start(results, bass.IndirectOffsetOnAxis(ap=number[h][:, a:a + 1], axis=0), out[h][a][:],
                                            None, bounds_check=results.shape[0] - 1, oob_is_err=False)\
                        .then_inc(scattered[h][a], 16)

            for_blocks(pool, body, after_expert=lambda w, turn, start:
                       split_lo((w + AHEAD) % NW, turn * NW + w + AHEAD))
            pairs = count_pairs(pool)
            results_out(2 * pairs, 1)
            for a in range(SUB):
                pool.wait_ge(scattered[0][a], pairs * 16)
                pool.wait_ge(scattered[1][a], pairs * 16 + 16)

        @block.vector
        def _(dve):
            def take_tags(m, h):
                dve.wait_ge(rows_loaded[h], m * 16 + 16)
                dve.tensor_copy(tags[h][:], rows[h][:, :, D:W]).then_inc(tags_taken, 1)

            def subtract_rowsT(n):
                dve.wait_ge(rowsT_hi_ready, n + 1)
                dve.tensor_tensor(rowsT_lo[:], ps_rowsT[:], rowsT_hi[:].bitcast(F32), ALU.subtract)\
                   .then_inc(rowsT_lo_ready, 1)

            def split_down_lo(w, e, before):
                dve.wait_ge(hi_split, e + 1)
                dve.wait_ge(down_lo_split, before)
                weights.split_lo(dve, w, (2, 3)).then_inc(down_lo_split, 1)

            def take_numbers(m, h):
                dve.wait_ge(tags_taken, 2 * m + h + 1)
                for a in range(SUB):
                    dve.wait_ge(scattered[1 - h][a], m * 16)
                dve.tensor_copy(number[1 - h][:], tags[1 - h][:, :, 1]).then_inc(number_ready, 1)

            def body(m, h, w, turn, q):
                n = 2 * m + h
                for f in range(2):
                    dve.wait_ge(silu_ready, n * 2 + f + 1)
                    dve.tensor_tensor(hidden[0:size[f], f, :], silu[0:size[f], f, :], up_sum[f], ALU.mult)\
                       .then_inc(hidden_ready, 1)
                subtract_rowsT(n + 1)
                dve.wait_ge(hidden_hi_ready, n * 2 + 3)
                dve.tensor_tensor(hidden_hi[h][HALF:HALF + FT, 0, :], hidden[0:FT, 0, :],
                                  hidden_hi[h][0:FT, 0, :].bitcast(F32), ALU.subtract).then_inc(hidden_lo_ready, 1)
                dve.wait_ge(hidden_hi_ready, n * 2 + 4)
                dve.tensor_tensor(hidden_lo[h][:], hidden[:, 1, :], hidden_hi[h][:, 1, :].bitcast(F32), ALU.subtract)\
                   .then_inc(hidden_lo_ready, 1)
                if h == 0:
                    split_down_lo((w + 1) % NW, turn * NW + w + 1, m + 1)
                take_numbers(m, h)
                dve.wait_ge(number_ready, n + 1)
                dve.wait_ge(out_ready[SUB - 1], n + 1)
                take_tags(*next_block(m, h))

            dve.memset(zeros[:], 0.0).then_inc(constants_ready, 1)
            dve.memset(far[:], float(FAR)).then_inc(constants_ready, 1)
            dve.wait_ge(constants_ready, 2)
            dve.tensor_copy(hidden_hi[0][0:HALF, 0, :], zeros[0:HALF, 0, :]).then_inc(constants_ready, 1)
            dve.tensor_copy(tags[1][:], far[:]).then_inc(tags_taken, 1)
            dve.tensor_copy(hidden_hi[1][0:HALF, 0, :], zeros[0:HALF, 0, :]).then_inc(hidden_hi_ready, 1)
            dve.tensor_copy(hidden_hi[1][:, 1, :], zeros[:, 1, :]).then_inc(hidden_hi_ready, 1)
            dve.tensor_copy(hidden_hi[1][HALF:P, 0, :], zeros[HALF:P, 0, :]).then_inc(hidden_lo_ready, 1)
            dve.tensor_copy(hidden_lo[1][:], zeros[:, 0, :]).then_inc(hidden_lo_ready, 1)
            subtract_rowsT(0)
            take_tags(0, 0)
            for_blocks(dve, body)
            pairs = count_pairs(dve)
            take_numbers(pairs, 0)


def combination_stage(nc, eps, base, results, out):
    _, B, D = base.shape
    NBUF = 4
    res_in = results.rearrange("(b p k) c -> b p k c", p=P, k=TOP_K)

    with ExitStack() as ctx:
        s = Scope(nc, ctx, "co_")
        res = s.sb("res", [P, NBUF, TOP_K, D])
        summed, normed = s.sb("summed", [P, 2, D]), s.sb("normed", [P, 2, D])
        stats, agg = s.sb("stats", [P, 1, 6]), s.sb("agg", [P, 1, 2])
        std, rstd, tick = s.sb("std", [P, 1]), s.sb("rstd", [P, 1]), s.sb("tick", [P, 1])
        loaded = [s.sem(f"loaded{n}") for n in range(NBUF)]
        tile_summed = [s.sem(f"tile_summed{n}") for n in range(NBUF)]
        stored = [s.sem(f"stored{n}") for n in range(2)]
        sum_steps, ln_steps, std_ready, normed_ready = (
            s.sem(n) for n in ("sum_steps", "ln_steps", "std_ready", "normed_ready"))

        block = ctx.enter_context(nc.Block())

        @block.sync
        def _(sp):
            with sp.Fori(0, B // NBUF) as turn:
                for n in range(NBUF):
                    b = turn * NBUF + n
                    sp.wait_ge(tile_summed[n], turn)
                    sp.dma_start(res[:, n], res_in[bass.ds(b, 1)].rearrange("b p k c -> p (b k) c"))\
                      .then_inc(loaded[n], 16)

        @block.scalar
        def _(act):
            with act.Fori(0, B // 2) as pair:
                for half in range(2):
                    b = pair * 2 + half
                    layer_norm_std(act, agg, std, eps, ln_steps, std_ready, b)
                    act.wait_ge(normed_ready, b + 1)
                    act.dma_start(out[bass.ds(b, 1)].rearrange("b p c -> p (b c)"), normed[:, half])\
                       .then_inc(stored[half], 16)
            for half in range(2):
                act.wait_ge(stored[half], 16 * (B // 2))

        @block.vector
        def _(dve):
            with dve.Fori(0, B // NBUF) as turn:
                for n in range(NBUF):
                    b = turn * NBUF + n
                    half = n % 2
                    dve.wait_ge(loaded[n], turn * 16 + 16)
                    dve.wait_ge(ln_steps, b * 3)
                    dve.tensor_reduce(summed[:, half], res[:, n].rearrange("p k c -> p c k"), AX.X, ALU.add)\
                       .then_inc(sum_steps, 1)
                    dve.wait_ge(sum_steps, b + 1)
                    dve.tensor_tensor(summed[:, half], summed[:, half],
                                      base[:, bass.ds(b, 1), :].rearrange("p b c -> p (b c)"), ALU.add).then_inc(tile_summed[n], 1)
                    dve.wait_ge(tile_summed[n], turn + 1)
                    dve.wait_ge(stored[half], (turn * 2 + n // 2) * 16)
                    layer_norm(dve, summed[:, half:half + 1], normed[:, half:half + 1], stats, agg, std, rstd,
                               ln_steps, std_ready, b, tick[:]).then_inc(normed_ready, 1)


def build(nc, x, skip, context, w_qkv, w_gates, w_out, k, wg_router, w_gate, w_up, w_down, ws_gate, ws_up,
          ws_down, out):
    B, N, D = x.shape
    E = w_gate.shape[0]
    capacity = CAP_FACTOR * (B * N * TOP_K // E)
    x1 = nc.dram_tensor("x1", [B, N, D], F32).ap()
    padded_kernels = nc.dram_tensor("padded_kernels", [P, k.shape[0], P + k.shape[1]], F32).ap()
    queues = nc.dram_tensor("queues", [E * capacity + BLOCK, D + 2], F32).ap()
    results = nc.dram_tensor("results", [B * N * TOP_K, D], F32).ap()

    with ExitStack() as ctx:
        s = Scope(nc, ctx, "")
        identity, eps = s.sb("identity", [P, P]), s.sb("eps", [P, 1])
        plan, router = s.sb("plan", [1, E // 4], I32), s.sb("router", [E, D])
        filler, zero_row = s.sb("filler", [P, D + 2]), s.sb("zero_row", [P, D])
        ones_written, identity_ready = s.sem("ones_written"), s.sem("identity_ready")

        with nc.Block() as block:
            @block.gpsimd
            def _(pool):
                pool.memset(identity[:], 1.0).then_inc(ones_written, 1)
                pool.wait_ge(ones_written, 1)
                pool.affine_select(out=identity[:], in_=identity[:], compare_op=ALU.is_equal, fill=0.0, base=0,
                                   pattern=[[-1, P]], channel_multiplier=1).then_inc(identity_ready, 1)

            @block.vector
            def _(dve):
                dve.memset(eps[:], LN_EPS)
                dve.memset(filler[:, 0:D + 1], 0.0)
                dve.memset(filler[:, D + 1:D + 2], float(FAR))
                dve.memset(zero_row[:], 0.0)

        H, L = k.shape
        pads = (padded_kernels[:, :, 0:P], zero_row[:, 0:P].unsqueeze(1).broadcast_to([P, H, P]))
        kernels = (padded_kernels[:, :, P:P + L], k.unsqueeze(0).broadcast_to([P, H, L]))
        empty_block = (queues[E * capacity:, :].rearrange("(p r) w -> p r w", p=P),
                       filler[:].unsqueeze(1).broadcast_to([P, BLOCK // P, D + 2]))
        mix = MixTiles(Scope(nc, ctx, "mix_"), context, D)
        attention_stage(nc, identity[:], eps[:], x, w_qkv, w_gates, w_out, x1, mix,
                        [(queues[0:E * capacity, :], filler), (results, zero_row)], [pads, kernels, empty_block,
                                                                           (router[:], wg_router)])
        x2 = s.sb("x2", [P, B, D])
        convolution_stage(nc, identity[:], eps[:], x1, context, skip, padded_kernels, x2[:], mix)
        base = s.sb("base", [P, B, D])
        weights = ExpertWeights(Scope(nc, ctx, "ew_"), w_gate, w_up, w_down)
        routing_stage(nc, identity[:], x2[:], router[:], ws_gate, ws_up, ws_down, queues, base[:], plan[:], weights,
                      zero_row[:])
        expert_stage(nc, identity[:], queues, weights, plan[:], results)
        combination_stage(nc, eps[:], base[:], results, out)


_INS = ["x", "fside_S2_0", "ctx_2048", "L0_attn_w_qkv", "L0_attn_w_gates", "L0_attn_w_out", "L0_xattn_k",
        "L0_ffn_wg_router", "L0_ffn_w_gate", "L0_ffn_w_up", "L0_ffn_w_down", "L0_ffn_ws_gate", "L0_ffn_ws_up",
        "L0_ffn_ws_down"]
_OUTS = [((16, 128, 256), "float32")]


def kernel(**inputs):
    import numpy as _np
    import concourse.bacc as _bacc
    from concourse import mybir as _mybir
    from concourse.bass_utils import run_bass_kernel_spmd as _run

    nc = _bacc.Bacc("TRN2", target_bir_lowering=False, num_devices=1)
    arrays, args = {}, []
    for name in _INS:
        a = _np.ascontiguousarray(inputs[name])
        arrays[f"in_{name}_dram"] = a
        args.append(nc.dram_tensor(f"in_{name}_dram", a.shape, _mybir.dt.from_np(a.dtype), kind="ExternalInput").ap())
    for i, (shape, dtype) in enumerate(_OUTS):
        dt = _mybir.dt.from_np(_np.dtype(dtype))
        args.append(nc.dram_tensor(f"out_{i}_dram", shape, dt, kind="ExternalOutput").ap())
    build(nc, *args)
    r = _run(nc, [arrays], core_ids=[0])
    return r.results[0]["out_0_dram"]
```
